# Optimizing a Trainium2 kernel written in Bass

```python
import numpy as np
import jax
import jax.numpy as jnp

def _softmax(x, axis=-1):
    return jax.nn.softmax(x, axis=axis)

def _gelu(x):
    return jax.nn.gelu(x, approximate=True)

def _silu(x):
    return jax.nn.silu(x)

def _sigmoid(x):
    return jax.nn.sigmoid(x)

def _layernorm(x, axis=-1, eps=1e-05):
    m = jnp.mean(x, axis=axis, keepdims=True)
    v = jnp.var(x, axis=axis, keepdims=True)
    return (x - m) / jnp.sqrt(v + eps)

def _scatter_add(tgt, idx, src, axis=0):
    return tgt.at[idx].add(src)

def _segment_sum(src, seg, n):
    return jax.ops.segment_sum(src, seg, n)
kernel_name = 'mk_seq_preln_d1_jaxref_r4_6d8ef3'

def setup_inputs(seed: int=0):
    np.random.seed(seed)
    _w = jnp.asarray

    def _L0_attn_setup():
        import jax, jax.numpy as jnp
        import numpy as np
        D_MODEL = 512
        N_QUERY = 4
        N_HEAD = 8
        D_HEAD = D_MODEL // (N_QUERY * N_HEAD)
        D_KV = D_HEAD * N_HEAD
        BATCH, SEQ = (2, 512)
        key = jax.random.key(seed)
        ks = jax.random.split(key, 5)
        w_scale = 1.0 / np.sqrt(D_MODEL).astype(np.float32)
        x = jax.random.normal(ks[0], (BATCH, SEQ, D_MODEL), jnp.float32)
        Wq = jax.random.normal(ks[1], (D_MODEL, D_MODEL), jnp.float32) * w_scale
        Wk = jax.random.normal(ks[2], (D_KV, D_MODEL), jnp.float32) * w_scale
        Wv = jax.random.normal(ks[3], (D_KV, D_MODEL), jnp.float32) * w_scale
        memory = jax.random.normal(ks[4], (D_KV, D_KV), jnp.float32) * 0.02
        memory_norm = jnp.ones((D_KV, 1), jnp.float32)
        memory_weight = jnp.ones((1,), jnp.float32)
        return dict(x=x, Wq=Wq, Wk=Wk, Wv=Wv, memory=memory, memory_norm=memory_norm, memory_weight=memory_weight)
    _L0_attn_in = _L0_attn_setup()

    def _L0_ffn_setup():
        import jax, jax.numpy as jnp
        import numpy as np
        TOP_K = 4
        ROUTED_SCALE = 1.0
        NORM_TOPK = True
        B, S, H = (1, 512, 512)
        E, I = (16, 192)
        IS = 192
        key = jax.random.key(seed)
        ks = jax.random.split(key, 8)
        s = 0.02
        return {'hidden_states': jax.random.normal(ks[0], (B, S, H), jnp.float32), 'router_w': jax.random.normal(ks[1], (E, H), jnp.float32) * s, 'e_bias': jax.random.normal(ks[2], (E,), jnp.float32) * s, 'gate_up_proj': jax.random.normal(ks[3], (E, 2 * I, H), jnp.float32) * s, 'down_proj': jax.random.normal(ks[4], (E, H, I), jnp.float32) * s, 'shared_gate_w': jax.random.normal(ks[5], (IS, H), jnp.float32) * s, 'shared_up_w': jax.random.normal(ks[6], (IS, H), jnp.float32) * s, 'shared_down_w': jax.random.normal(ks[7], (H, IS), jnp.float32) * s}
    _L0_ffn_in = _L0_ffn_setup()
    _d = {'L0_attn_x': _L0_attn_in['x'], 'L0_attn_Wq': _L0_attn_in['Wq'], 'L0_attn_Wk': _L0_attn_in['Wk'], 'L0_attn_Wv': _L0_attn_in['Wv'], 'L0_attn_memory': _L0_attn_in['memory'], 'L0_attn_memory_norm': _L0_attn_in['memory_norm'], 'L0_attn_memory_weight': _L0_attn_in['memory_weight'], 'L0_ffn_router_w': _L0_ffn_in['router_w'], 'L0_ffn_e_bias': _L0_ffn_in['e_bias'], 'L0_ffn_gate_up_proj': _L0_ffn_in['gate_up_proj'], 'L0_ffn_down_proj': _L0_ffn_in['down_proj'], 'L0_ffn_shared_gate_w': _L0_ffn_in['shared_gate_w'], 'L0_ffn_shared_up_w': _L0_ffn_in['shared_up_w'], 'L0_ffn_shared_down_w': _L0_ffn_in['shared_down_w']}
    _x0 = _d['L0_attn_x']
    _d['L0_attn_x'] = jax.random.normal(jax.random.fold_in(jax.random.key(seed), 1), (8, 512, 512), dtype=_x0.dtype)
    del _x0
    return _d

def reference(L0_attn_x, L0_attn_Wq, L0_attn_Wk, L0_attn_Wv, L0_attn_memory, L0_attn_memory_norm, L0_attn_memory_weight, L0_ffn_router_w, L0_ffn_e_bias, L0_ffn_gate_up_proj, L0_ffn_down_proj, L0_ffn_shared_gate_w, L0_ffn_shared_up_w, L0_ffn_shared_down_w):

    def _L0_attn_ref(x, Wq, Wk, Wv, memory, memory_norm, memory_weight):
        import jax, jax.numpy as jnp
        import numpy as np
        D_MODEL = 512
        N_QUERY = 4
        N_HEAD = 8
        D_HEAD = D_MODEL // (N_QUERY * N_HEAD)
        D_KV = D_HEAD * N_HEAD
        BATCH, SEQ = (2, 512)
        b, s, d = x.shape
        q = x @ Wq.T
        k = x @ Wk.T
        v = x @ Wv.T
        qh = q.reshape(b, s, N_QUERY, N_HEAD, D_HEAD)
        kh = k.reshape(b, s, N_HEAD, D_HEAD)
        vh = v.reshape(b, s, N_HEAD, D_HEAD)
        scale = np.float32(1.0 / np.sqrt(np.float32(D_HEAD)))
        scores = jnp.einsum('bsqhd,bthd->bqhst', qh, kh) * scale
        probs = jax.nn.softmax(scores, axis=-1)
        a_dot = jnp.einsum('bqhst,bthd->bsqhd', probs, vh)
        a_dot = a_dot.reshape(b, s, N_QUERY * N_HEAD, D_HEAD)
        sigma_q = jax.nn.elu(q.reshape(b, s, N_QUERY, D_KV))
        a_mem = sigma_q @ memory / (sigma_q @ memory_norm)
        a_mem = a_mem.reshape(b, s, N_QUERY * N_HEAD, D_HEAD)
        w = jax.nn.sigmoid(memory_weight)
        out = a_dot * (1.0 - w) + a_mem * w
        return out.reshape(b, s, D_MODEL)

    def _L0_ffn_ref(hidden_states, router_w, e_bias, gate_up_proj, down_proj, shared_gate_w, shared_up_w, shared_down_w):
        import jax, jax.numpy as jnp
        import numpy as np
        TOP_K = 4
        ROUTED_SCALE = 1.0
        NORM_TOPK = True
        B, S, H = (1, 512, 512)
        E, I = (16, 192)
        IS = 192
        orig_shape = hidden_states.shape
        x = hidden_states.reshape(-1, orig_shape[-1])
        T = x.shape[0]
        scores = jax.nn.sigmoid(x @ router_w.T)
        _, topk_idx = jax.lax.top_k(scores + e_bias[None, :], TOP_K)
        topk_w = jnp.take_along_axis(scores, topk_idx, axis=1)
        if NORM_TOPK:
            topk_w = topk_w / (topk_w.sum(axis=-1, keepdims=True) + 1e-20)
        topk_w = topk_w * ROUTED_SCALE
        combine = jnp.zeros((T, E), x.dtype).at[jnp.arange(T)[:, None], topk_idx].add(topk_w)

        def step(acc, xs):
            gu_w, d_w, c = xs
            gu = x @ gu_w.T
            g, u = jnp.split(gu, 2, axis=1)
            y = jax.nn.silu(g) * u @ d_w.T
            return (acc + c[:, None] * y, None)
        routed, _ = jax.lax.scan(step, jnp.zeros_like(x), (gate_up_proj, down_proj, combine.T))
        shared = jax.nn.silu(x @ shared_gate_w.T) * (x @ shared_up_w.T) @ shared_down_w.T
        return (routed + shared).reshape(orig_shape)
    x = L0_attn_x
    x = x + _L0_attn_ref(_layernorm(x, axis=-1), L0_attn_Wq, L0_attn_Wk, L0_attn_Wv, L0_attn_memory, L0_attn_memory_norm, L0_attn_memory_weight)
    x = x + _L0_ffn_ref(_layernorm(x, axis=-1), L0_ffn_router_w, L0_ffn_e_bias, L0_ffn_gate_up_proj, L0_ffn_down_proj, L0_ffn_shared_gate_w, L0_ffn_shared_up_w, L0_ffn_shared_down_w)
    return x

_drawn_inputs = setup_inputs


def setup_inputs(seed=0):
    import zlib

    import numpy as np

    out = dict(_drawn_inputs(seed))
    spreads = {'L0_attn_memory_norm': (1.0, 0.2)}
    factors = {'L0_ffn_router_w': 4.583,
     'L0_ffn_e_bias': 8.0,
     'L0_ffn_gate_up_proj': 3.954,
     'L0_ffn_down_proj': 3.957,
     'L0_ffn_shared_gate_w': 3.002,
     'L0_ffn_shared_up_w': 2.937,
     'L0_ffn_shared_down_w': 2.939}
    for name, (base, spread) in spreads.items():
        noise = np.random.default_rng([zlib.crc32(name.encode()), seed]).standard_normal(out[name].shape)
        drawn = base * np.exp(spread * noise) if base else spread * noise
        out[name] = jnp.asarray(drawn.astype(out[name].dtype))
    for name, factor in factors.items():
        out[name] = (out[name] * factor).astype(out[name].dtype)
    return out
```

```python
from contextlib import ExitStack

import numpy as np

import concourse.bass as bass
from concourse import mybir

ALU = mybir.AluOpType
ACT = mybir.ActivationFunctionType
F32 = mybir.dt.float32
BF16 = mybir.dt.bfloat16
U32 = mybir.dt.uint32
I32 = mybir.dt.int32
AX_X = mybir.AxisListType.X

P = 128
D = 512
DC = D // P
SEQ = 512
NQ = 4
NH = 8
DH = 16
UT = 256
EPS = 1e-5
E = 16
K = 4
I = 192
IR = I - P
PARTS = 3
ROWS = 6 * DH
MROWS = 2
SCALE = 1.0 / float(np.sqrt(np.float32(DH)))


def sizes(T):
    stride = T + P
    return stride, E * stride


def attention(nc, T, io, keep, scratch):
    x, wq, wk, wv, memory, memory_norm, memory_weight, router_w, e_bias = io
    NU = T // UT
    ctx = ExitStack()

    def sb(name, shape, dt=F32):
        return ctx.enter_context(nc.sbuf_tensor(name, shape, dt))

    def sem(name):
        return ctx.enter_context(nc.semaphore(name))

    w_sb = sb("w_sb", [P, DC, D + 2 * P])
    mem_sb = sb("mem_sb", [P, P])
    memn_sb = sb("memn_sb", [P, 1])
    rw_sb = sb("rw_sb", [P, DC, E])
    eb_sb = sb("eb_sb", [P, E])
    identb = sb("identb", [P, P], BF16)
    before = sb("before", [P, P], BF16)
    ones = sb("ones", [P, P], BF16)
    gate = sb("gate", [P, 4])
    half = sb("half", [P, 2])
    x_sb = sb("x_sb", [P, 2, D])
    xn = sb("xn", [P, 2, D])
    xnT = sb("xnT", [P, DC, UT])
    stats = sb("stats", [P, 2, 6])
    mv = sb("mv", [P, 2, 2])
    rs = sb("rs", [P, 4, 2])
    qf = sb("qf", [P, NQ + 1, UT])
    rest = sb("rest", [P, NQ + 1, UT])
    parts = sb("parts", [P, NQ + 1, PARTS, UT], BF16)
    sg = sb("sg", [P, NQ, UT])
    sig = sb("sig", [P, NQ, UT])
    rn = sb("rn", [P, 2, 2, NQ])
    am = sb("am", [P, 2, D])
    v_all = sb("v_all", [P, T // P, P])
    qs = sb("qs", [P, 4, NQ, SEQ], BF16)
    ks = sb("ks", [P, 4, SEQ], BF16)
    vs = sb("vs", [P, 4, 4, 32])
    prob = sb("prob", [P, 4, NQ, SEQ])
    mx = sb("mx", [P, 2, 16])
    mb = sb("mb", [P, 2, 2, 16], BF16)
    mT = sb("mT", [32, 2, P], BF16)
    oT = sb("oT", [P, SEQ])
    rec = sb("rec", [P, 16])
    o_all = sb("o_all", [P, 8, 16, 4, DH])
    xm_sb = sb("xm_sb", [P, 2, D])
    x2 = sb("x2", [P, 2, D])
    xn2 = sb("xn2", [P, 2, D])
    xn2T = sb("xn2T", [P, DC, UT])
    stats2 = sb("stats2", [P, 2, 6])
    mv2 = sb("mv2", [P, 2, 2])
    rs2 = sb("rs2", [P, 4, 2])
    rt = sb("rt", [P, 3, 2, E])
    top8 = sb("top8", [P, 2, 8])
    idx8 = sb("idx8", [P, 2, 8], U32)
    idxf = sb("idxf", [P, 2, K])
    mk = sb("mk", [P, 2, K, E])
    mw = sb("mw", [P, 2, K, E])
    mkb = sb("mkb", [P, 2, E], BF16)
    wk4 = sb("wk4", [P, 3, 2, K])
    rk = sb("rk", [P, 2, 2, E])
    slotf = sb("slotf", [P, 2, K])
    slot_now = sb("slot_now", [P, 2, K], U32)

    ps_max = ctx.enter_context(nc.psum_tensor("ps_max", [P, 2, 2, SEQ], F32))
    ps_exp = ctx.enter_context(nc.psum_tensor("ps_exp", [P, 2, SEQ], F32))
    ps_pv = ctx.enter_context(nc.psum_tensor("ps_pv", [P, SEQ], F32))
    ps_misc = ctx.enter_context(nc.psum_tensor("ps_misc", [P, SEQ], F32))
    misc_b = ps_misc[:, :].bitcast(BF16)

    identf, iota16, iotap, ebase, cnt, w_all, slot_all, e_all = (
        keep[k] for k in ("identf", "iota16", "iotap", "ebase", "cnt", "w_all", "slot_all", "e_all"))
    QK, XM, X2, XN2, XS = (scratch[k] for k in ("QK", "XM", "X2", "XN2", "XS"))
    STRIDE, ZERO_ROW = sizes(T)

    s_w = sem("s_weights")
    s_eb = sem("s_router_weights")
    s_const = sem("s_constants")
    s_cst = sem("s_constants_dve")
    s_cstp = sem("s_constants_pool")
    s_gate = sem("s_gate")
    s_x = sem("s_x_loaded")
    s_bn = sem("s_bn")
    s_mv = sem("s_mean_var")
    s_rst = sem("s_rstd_steps")
    s_rstd = sem("s_rstd")
    s_xn = sem("s_xn")
    s_xnTp = sem("s_xnT_in_psum")
    s_xnT = sem("s_xnT")
    s_proj = sem("s_proj_in_psum")
    s_qf = sem("s_qkv_in_sbuf")
    s_v = sem("s_v")
    s_eq = sem("s_exp_q")
    s_eq1 = sem("s_exp_q_minus_1")
    s_sig = sem("s_sigma")
    s_split = sem("s_split_steps")
    s_parts = sem("s_parts")
    s_qk = sem("s_qk_stored")
    s_den = sem("s_mem_norm_in_psum")
    s_rn = sem("s_mem_norm_steps")
    s_amp = sem("s_mem_in_psum")
    s_am = sem("s_mem_read")
    s_xmst = sem("s_xm_stored")
    s_stage = [sem(f"s_head_staged{k}") for k in range(4)]
    s_maxp = sem("s_scores_for_max")
    s_maxd = sem("s_max_taken")
    s_mh = sem("s_max_high")
    s_mb = sem("s_max_parts")
    s_mTp = sem("s_maxT_in_psum")
    s_mT = sem("s_maxT")
    s_mrow = [sem(f"s_max_rows{k}") for k in range(4)]
    s_sc = sem("s_scores")
    s_exp = sem("s_exp")
    s_vs = sem("s_vs")
    s_pv = sem("s_pv")
    s_oT = sem("s_oT")
    s_otp = sem("s_o_in_psum")
    s_rec = sem("s_o_reciprocal")
    s_o = sem("s_o")
    s_misc = sem("s_misc_free")
    s_xml = sem("s_xm_loaded")
    s_x2 = sem("s_x2")
    s_x2st = sem("s_x2_xn2_stored")
    s_bn2 = sem("s_bn2")
    s_mv2 = sem("s_mean_var2")
    s_rst2 = sem("s_rstd2_steps")
    s_rstd2 = sem("s_rstd2")
    s_xn2 = sem("s_xn2")
    s_xn2Tp = sem("s_xn2T_in_psum")
    s_xn2T = sem("s_xn2T")
    s_lg = sem("s_logits")
    s_el = sem("s_exp_logits")
    s_rt = sem("s_router_steps")
    s_mkb = sem("s_chosen")
    s_rkp = sem("s_rank_in_psum")
    s_rt2 = sem("s_slot_steps")
    s_slot = sem("s_slots")
    s_sct = sem("s_scattered")
    s_spg = sem("s_sp_gate")
    s_plg = sem("s_pool_gate")
    s_dvg = sem("s_dve_gate")

    QK_DMAS = NH * 16
    STAGED = 9 * 16
    ROUTER = 13
    SLOTS = 6

    NB = NU
    PHASES = [(0, None, None, 1), (1, None, None, 2), (3, 0, None, 1), (4, 1, None, 2), (6, 3, 0, 1), (7, 4, 1, NU - 7),
              (None, NB - 3, NU - 6, 1), (None, NB - 2, NU - 5, 2), (None, NB, NU - 3, 1), (None, None, NU - 2, 2)]

    def phases(eng, body):
        for a0, b0, c0, repeats in PHASES:
            if repeats == 1:
                body(a0, b0, c0)
            else:
                with eng.Fori(0, repeats) as r:
                    body(*(None if i is None else r + i for i in (a0, b0, c0)))

    def heads_of(b):
        return [(k, 4 * b + k) for k in range(4)]

    MID, END = 0.0, 0.5

    def schedule(a, c, of_a, of_c):
        def at(place):
            for of, unit in ((of_a, a), (of_c, c)):
                for task in of.get(place, []) if unit is not None else []:
                    task()
        return at

    def alone(at):
        for e in range(16):
            at(e + MID)
            at(e + END)

    def runs(g, lo, hi):
        return lo <= g < hi if isinstance(g, int) else True

    NG = 4 * NB

    block = ctx.enter_context(nc.Block())

    @block.sync
    def _(sp):
        def wait(s, n):
            sp.wait_ge(s, n)
            sp.sem_inc(s_spg, 1)

        sp.dma_start(identf[:], scratch["c_identf"]).then_inc(s_const, 16)
        sp.dma_start(iota16[:], scratch["c_iota16"]).then_inc(s_const, 16)
        sp.dma_start(iotap[:], scratch["c_iotap"]).then_inc(s_const, 16)
        sp.dma_start(rest[:, 0, 0:P], scratch["c_before"]).then_inc(s_const, 16)
        sp.dma_start(gate[:, 0:1], memory_weight.partition_broadcast(P)).then_inc(s_const, 16)

        def store_xm(a):
            wait(s_am, 2 * a + 2)
            sp.dma_start(XM[bass.ds(a, 1)].rearrange("o t p d -> (o p) t d"), am[:]).then_inc(s_xmst, 16)

        def load_x(a):
            if not (isinstance(a, int) and a == 0):
                store_xm(a - 1)
            rows = x.rearrange("(u t p) d -> p u t d", p=P, t=2)
            sp.dma_start(x_sb[:], rows[:, bass.ds(a, 1), :, :]).then_inc(s_x, 16)

        def stage_head(b, k, g):
            if not (isinstance(g, int) and g < 4):
                wait(s_sc, 16 * g - 48)
            if k == 0:
                wait(s_qk, QK_DMAS * 2 * (b // 2) + 2 * QK_DMAS)
            src = QK[bass.ds(b, 1), k]
            q = src[:, 0:NQ].rearrange("o q r t -> (o r) q t")
            kk = src[:, NQ].rearrange("o r t -> (o r) t")
            for to, n in ((0, 3), (3, 2), (5, 1)):
                sp.dma_start(qs[to * DH:(to + n) * DH, k], q[0:n * DH]).then_inc(s_stage[k], 16)
            for to, part in enumerate((0, 0, 0, 1, 1, 2)):
                sp.dma_start(ks[to * DH:(to + 1) * DH, k], kk[part * DH:(part + 1) * DH]).then_inc(s_stage[k], 16)

        def max_rows(g, k):
            wait(s_mT, g + 1)
            for part in range(MROWS):
                sp.dma_start(qs[ROWS + part:ROWS + part + 1, k].rearrange("p q (s j) -> p (q s) j", j=P),
                             mT[16 * part:16 * part + 16, k % 2]).then_inc(s_mrow[k], 16)

        def loads(a, b, c):
            if a is not None:
                load_x(a)
            elif isinstance(b, int) and b == NB - 3:
                store_xm(NU - 1)
            if c is not None:
                if not (isinstance(c, int) and c == 0):
                    wait(s_x2, 2 * c)
                wait(s_xmst, 16 * c + 16)
                sp.dma_start(xm_sb[:], XM[bass.ds(c, 1)].rearrange("o t p d -> (o p) t d")).then_inc(s_xml, 16)

        def body(a, b, c):
            if b is not None:
                for k, g in heads_of(b):
                    if k == 1:
                        loads(a, b, c)
                    if runs(g, 0, NG):
                        stage_head(b, k, g)
                    if runs(g, 2, NG + 2):
                        max_rows(g - 2, (k + 2) % 4)
            else:
                loads(a, b, c)
            if c is not None:
                wait(s_x2, 2 * c + 2)
                sp.dma_start(X2[bass.ds(c, 1)].rearrange("o t p d -> (o p) t d"), x2[:]).then_inc(s_x2st, 16)
                wait(s_xn2, 2 * c + 2)
                sp.dma_start(XN2[bass.ds(c, 1)].rearrange("o t p d -> (o p) t d"), xn2[:]).then_inc(s_x2st, 16)

        sp.dma_start(w_sb[:, :, 0:D], wq).then_inc(s_w, 16)
        sp.dma_start(w_sb[:, :, D:D + P], wk).then_inc(s_w, 16)
        sp.dma_start(w_sb[:, :, D + P:], wv).then_inc(s_w, 16)
        sp.dma_start(mem_sb[:], memory).then_inc(s_w, 16)
        sp.dma_start(memn_sb[:], memory_norm).then_inc(s_w, 16)
        sp.dma_start(rw_sb[:], router_w).then_inc(s_eb, 16)
        sp.dma_start(eb_sb[:], e_bias.partition_broadcast(P)).then_inc(s_eb, 16)
        sp.dma_start(ebase[:], scratch["c_ebase"]).then_inc(s_eb, 16)
        phases(sp, body)
        sp.wait_ge(s_x2st, 32 * NU)

    @block.gpsimd
    def _(pool):
        def wait(s, n):
            pool.wait_ge(s, n)
            pool.sem_inc(s_plg, 1)

        def copy(out, in_):
            return pool.tensor_scalar(out, in_, 1.0, 0.0, ALU.mult, ALU.add)

        pool.memset(half[:], -0.5).then_inc(s_cstp, 1)
        pool.memset(vs[:], 0.0).then_inc(s_cstp, 1)
        pool.wait_ge(s_cstp, 2)
        pool.memset(vs[:, :, :, DH:DH + 1], 1.0).then_inc(s_cstp, 1)
        pool.wait_ge(s_cstp, 3)

        def rstd(u, mv_, rs_, ready, steps, done):
            wait(ready, 2 * u + 2)
            var = mv_[:, :, 1]
            pool.tensor_scalar(rs_[:, 0, :], var, 1.0, EPS, ALU.mult, ALU.add).then_inc(steps, 1)
            wait(steps, 5 * u + 1)
            pool.tensor_tensor(rs_[:, 1, :], rs_[:, 0, :], half[:], ALU.pow).then_inc(steps, 1)
            wait(steps, 5 * u + 2)
            pool.tensor_tensor(rs_[:, 2, :], rs_[:, 0, :], rs_[:, 1, :], ALU.mult).then_inc(steps, 1)
            wait(steps, 5 * u + 3)
            pool.tensor_tensor(rs_[:, 2, :], rs_[:, 2, :], rs_[:, 1, :], ALU.mult).then_inc(steps, 1)
            wait(steps, 5 * u + 4)
            pool.tensor_scalar(rs_[:, 2, :], rs_[:, 2, :], -0.5, 1.5, ALU.mult, ALU.add).then_inc(steps, 1)
            wait(steps, 5 * u + 5)
            pool.tensor_tensor(rs_[:, 3, :], rs_[:, 1, :], rs_[:, 2, :], ALU.mult).then_inc(done, 1)

        def split(a):
            wait(s_qf, 3 * a + 3)
            if not (isinstance(a, int) and a == 0):
                wait(s_qk, QK_DMAS * a)
            copy(parts[:, :, 0], qf[:]).then_inc(s_split, 1)
            wait(s_split, 3 * a + 1)
            pool.tensor_tensor(rest[:], qf[:], parts[:, :, 0], ALU.subtract).then_inc(s_split, 1)
            wait(s_split, 3 * a + 2)
            copy(parts[:, :, 1], rest[:]).then_inc(s_split, 1)
            wait(s_split, 3 * a + 3)
            pool.tensor_tensor(parts[:, :, 2], rest[:], parts[:, :, 1], ALU.subtract).then_inc(s_parts, 1)

        def store_split(a):
            wait(s_parts, a + 1)
            for h in range(NH):
                dst = QK[bass.ds(2 * (a // 2) + h // 4, 1), h % 4].rearrange("o q (s d) t -> (o d) (q s) t", d=DH)
                pool.dma_start(dst[:, :, bass.ds((a % 2) * UT, UT)],
                               parts[h * DH:(h + 1) * DH].rearrange("p q s t -> p (q s) t")).then_inc(s_qk, 16)

        def stage_v(b, k, g):
            if not (isinstance(g, int) and g < 4):
                wait(s_pv, 4 * g - 12)
            if k == 0:
                wait(s_v, 2 * (b // 2) + 2)
            src = v_all[:, bass.ds((b // 2) * 4, 4), bass.ds((b % 2) * 4 * DH + k * DH, DH)]
            pool.tensor_copy(vs[:, k, :, 0:DH], src).then_inc(s_vs, 1)

        def scatter(c):
            wait(s_slot, c + 1)
            wait(s_xn2, 2 * c + 2)
            for t in range(2):
                for j in range(K):
                    at = slot_now[:, t, j:j + 1]
                    pool.indirect_dma_start(XS, bass.IndirectOffsetOnAxis(ap=at, axis=0), xn2[:, t], None).then_inc(s_sct, 16)

        def body(a, b, c):
            def head_v(k):
                if b is not None and runs(4 * b + k, 0, NG):
                    stage_v(b, k, 4 * b + k)

            head_v(0)
            head_v(1)
            if a is not None:
                rstd(a, mv, rs, s_mv, s_rst, s_rstd)
            if c is not None:
                rstd(c, mv2, rs2, s_mv2, s_rst2, s_rstd2)
            head_v(2)
            if a is not None:
                split(a)
            head_v(3)
            if a is not None:
                store_split(a)
            if c is not None:
                scatter(c)

        phases(pool, body)
        pool.wait_ge(s_sct, NU * 2 * K * 16)

    @block.scalar
    def _(act):
        act.wait_ge(s_const, 16 * 5)
        act.activation(gate[:, 1:2], gate[:, 0:1], ACT.Exp, scale=-1.0).then_inc(s_gate, 1)

        def body(a, b, c):
            def xnT_out(t):
                act.wait_ge(s_xnTp, 2 * a + t + 1)
                act.activation(xnT[:, :, t * P:(t + 1) * P], ps_misc[:, :].rearrange("p (c t) -> p c t", c=DC),
                               ACT.Copy).then_inc(s_xnT, 1)

            def q_out(j):
                act.wait_ge(s_proj, 3 * a + j + 1)
                if j == 0 and not (isinstance(a, int) and a == 0):
                    act.wait_ge(s_parts, a)
                    act.wait_ge(s_sig, a)
                act.activation(qf[:, 2 * j:2 * j + 2], ps_misc[:, :].rearrange("p (q t) -> p q t", q=2),
                               ACT.Copy).then_inc(s_qf, 1)

            def kv_out():
                act.wait_ge(s_proj, 3 * a + 3)
                act.activation(v_all[:, bass.ds(2 * a, 2)], ps_misc[:, UT:].rearrange("p (t f) -> p t f", t=2),
                               ACT.Copy).then_inc(s_v, 1)
                act.activation(qf[:, NQ], ps_misc[:, 0:UT], ACT.Copy).then_inc(s_qf, 1)

            def exp_q():
                act.wait_ge(s_qf, 3 * a + 3)
                act.activation(sg[:], qf[:, 0:NQ], ACT.Exp).then_inc(s_eq, 1)

            def xn2T_out(t):
                act.wait_ge(s_xn2Tp, 2 * c + t + 1)
                act.activation(xn2T[:, :, t * P:(t + 1) * P], ps_misc[:, :].rearrange("p (c t) -> p c t", c=DC),
                               ACT.Copy).then_inc(s_xn2T, 1)

            def exp_logits():
                act.wait_ge(s_lg, c + 1)
                act.activation(rt[:, 0], ps_misc[:, 0:2 * E].rearrange("p (t e) -> p t e", t=2), ACT.Exp,
                               scale=-1.0).then_inc(s_el, 1)

            at = schedule(a, c, {5: [lambda: xnT_out(0)], 6: [lambda: xnT_out(1)], 7: [lambda: q_out(0)],
                                 8: [lambda: q_out(1)], 9: [kv_out, exp_q]},
                          {7 + END: [lambda: xn2T_out(0)], 8 + END: [lambda: xn2T_out(1)], 11 + END: [exp_logits]})

            def exps(g, s, qs_):
                for q in qs_:
                    n = 16 * g + 4 * s + q - 32
                    act.wait_ge(s_sc, n + 1)
                    if q == 0 and not (isinstance(g, int) and g < 3):
                        act.wait_ge(s_pv, 4 * g + s - 11)
                    act.activation(prob[:, s, q], ps_exp[:, q % 2], ACT.Exp, scale=SCALE).then_inc(s_exp, 1)

            def oT_out(g):
                act.wait_ge(s_pv, 4 * g - 8)
                if not (isinstance(g, int) and g == 3):
                    act.wait_ge(s_otp, g - 3)
                act.activation(oT[:], ps_pv[:], ACT.Copy).then_inc(s_oT, 1)

            def mT_out(g, k):
                act.wait_ge(s_mTp, g)
                if not (isinstance(g, int) and g < 3):
                    times = (g - 3) // 4 + 1 if isinstance(g, int) else b + (k == 3)
                    act.wait_ge(s_mrow[(k + 1) % 4], 16 * MROWS * times)
                act.activation(mT[:, (k + 1) % 2], misc_b[0:32, 0:P], ACT.Copy).then_inc(s_mT, 1)

            if b is None:
                alone(at)
                return
            for k, g in heads_of(b):
                for s in range(4):
                    if runs(g, 2, NG + 2):
                        exps(g, s, (0, 1))
                    at(4 * k + s + MID)
                    if runs(g, 2, NG + 2):
                        exps(g, s, (2, 3))
                    at(4 * k + s + END)
                    if s == 0 and runs(g, 3, NG + 3):
                        oT_out(g)
                    if s == 1 and runs(g, 1, NG + 1):
                        mT_out(g, k)

        phases(act, body)

    @block.vector
    def _(dve):
        dve.memset(ones[:], 1.0).then_inc(s_cst, 1)
        dve.memset(ks[ROWS:ROWS + 32, :, :], 1.0).then_inc(s_cst, 1)
        dve.memset(cnt[:], 0.0).then_inc(s_cst, 1)
        dve.wait_ge(s_gate, 1)
        dve.tensor_scalar(gate[:, 2:3], gate[:, 1:2], 1.0, None, ALU.add).then_inc(s_gate, 1)
        dve.wait_ge(s_gate, 2)
        dve.reciprocal(gate[:, 1:2], gate[:, 2:3]).then_inc(s_gate, 1)
        dve.wait_ge(s_gate, 3)
        dve.tensor_scalar(gate[:, 3:4], gate[:, 1:2], -1.0, 1.0, ALU.mult, ALU.add).then_inc(s_gate, 1)
        dve.wait_ge(s_gate, 4)
        dve.wait_ge(s_cst, 3)
        dve.wait_ge(s_eb, 48)
        dve.wait_ge(s_const, 16 * 5)
        dve.tensor_copy(identb[:], identf[:]).then_inc(s_cst, 1)
        dve.tensor_copy(before[:], rest[:, 0, 0:P]).then_inc(s_cst, 1)
        dve.sem_inc(s_misc, 1)

        def gated(s, n):
            dve.wait_ge(s, n)
            dve.sem_inc(s_dvg, 1)

        def body(a, b, c):
            def stats_of(u, src, st, mv_, bn, done):
                for t in range(2):
                    dve.bn_stats(st[:, t], src[:, t]).then_inc(bn, 1)
                    gated(bn, 2 * u + t + 1)
                    dve.bn_aggr(mv_[:, t], st[:, t]).then_inc(done, 1)

            def normalise(u, src, out, mv_, rs_, ready, done):
                dve.wait_ge(ready, u + 1)
                for t in range(2):
                    dve.tensor_scalar(out[:, t], src[:, t], mv_[:, t, 0:1], rs_[:, 3, t:t + 1], ALU.subtract,
                                      ALU.mult).then_inc(done, 1)

            def a_stats():
                gated(s_x, 16 * a + 16)
                stats_of(a, x_sb, stats, mv, s_bn, s_mv)

            def a_norm():
                if not (isinstance(a, int) and a == 0):
                    dve.wait_ge(s_xnTp, 2 * a)
                normalise(a, x_sb, xn, mv, rs, s_rstd, s_xn)

            def a_elu():
                dve.wait_ge(s_eq, a + 1)
                dve.tensor_scalar(sg[:], sg[:], 1.0, -1.0, ALU.min, ALU.add).then_inc(s_eq1, 1)
                dve.wait_ge(s_eq1, a + 1)
                dve.tensor_tensor(sig[:], qf[:, 0:NQ], sg[:], ALU.max).then_inc(s_sig, 1)

            def mem_norm():
                dve.wait_ge(s_den, a + 1)
                dve.reciprocal(rn[:, 0], ps_misc[:, 0:2 * NQ].rearrange("p (t q) -> p t q", t=2)).then_inc(s_rn, 1)
                dve.wait_ge(s_rn, 2 * a + 1)
                dve.tensor_scalar(rn[:, 1], rn[:, 0], gate[:, 1:2], None, ALU.mult).then_inc(s_rn, 1)

            def mem_out(t):
                dve.wait_ge(s_rn, 2 * a + 2)
                dve.wait_ge(s_amp, 2 * a + t + 1)
                if t == 0 and not (isinstance(a, int) and a == 0):
                    dve.wait_ge(s_xmst, 16 * a)
                for q in range(NQ):
                    f = slice(q * P, (q + 1) * P)
                    last = dve.scalar_tensor_tensor(am[:, t, f], ps_misc[:, f], rn[:, 1, t, q:q + 1], x_sb[:, t, f],
                                                    ALU.mult, ALU.add)
                last.then_inc(s_am, 1)

            def c_residual():
                dve.wait_ge(s_xml, 16 * c + 16)
                dve.wait_ge(s_o, 8 * (c // 2) + 8)
                if not (isinstance(c, int) and c == 0):
                    dve.wait_ge(s_x2st, 32 * c)
                for t in range(2):
                    for hf in range(2):
                        ring = (2 * (c // 2) + hf) % 8
                        o = o_all[:, bass.ds(ring, 1), bass.ds((2 * (c % 2) + t) * NQ, NQ)].rearrange("p r q h d -> p (r q) (h d)")
                        x4 = x2[:, t].rearrange("p (q v f) -> p q v f", q=NQ, v=2)[:, :, hf]
                        m4 = xm_sb[:, t].rearrange("p (q v f) -> p q v f", q=NQ, v=2)[:, :, hf]
                        last = dve.scalar_tensor_tensor(x4, o, gate[:, 3:4], m4, ALU.mult, ALU.add)
                    last.then_inc(s_x2, 1)

            def c_stats():
                gated(s_x2, 2 * c + 2)
                stats_of(c, x2, stats2, mv2, s_bn2, s_mv2)

            def c_norm():
                if not (isinstance(c, int) and c == 0):
                    dve.wait_ge(s_sct, 2 * K * 16 * c)
                    dve.wait_ge(s_xn2Tp, 2 * c)
                normalise(c, x2, xn2, mv2, rs2, s_rstd2, s_xn2)

            def link(ins, n):
                ins.then_inc(s_rt, 1)
                gated(s_rt, ROUTER * c + n)

            def router():
                dve.wait_ge(s_el, c + 1)
                link(dve.tensor_scalar(rt[:, 2], rt[:, 0], 1.0, None, ALU.add), 1)
                link(dve.reciprocal(rt[:, 1], rt[:, 2]), 2)
                link(dve.tensor_tensor(rt[:, 2], rt[:, 1], eb_sb[:, :].unsqueeze(1).to_broadcast([P, 2, E]), ALU.add), 3)
                for t in range(2):
                    link(dve.max(top8[:, t], rt[:, 2, t]), 4 + t)
                for t in range(2):
                    link(dve.max_index(idx8[:, t], top8[:, t], rt[:, 2, t]), 6 + t)

            def chosen():
                link(dve.tensor_copy(idxf[:], idx8[:, :, 0:K]), 8)
                link(dve.tensor_tensor(mk[:], iota16[:, 0:E].unsqueeze(1).unsqueeze(1).to_broadcast([P, 2, K, E]),
                                       idxf[:, :, :].unsqueeze(3).to_broadcast([P, 2, K, E]), ALU.is_equal), 9)
                dve.tensor_reduce(mkb[:], mk[:, :, :, :].rearrange("p t k e -> p t e k"), AX_X, ALU.max).then_inc(s_mkb, 1)
                link(dve.tensor_tensor(mw[:], mk[:], rt[:, 1].unsqueeze(2).to_broadcast([P, 2, K, E]), ALU.mult), 10)
                link(dve.tensor_reduce(wk4[:, 0], mw[:], AX_X, ALU.add), 11)
                link(dve.tensor_reduce(wk4[:, 1, :, 0:1], wk4[:, 0], AX_X, ALU.add), 12)
                dve.tensor_scalar(wk4[:, 1, :, 1:2], wk4[:, 1, :, 0:1], 1e-20, None, ALU.add).then_inc(s_rt, 1)
                dve.wait_ge(s_rt, ROUTER * c + 13)

            def slots():
                def link(ins, n):
                    ins.then_inc(s_rt2, 1)
                    dve.wait_ge(s_rt2, SLOTS * c + n)

                link(dve.reciprocal(wk4[:, 2, :, 0:1], wk4[:, 1, :, 1:2]), 1)
                link(dve.tensor_tensor(w_all[:, bass.ds(2 * c, 2)], wk4[:, 0], wk4[:, 2, :, 0:1].to_broadcast([P, 2, K]),
                                       ALU.mult), 2)
                dve.wait_ge(s_rkp, c + 1)
                ranks = ps_misc[:, 0:3 * E].rearrange("p (t e) -> p t e", e=E)
                link(dve.tensor_tensor(rk[:, 0], ranks[:, 0:2], cnt[:, 0].unsqueeze(1).to_broadcast([P, 2, E]), ALU.add), 3)
                dve.tensor_tensor(cnt[:, 0], ranks[:, 2], cnt[:, 0], ALU.add).then_inc(s_misc, 1)
                link(dve.tensor_tensor(rk[:, 1], rk[:, 0], ebase[:, :].unsqueeze(1).to_broadcast([P, 2, E]), ALU.add), 4)
                link(dve.tensor_tensor(mw[:], mk[:], rk[:, 1].unsqueeze(2).to_broadcast([P, 2, K, E]), ALU.mult), 5)
                link(dve.tensor_reduce(slotf[:], mw[:], AX_X, ALU.add), 6)
                if not (isinstance(c, int) and c == 0):
                    dve.wait_ge(s_sct, 2 * K * 16 * c)
                dve.tensor_copy(slot_all[:, bass.ds(2 * c, 2)], slotf[:])
                dve.tensor_copy(e_all[:, bass.ds(2 * c, 2)], idxf[:])
                dve.tensor_copy(slot_now[:], slotf[:]).then_inc(s_slot, 1)

            at = schedule(a, c, {2: [a_stats], 4: [a_norm], 10: [a_elu], 12: [mem_norm], 13: [lambda: mem_out(0)],
                                 14: [lambda: mem_out(1)]},
                          {1: [c_residual], 3: [c_stats], 5: [c_norm], 12 + END: [router], 13 + END: [chosen],
                           15 + END: [slots]})

            def split_max(g, k):
                dve.wait_ge(s_maxd, 8 * g)
                j = (k + 1) % 2
                if not (isinstance(g, int) and g < 3):
                    dve.wait_ge(s_mTp, g - 2)
                dve.tensor_scalar(mb[:, j, 0], mx[:, j], -1.0, None, ALU.mult).then_inc(s_mh, 1)
                dve.wait_ge(s_mh, g)
                dve.scalar_tensor_tensor(mb[:, j, 1], mx[:, j], -1.0, mb[:, j, 0], ALU.mult, ALU.subtract).then_inc(s_mb, 1)

            def maxima(g, k, s, p):
                dve.wait_ge(s_maxp, 8 * g + 2 * s + p + 1)
                dve.tensor_reduce(mx[:, k % 2, 4 * s + 2 * p:4 * s + 2 * p + 2], ps_max[:, p], AX_X,
                                  ALU.max).then_inc(s_maxd, 1)

            def o_out(g, k):
                v = ps_misc[:, :].rearrange("p (n e) -> p n e", e=32)
                dve.wait_ge(s_otp, g - 2)
                dve.reciprocal(rec[:, :].unsqueeze(2), v[:, :, DH:DH + 1]).then_inc(s_rec, 1)
                dve.wait_ge(s_rec, g - 2)
                kk = (k + 1) % 4
                bb = b if k == 3 else b - 1
                dve.tensor_tensor(o_all[:, bass.ds(bb % 8, 1), :, kk].rearrange("p r n d -> p (r n) d"), v[:, :, 0:DH],
                                  rec[:, :].unsqueeze(2).to_broadcast([P, 16, DH]), ALU.mult).then_inc(s_o, 1)

            if b is None:
                alone(at)
                return
            for k, g in heads_of(b):
                for s in range(4):
                    if s == 0 and runs(g, 1, NG + 1):
                        split_max(g, k)
                    if runs(g, 0, NG):
                        maxima(g, k, s, 0)
                    at(4 * k + s + MID)
                    if runs(g, 0, NG):
                        maxima(g, k, s, 1)
                    at(4 * k + s + END)
                    if s == 2 and runs(g, 3, NG + 3):
                        o_out(g, k)

        phases(dve, body)

    @block.tensor
    def _(pe):
        pe.wait_ge(s_const, 16 * 5)
        pe.wait_ge(s_w, 16 * 5)
        pe.wait_ge(s_eb, 48)
        pe.wait_ge(s_cst, 5)

        def body(a, b, c):
            def free_misc():
                for s, n in last_use:
                    pe.wait_ge(s, n)

            def set_free(s, n):
                last_use[:] = [(s, n)]

            def transposes(src, t, ready, n, done):
                pe.wait_ge(ready, n)
                for i in range(DC):
                    mm = pe.transpose(ps_misc[:, i * P:(i + 1) * P], src[:, t, i * P:(i + 1) * P], identf[:])
                mm.then_inc(done, 1)

            def a_T(t):
                free_misc()
                transposes(xn, t, s_xn, 2 * a + t + 1, s_xnTp)
                set_free(s_xnT, 2 * a + t + 1)

            def a_q(j):
                free_misc()
                pe.wait_ge(s_xnT, 2 * a + 2)
                for q in range(2):
                    o = (2 * j + q) * P
                    for i in range(DC):
                        mm = pe.matmul(ps_misc[:, q * UT:(q + 1) * UT], w_sb[:, i, o:o + P], xnT[:, i], start=(i == 0),
                                       stop=(i == DC - 1))
                mm.then_inc(s_proj, 1)
                set_free(s_qf, 3 * a + j + 1)

            def a_kv():
                free_misc()
                for i in range(DC):
                    pe.matmul(ps_misc[:, 0:UT], w_sb[:, i, D:D + P], xnT[:, i], start=(i == 0), stop=(i == DC - 1))
                for t in range(2):
                    for i in range(DC):
                        mm = pe.matmul(ps_misc[:, UT + t * P:UT + (t + 1) * P], xnT[:, i, t * P:(t + 1) * P],
                                       w_sb[:, i, D + P:D + 2 * P], start=(i == 0), stop=(i == DC - 1))
                mm.then_inc(s_proj, 1)
                set_free(s_qf, 3 * a + 3)

            def a_den():
                free_misc()
                pe.wait_ge(s_sig, a + 1)
                for t in range(2):
                    for q in range(NQ):
                        mm = pe.matmul(ps_misc[:, t * NQ + q:t * NQ + q + 1], sig[:, q, t * P:(t + 1) * P], memn_sb[:],
                                       start=True, stop=True)
                mm.then_inc(s_den, 1)
                set_free(s_rn, 2 * a + 1)

            def a_mem(t):
                free_misc()
                for q in range(NQ):
                    mm = pe.matmul(ps_misc[:, q * P:(q + 1) * P], sig[:, q, t * P:(t + 1) * P], mem_sb[:], start=True,
                                   stop=True)
                mm.then_inc(s_amp, 1)
                set_free(s_am, 2 * a + t + 1)

            def c_T(t):
                free_misc()
                transposes(xn2, t, s_xn2, 2 * c + t + 1, s_xn2Tp)
                set_free(s_xn2T, 2 * c + t + 1)

            def c_logits():
                free_misc()
                pe.wait_ge(s_xn2T, 2 * c + 2)
                for t in range(2):
                    for i in range(DC):
                        mm = pe.matmul(ps_misc[:, t * E:(t + 1) * E], xn2T[:, i, t * P:(t + 1) * P], rw_sb[:, i],
                                       start=(i == 0), stop=(i == DC - 1))
                mm.then_inc(s_lg, 1)
                set_free(s_el, c + 1)

            def c_rank():
                free_misc()
                pe.wait_ge(s_mkb, c + 1)
                for to, terms in enumerate((((before, 0),), ((before, 1), (ones, 0)), ((ones, 0), (ones, 1)))):
                    for n, (m, t) in enumerate(terms):
                        mm = pe.matmul(ps_misc[:, to * E:(to + 1) * E], m[:], mkb[:, t], start=(n == 0),
                                       stop=(n == len(terms) - 1))
                mm.then_inc(s_rkp, 1)
                set_free(s_misc, c + 2)

            last_use = [(s_am, 2 * a)] if a is not None and (b is None or isinstance(b, int) and b == 0) else []
            if b is not None and not (isinstance(b, int) and b == 0):
                last_use.append((s_o, 4 * b - 3))
            if c is not None:
                last_use.append((s_misc, c + 1))
            if isinstance(a, int) and a == 0:
                last_use = []
            at = schedule(a, c, {5: [lambda: a_T(0)], 6: [lambda: a_T(1)], 7: [lambda: a_q(0)], 8: [lambda: a_q(1)],
                                 9: [a_kv], 12: [a_den], 13: [lambda: a_mem(0)], 14: [lambda: a_mem(1)]},
                          {7 + END: [lambda: c_T(0)], 8 + END: [lambda: c_T(1)], 11 + END: [c_logits], 15: [c_rank]})

            def scores_for_max(g, k, s, p):
                if not (isinstance(g, int) and 8 * g + 2 * s + p < 2):
                    pe.wait_ge(s_maxd, 8 * g + 2 * s + p - 1)
                if s == 0 and p == 0:
                    pe.wait_ge(s_stage[k], STAGED * (b + 1))
                for i in range(2):
                    st = 2 * p + i
                    mm = pe.matmul(ps_max[:, p, i], qs[0:ROWS, k, s, st * P:(st + 1) * P], ks[0:ROWS, k], start=True,
                                   stop=True)
                mm.then_inc(s_maxp, 1)

            def scores(g, k, s, qs_):
                kk = (k + 2) % 4
                for q in qs_:
                    n = 16 * g + 4 * s + q - 32
                    if not (isinstance(g, int) and n < 2):
                        pe.wait_ge(s_exp, n - 1)
                    if s == 0 and q == 0:
                        times = (g - 2) // 4 + 1 if isinstance(g, int) else (b + 1 if k >= 2 else b)
                        pe.wait_ge(s_mrow[kk], 16 * MROWS * times)
                    pe.matmul(ps_exp[:, q % 2], ks[0:ROWS + MROWS, kk, s * P:(s + 1) * P], qs[0:ROWS + MROWS, kk, q],
                              start=True, stop=True).then_inc(s_sc, 1)

            def pv(g, kk, t, n):
                pe.wait_ge(s_exp, 4 * n + 4)
                if t == 0:
                    if not (isinstance(g, int) and g == 2):
                        pe.wait_ge(s_oT, g - 2)
                    pe.wait_ge(s_vs, g - 1)
                for q in range(NQ):
                    mm = pe.matmul(ps_pv[32 * q:32 * q + 32, :], vs[:, kk, t], prob[:, t, q], start=(t == 0), stop=(t == 3))
                mm.then_inc(s_pv, 1)

            def max_T(g, k):
                free_misc()
                pe.wait_ge(s_mb, g)
                pe.transpose(misc_b[0:32, 0:P], mb[:, (k + 1) % 2].rearrange("p a n -> p (a n)"), identb[:]).then_inc(s_mTp, 1)
                set_free(s_mT, g)

            def o_T(g):
                free_misc()
                pe.wait_ge(s_oT, g - 2)
                for i in range(4):
                    mm = pe.transpose(ps_misc[:, i * P:(i + 1) * P], oT[:, i * P:(i + 1) * P], identf[:])
                mm.then_inc(s_otp, 1)
                set_free(s_o, g - 2)

            if b is None:
                alone(at)
                return
            for k, g in heads_of(b):
                for s in range(4):
                    for half_ in range(2):
                        if runs(g, 2, NG + 2):
                            scores(g, k, s, (2 * half_,))
                        if runs(g, 0, NG):
                            scores_for_max(g, k, s, half_)
                        if runs(g, 2, NG + 2):
                            scores(g, k, s, (2 * half_ + 1,))
                        if half_ == 0:
                            at(4 * k + s + MID)
                            if s == 0:
                                if runs(g, 3, NG + 3):
                                    pv(g - 1, (k + 1) % 4, 3, 4 * g - 9)
                            elif runs(g, 2, NG + 2):
                                pv(g, (k + 2) % 4, s - 1, 4 * g - 8 + s - 1)
                    at(4 * k + s + END)
                    if s == 1 and runs(g, 1, NG + 1):
                        max_T(g, k)
                    if s == 2 and runs(g, 3, NG + 3):
                        o_T(g)

        phases(pe, body)

    ctx.close()



def feed_forward(nc, T, io, keep, scratch, out):
    gu_w, dn_w, dnr_w, sgu_w, sdn_w, sdnr_w = io
    NT = T // P
    NR = NT * K + E
    NS0 = NT // 2
    R0, R1 = NS0, NS0 + NR
    NTILES = NT + NR
    LATE = 2
    NREST = NT - (NTILES - R1 - LATE)
    STRIDE, ZERO_ROW = sizes(T)
    ctx = ExitStack()

    def sb(name, shape, dt=F32):
        return ctx.enter_context(nc.sbuf_tensor(name, shape, dt))

    def sem(name):
        return ctx.enter_context(nc.semaphore(name))

    identf, iota16, iotap, ebase, cnt, w_all, slot_all, e_all = (
        keep[k] for k in ("identf", "iota16", "iotap", "ebase", "cnt", "w_all", "slot_all", "e_all"))
    X2, XN2, XS, Y, XO = (scratch[k] for k in ("X2", "XN2", "XS", "Y", "XO"))

    gu_sb = sb("gu_sb", [P, E, DC, 2 * I])
    dn_sb = sb("dn_sb", [P, E, D])
    dnr_sb = sb("dnr_sb", [P, E // 2, D])
    sgu_sb = sb("sgu_sb", [P, DC, 2 * I])
    sdn_sb = sb("sdn_sb", [P, D])
    sdnr_sb = sb("sdnr_sb", [IR, D])
    xt = sb("xt", [P, 2, D])
    xT = sb("xT", [P, 2, DC, P])
    gs = sb("gs", [P, 2, I])
    hid = sb("hid", [P, 2, 2, P])
    hT = sb("hT", [P, 2, 2, P])
    yt = sb("yt", [P, 2, D])
    x2t = sb("x2t", [P, 2, D])
    rows = sb("rows", [P, 2, K, D])
    acc = sb("acc", [P, 2, D])
    at_now = sb("at_now", [P, 2, K], U32)
    par = sb("par", [P, 2, NR])
    tab = sb("tab", [1, 2, NR], U32)
    small = sb("small", [P, 8, E])
    smi = sb("smi", [P, E], I32)
    zero = sb("zero", [P, D])
    shift = sb("shift", [P, NT * K])
    at_all = sb("at_all", [P, NT * K], U32)
    padf = sb("padf", [P, E])
    padi = sb("padi", [P, E], U32)
    ji = sb("ji", [P, NR], I32)
    room = rows[:, :, :, :].rearrange("p a k d -> p (a k d)")
    big = room[:, 0:NR * E].rearrange("p (j e) -> p j e", e=E)
    jrow = room[:, NR * E:NR * (E + 3)].rearrange("p (k j) -> p k j", k=3)
    jt = room[:, NR * (E + 3):NR * (E + 9)].rearrange("p (k j) -> p k j", k=6)

    ps_x = ctx.enter_context(nc.psum_tensor("ps_x", [P, 2, DC, P], F32))
    ps_gu = ctx.enter_context(nc.psum_tensor("ps_gu", [P, 2, D], F32))
    ps_h = ctx.enter_context(nc.psum_tensor("ps_h", [P, 2, DC, P], F32))
    ps_y = ctx.enter_context(nc.psum_tensor("ps_y", [P, 2, D], F32))

    s_ws = sem("f_shared_weights")
    s_wr = sem("f_routed_weights")
    s_tc = sem("f_table_constants")
    s_tb = sem("f_table_steps")
    s_tab = sem("f_tables")
    s_zero = sem("f_zero")
    s_pad = sem("f_pads")
    s_x = [sem(f"f_x_loaded{p}") for p in range(2)]
    s_xp = sem("f_xT_in_psum")
    s_xT = sem("f_xT")
    s_gu = sem("f_gate_up")
    s_si = sem("f_silu")
    s_h = sem("f_hidden")
    s_hp = sem("f_hT_in_psum")
    s_hT = sem("f_hT")
    s_yp = sem("f_y_in_psum")
    s_y = sem("f_y")
    s_yst = [sem(f"f_y_stored{p}") for p in range(2)]
    s_x2 = [sem(f"f_x2_loaded{p}") for p in range(2)]
    s_at = sem("f_rows_wanted")
    s_rows = [sem(f"f_rows{p}") for p in range(2)]
    s_acc = [sem(f"f_acc_loaded{p}") for p in range(2)]
    s_sum = sem("f_sum_steps")
    s_out = [sem(f"f_out_stored{p}") for p in range(2)]
    s_spg = sem("f_sp_gate")
    s_plg = sem("f_pool_gate")

    SHARED, ROUTED = 0, 1

    class Tile:

        def __init__(self, h, p):
            self.h, self.p, self.n = h, p, h * 2 + p

        def of(self, kind, late):
            self.kind, self.late = kind, late
            self.th = self.h - NR // 2 if late else self.h
            self.t = self.th * 2 + self.p
            self.j = None if kind == SHARED else self.n - R0
            return self

    RUNS = [run for h0, h1, kind, late in ((0, R0 // 2, SHARED, False), (R0 // 2, R1 // 2, ROUTED, False),
                                           (R1 // 2, NTILES // 2, SHARED, True))
            for run in ((h0, kind, late, 1), (h0 + 1, kind, late, h1 - h0 - 2), (h1 - 1, kind, late, 1))]

    def kind_of(h):
        return (SHARED, False) if h < R0 // 2 else (ROUTED, False) if h < R1 // 2 else (SHARED, True)

    def slots(eng, body):
        for h0, kind, late, repeats in RUNS:
            def pair(h, kinds):
                made = [Tile(h + i // 2, i % 2).of(*kinds(i // 2)) for i in range(-1, 5)]
                for p in range(2):
                    body(*made[p:p + 4])

            if repeats == 1:
                pair(h0, lambda i, h0=h0: kind_of(h0 + i))
            else:
                with eng.Fori(0, repeats) as r:
                    pair(r + h0, lambda i, kind=kind, late=late: (kind, late))

    def exists(tile):
        return not isinstance(tile.n, int) or 0 <= tile.n < NTILES

    def after(eng_wait, s, n):
        if not (isinstance(n, int) and n <= 0):
            eng_wait(s, n)

    block = ctx.enter_context(nc.Block())

    @block.sync
    def _(sp):
        def wait(s, n):
            sp.wait_ge(s, n)
            sp.sem_inc(s_spg, 1)

        def rows_of(dram, t):
            return dram[bass.ds(t, 1)].rearrange("o p d -> (o p) d")

        def load_x(tile):
            after(wait, s_xp, tile.n - 1)
            if tile.kind == SHARED:
                sp.dma_start(xt[:, tile.p], rows_of(XN2, tile.t)).then_inc(s_x[tile.p], 16)
            else:
                row = sp.value_load(tab[0:1, 0, bass.ds(tile.j, 1)], min_val=0, max_val=ZERO_ROW)
                sp.dma_start(xt[:, tile.p], XS[bass.ds(row, P)]).then_inc(s_x[tile.p], 16)

        def load_x2(tile):
            after(wait, s_y, tile.n - 1)
            sp.dma_start(x2t[:, tile.p], rows_of(X2, tile.t)).then_inc(s_x2[tile.p], 16)

        def store(tile):
            wait(s_y, tile.n + 1)
            if tile.kind == SHARED:
                sp.dma_start(rows_of(XO, tile.t), yt[:, tile.p]).then_inc(s_yst[tile.p], 16)
            else:
                sp.dma_start(rows_of(Y, tile.j), yt[:, tile.p]).then_inc(s_yst[tile.p], 16)

        def load_acc(th, p):
            after(wait, s_out[p], 16 * th)
            sp.dma_start(acc[:, p], rows_of(XO, 2 * th + p)).then_inc(s_acc[p], 16)

        def store_out(th, p):
            wait(s_sum, K * (2 * th + p) + K)
            sp.dma_start(rows_of(out, 2 * th + p), acc[:, p]).then_inc(s_out[p], 16)

        first = [Tile(0, p).of(SHARED, False) for p in range(2)]
        load_x(first[0])
        sp.dma_start(sgu_sb[:], sgu_w).then_inc(s_ws, 16)
        sp.dma_start(sdn_sb[:], sdn_w).then_inc(s_ws, 16)
        sp.dma_start(sdnr_sb[:], sdnr_w).then_inc(s_ws, 16)
        sp.dma_start(jrow, scratch["c_jrow"]).then_inc(s_tc, 16)
        load_x(first[1])
        load_x2(first[0])
        for e in range(0, E, 2):
            sp.dma_start(gu_sb[:, e:e + 2], gu_w[:, e:e + 2]).then_inc(s_wr, 16)
            sp.dma_start(dn_sb[:, e:e + 2], dn_w[:, e:e + 2]).then_inc(s_wr, 16)
        sp.dma_start(dnr_sb[:], dnr_w).then_inc(s_wr, 16)

        def body(before, tile, following, later):
            if exists(later):
                if isinstance(later.n, int) and later.n == R0:
                    wait(s_tab, 1)
                    wait(s_pad, 16 * (E + 1))
                load_x(later)
            if tile.late and not (isinstance(tile.n, int) and tile.n < R1 + LATE):
                load_acc(tile.th - R0 // 2 - LATE // 2, tile.p)
            if exists(before):
                store(before)
            if exists(following) and following.kind == SHARED:
                load_x2(following)
            if tile.late and not (isinstance(tile.n, int) and tile.n < R1 + LATE):
                store_out(tile.th - R0 // 2 - LATE // 2, tile.p)

        slots(sp, body)
        store(Tile(NTILES // 2 - 1, 1).of(SHARED, True))
        for p in range(2):
            sp.wait_ge(s_yst[p], 16 * (NTILES // 2))
        with sp.Fori(0, NREST // 2) as r:
            for p in range(2):
                load_acc(r + (NT - NREST) // 2, p)
            for p in range(2):
                store_out(r + (NT - NREST) // 2, p)
        for p in range(2):
            sp.wait_ge(s_out[p], 16 * (NT // 2))

    @block.gpsimd
    def _(pool):
        def wait(s, n):
            pool.wait_ge(s, n)
            pool.sem_inc(s_plg, 1)

        pool.memset(zero[:], 0.0).then_inc(s_zero, 1)
        wait(s_zero, 1)
        pool.dma_start(XS[ZERO_ROW:ZERO_ROW + P], zero[:]).then_inc(s_pad, 16)
        wait(s_tb, 2)
        for e in range(E):
            pool.indirect_dma_start(XS, bass.IndirectOffsetOnAxis(ap=padi[:, e:e + 1], axis=0), zero[:],
                                    None).then_inc(s_pad, 16)

        for p in range(2):
            wait(s_yst[p], 16 * (R1 // 2))
        with pool.Fori(0, NT // 2) as r:
            for p in range(2):
                wait(s_at, 2 * r + p + 1)
                for j in range(K):
                    pool.indirect_dma_start(rows[:, p, j], None, Y.rearrange("j p d -> (j p) d"),
                                            bass.IndirectOffsetOnAxis(ap=at_now[:, p, j:j + 1], axis=0)).then_inc(s_rows[p], 16)

    @block.scalar
    def _(act):
        def x_out(tile):
            act.wait_ge(s_xp, tile.n + 1)
            after(act.wait_ge, s_gu, tile.n - 1)
            act.activation(xT[:, tile.p], ps_x[:, tile.p], ACT.Copy).then_inc(s_xT, 1)

        def y_out(tile):
            act.wait_ge(s_yp, tile.n + 1)
            after(act.wait_ge, s_yst[tile.p], 16 * tile.h)
            act.activation(yt[:, tile.p], ps_y[:, tile.p], ACT.Copy).then_inc(s_y, 1)

        def body(before, tile, following, later):
            if exists(following):
                x_out(following)
            act.wait_ge(s_gu, tile.n + 1)
            act.activation(gs[:, tile.p], ps_gu[:, tile.p, 0:I], ACT.Silu).then_inc(s_si, 1)
            if exists(before) and before.kind == ROUTED:
                y_out(before)

        x_out(Tile(0, 0))
        slots(act, body)

    @block.vector
    def _(dve):
        steps = [0]

        def step(ins):
            steps[0] += 1
            ins.then_inc(s_tb, 1)
            dve.wait_ge(s_tb, steps[0])

        def tables():
            dve.wait_ge(s_tc, 16)
            step(dve.tensor_scalar(padf[:], cnt[:, 0], iotap[:, 0:1], None, ALU.add))
            step(dve.tensor_tensor(padi[:], padf[:], ebase[:], ALU.add))
            step(dve.tensor_scalar(smi[:], cnt[:, 0], float(P - 1), None, ALU.add))
            step(dve.tensor_scalar(smi[:], smi[:], 7, None, ALU.logical_shift_right))
            step(dve.tensor_copy(small[:, 0], smi[:]))
            for i, s in enumerate((1, 2, 4, 8)):
                step(dve.tensor_copy(small[:, i + 1, 0:s], small[:, i, 0:s]))
                step(dve.tensor_tensor(small[:, i + 1, s:E], small[:, i, s:E], small[:, i, 0:E - s], ALU.add))
            upto = small[:, 4]
            step(dve.tensor_tensor(small[:, 5], upto, small[:, 0], ALU.subtract))
            step(dve.scalar_tensor_tensor(small[:, 6], small[:, 5], -float(P), ebase[:], ALU.mult, ALU.add))
            bc = [P, NR, E]
            step(dve.tensor_tensor(big, jrow[:, 0].unsqueeze(2).to_broadcast(bc), upto.unsqueeze(1).to_broadcast(bc), ALU.is_ge))
            step(dve.tensor_reduce(jt[:, 0], big, AX_X, ALU.add))
            step(dve.tensor_scalar(jt[:, 1], jt[:, 0], float(E - 1), None, ALU.min))
            step(dve.tensor_scalar(jt[:, 2], jt[:, 0], float(E), None, ALU.is_lt))
            step(dve.tensor_tensor(big, jt[:, 1].unsqueeze(2).to_broadcast(bc), iota16[:, :].unsqueeze(1).to_broadcast(bc),
                                   ALU.is_equal))
            step(dve.tensor_tensor(big, big, small[:, 6].unsqueeze(1).to_broadcast(bc), ALU.mult))
            step(dve.tensor_reduce(jt[:, 3], big, AX_X, ALU.add))
            step(dve.tensor_tensor(jt[:, 3], jt[:, 3], jrow[:, 1], ALU.add))
            step(dve.tensor_tensor(jt[:, 4], jt[:, 3], jrow[:, 2], ALU.subtract))
            step(dve.tensor_tensor(jt[:, 5], jt[:, 4], jt[:, 2], ALU.mult))
            step(dve.tensor_tensor(tab[0:1, 0], jt[0:1, 5], jrow[0:1, 2], ALU.add))
            step(dve.tensor_copy(tab[0:1, 1], jt[0:1, 1]))
            step(dve.tensor_copy(ji[:], jt[:, 1]))
            step(dve.tensor_scalar(ji[:], ji[:], 1, None, ALU.bitwise_and))
            step(dve.tensor_copy(par[:, 1], ji[:]))
            dve.tensor_scalar(par[:, 0], par[:, 1], -1.0, 1.0, ALU.mult, ALU.add).then_inc(s_tab, 1)
            dve.wait_ge(s_tab, 1)

        def result_rows():
            bc = [P, NT * K, E]
            of_tokens = room[:, 0:NT * K * E].rearrange("p (n e) -> p n e", e=E)
            slots_ = slot_all[:, :, :].rearrange("p t k -> p (t k)")
            step(dve.tensor_tensor(of_tokens, e_all[:, :, :].rearrange("p t k -> p (t k)").unsqueeze(2).to_broadcast(bc),
                                   iota16[:, :].unsqueeze(1).to_broadcast(bc), ALU.is_equal))
            step(dve.tensor_tensor(of_tokens, of_tokens, small[:, 6].unsqueeze(1).to_broadcast(bc), ALU.mult))
            step(dve.tensor_reduce(shift[:], of_tokens, AX_X, ALU.add))
            step(dve.tensor_tensor(at_all[:], slots_, shift[:], ALU.subtract))

        def hT_out(tile):
            dve.wait_ge(s_hp, tile.n + 1)
            after(dve.wait_ge, s_yp, tile.n - 1)
            if tile.kind == ROUTED:
                dve.tensor_copy(hT[:, tile.p], ps_h[:, tile.p, 0:2]).then_inc(s_hT, 1)
            else:
                dve.tensor_copy(hT[:, tile.p, 0], ps_h[:, tile.p, 0])
                dve.tensor_copy(hT[0:IR, tile.p, 1], ps_h[0:IR, tile.p, 1]).then_inc(s_hT, 1)

        def hidden(tile):
            dve.wait_ge(s_si, tile.n + 1)
            after(dve.wait_ge, s_hp, tile.n - 1)
            up = ps_gu[:, tile.p, I:2 * I]
            h = hid[:, tile.p].rearrange("p a b -> p (a b)")
            if tile.kind == ROUTED:
                dve.tensor_tensor(h[:, 0:P], up[:, 0:P], gs[:, tile.p, 0:P], ALU.mult)
                for k in range(2):
                    last = dve.scalar_tensor_tensor(h[:, P + k * IR:P + (k + 1) * IR], up[:, P:I],
                                                    par[:, k, bass.ds(tile.j, 1)], gs[:, tile.p, P:I], ALU.mult, ALU.mult)
            else:
                last = dve.tensor_tensor(h[:, 0:I], up, gs[:, tile.p], ALU.mult)
            last.then_inc(s_h, 1)

        def y_sum(tile):
            dve.wait_ge(s_yp, tile.n + 1)
            dve.wait_ge(s_x2[tile.p], 16 * tile.th + 16)
            after(dve.wait_ge, s_yst[tile.p], 16 * tile.h)
            dve.tensor_tensor(yt[:, tile.p], ps_y[:, tile.p], x2t[:, tile.p], ALU.add).then_inc(s_y, 1)

        def want(th, p):
            dve.tensor_copy(at_now[:, p], at_all[:, bass.ds(K * (2 * th + p), K)]).then_inc(s_at, 1)

        def combine(th, p, last):
            dve.wait_ge(s_acc[p], 16 * th + 16)
            dve.wait_ge(s_rows[p], 16 * K * th + 16 * K)
            w = w_all[:, :, :].rearrange("p t k -> p (t k)")
            for j in range(K):
                dve.scalar_tensor_tensor(acc[:, p], rows[:, p, j], w[:, bass.ds(K * (2 * th + p) + j, 1)], acc[:, p],
                                         ALU.mult, ALU.add).then_inc(s_sum, 1)
                dve.wait_ge(s_sum, K * (2 * th + p) + j + 1)
            if not last:
                want(th + 1, p)

        def body(before, tile, following, later):
            if exists(before):
                hT_out(before)
            hidden(tile)
            if exists(before) and before.kind == SHARED:
                y_sum(before)
            if isinstance(tile.n, int) and tile.n == R0:
                result_rows()
            if isinstance(tile.n, int) and tile.n == R1:
                want(0, 0)
                want(0, 1)
            if tile.late and not (isinstance(tile.n, int) and tile.n < R1 + LATE):
                combine(tile.th - R0 // 2 - LATE // 2, tile.p, False)

        tables()
        slots(dve, body)
        end = Tile(NTILES // 2 - 1, 1).of(SHARED, True)
        hT_out(end)
        y_sum(end)
        with dve.Fori(0, NREST // 2 - 1) as r:
            for p in range(2):
                combine(r + (NT - NREST) // 2, p, False)
        for p in range(2):
            combine(NT // 2 - 1, p, True)

    @block.tensor
    def _(pe):
        def transpose_x(tile):
            pe.wait_ge(s_x[tile.p], 16 * tile.h + 16)
            after(pe.wait_ge, s_xT, tile.n - 1)
            for i in range(DC):
                mm = pe.transpose(ps_x[:, tile.p, i], xt[:, tile.p, i * P:(i + 1) * P], identf[:])
            mm.then_inc(s_xp, 1)

        def expert(tile):
            return pe.value_load(tab[0:1, 1, bass.ds(tile.j, 1)], min_val=0, max_val=E - 1)

        def gate_up(tile):
            if tile.kind == ROUTED:
                e = expert(tile)
            pe.wait_ge(s_xT, tile.n + 1)
            after(pe.wait_ge, s_h, tile.n - 1)
            for i in range(DC):
                w = sgu_sb[:, i] if tile.kind == SHARED else gu_sb[:, bass.ds(e, 1), i].rearrange("p o n -> p (o n)")
                mm = pe.matmul(ps_gu[:, tile.p, 0:2 * I], xT[:, tile.p, i], w, start=(i == 0), stop=(i == DC - 1))
            mm.then_inc(s_gu, 1)

        def transpose_h(tile):
            pe.wait_ge(s_h, tile.n + 1)
            after(pe.wait_ge, s_hT, tile.n - 1)
            pe.transpose(ps_h[:, tile.p, 0], hid[:, tile.p, 0], identf[:])
            if tile.kind == ROUTED:
                mm = pe.transpose(ps_h[:, tile.p, 1], hid[:, tile.p, 1], identf[:])
            else:
                mm = pe.transpose(ps_h[0:IR, tile.p, 1], hid[:, tile.p, 1, 0:IR], identf[:])
            mm.then_inc(s_hp, 1)

        def down(tile):
            if tile.kind == ROUTED:
                e = expert(tile)
            pe.wait_ge(s_hT, tile.n + 1)
            after(pe.wait_ge, s_y, tile.n - 1)
            if tile.kind == ROUTED:
                pe.matmul(ps_y[:, tile.p], hT[:, tile.p, 0], dn_sb[:, bass.ds(e, 1)].rearrange("p o n -> p (o n)"),
                          start=True, stop=False)
                mm = pe.matmul(ps_y[:, tile.p], hT[:, tile.p, 1], dnr_sb[:, bass.ds(e // 2, 1)].rearrange("p o n -> p (o n)"),
                               start=False, stop=True)
            else:
                pe.matmul(ps_y[:, tile.p], hT[:, tile.p, 0], sdn_sb[:], start=True, stop=False)
                mm = pe.matmul(ps_y[:, tile.p], hT[0:IR, tile.p, 1], sdnr_sb[:], start=False, stop=True)
            mm.then_inc(s_yp, 1)

        def body(before, tile, following, later):
            if isinstance(tile.n, int) and tile.n == R0:
                pe.wait_ge(s_wr, 16 * (E + 1))
                pe.wait_ge(s_tab, 1)
            if exists(before):
                transpose_h(before)
            if exists(following):
                transpose_x(following)
            gate_up(tile)
            if exists(before):
                down(before)

        transpose_x(Tile(0, 0))
        pe.wait_ge(s_ws, 48)
        slots(pe, body)
        end = Tile(NTILES // 2 - 1, 1).of(SHARED, True)
        transpose_h(end)
        down(end)

    ctx.close()


INPUTS = ["wq", "wk", "wv", "memory", "memory_norm", "memory_weight", "router_w", "e_bias"]


def build(nc, T, a, out):
    stride, zero_row = sizes(T)
    NU, NT = T // UT, T // P

    def dram(name, shape, dt=F32):
        return nc.dram_tensor(name, shape, dt).ap()

    scratch = {
        "QK": dram("qk_parts", [NU, NH // 2, NQ + 1, PARTS * DH, SEQ], BF16),
        "XM": dram("x_plus_memory", [NU, 2, P, D]),
        "X2": dram("x2_rows", [NU, 2, P, D]),
        "XN2": dram("xn2_rows", [NU, 2, P, D]),
        "XS": dram("rows_by_expert", [zero_row + P, D]),
        "Y": dram("results_by_expert", [NT * K + E, P, D]),
        "XO": dram("x2_plus_shared", [NT, P, D]),
    } | {k: v for k, v in a.items() if k.startswith("c_")}
    with ExitStack() as ctx:
        keep = kept(nc, ctx, T)
        attention(nc, T, [a["x"]] + [a[k] for k in INPUTS], keep, scratch)
        for k in ("X2", "XN2"):
            scratch[k] = scratch[k].rearrange("u t p d -> (u t) p d")
        feed_forward(nc, T, [a[k] for k in ("gu", "dn", "dnr", "sgu", "sdn", "sdnr")], keep, scratch,
                     out.rearrange("b (s p) d -> (b s) p d", p=P))


def constants(T):
    i = np.arange(P)
    stride, zero_row = sizes(T)
    nr = T // P * K + E
    j = np.arange(nr)
    jrow = np.stack([j, j * P, np.full(nr, zero_row)])
    return {
        "c_identf": np.eye(P, dtype=np.float32),
        "c_before": (i[:, None] < i[None, :]).astype(np.float32),
        "c_iota16": np.tile(np.arange(E, dtype=np.float32), (P, 1)),
        "c_iotap": i[:, None].astype(np.float32),
        "c_ebase": np.tile(np.arange(E, dtype=np.float32) * stride, (P, 1)),
        "c_jrow": np.tile(jrow.astype(np.float32), (P, 1, 1)),
    }


def kept(nc, ctx, T):
    def sb(name, shape, dt=F32):
        return ctx.enter_context(nc.sbuf_tensor(name, shape, dt))
    return {"identf": sb("identf", [P, P]), "iota16": sb("iota16", [P, E]), "iotap": sb("iotap", [P, 1]),
            "ebase": sb("ebase", [P, E]), "cnt": sb("cnt", [P, 1, E]), "w_all": sb("w_all", [P, T // P, K]),
            "slot_all": sb("slot_all", [P, T // P, K]), "e_all": sb("e_all", [P, T // P, K])}


def kernel(L0_attn_x, L0_attn_Wq, L0_attn_Wk, L0_attn_Wv, L0_attn_memory, L0_attn_memory_norm, L0_attn_memory_weight,
           L0_ffn_router_w, L0_ffn_e_bias, L0_ffn_gate_up_proj, L0_ffn_down_proj, L0_ffn_shared_gate_w,
           L0_ffn_shared_up_w, L0_ffn_shared_down_w):
    import concourse.bacc as bacc
    from concourse.bass_utils import run_bass_kernel_spmd

    def chunks(w, rows=P):
        w = np.asarray(w)
        return np.ascontiguousarray(w.reshape(w.shape[0] // rows, rows, -1).transpose(1, 0, 2))

    x = np.asarray(L0_attn_x)
    B, S, _ = x.shape
    T = B * S
    gu = np.asarray(L0_ffn_gate_up_proj)
    dn = np.asarray(L0_ffn_down_proj).transpose(0, 2, 1)
    sdn = np.asarray(L0_ffn_shared_down_w).T
    arrays = {
        "x": np.ascontiguousarray(x.reshape(T, D)),
        "wq": chunks(np.asarray(L0_attn_Wq).T),
        "wk": chunks(np.asarray(L0_attn_Wk).T),
        "wv": chunks(np.asarray(L0_attn_Wv).T),
        "memory": np.ascontiguousarray(L0_attn_memory),
        "memory_norm": np.ascontiguousarray(L0_attn_memory_norm),
        "memory_weight": np.ascontiguousarray(L0_attn_memory_weight),
        "router_w": chunks(np.asarray(L0_ffn_router_w).T),
        "e_bias": np.ascontiguousarray(L0_ffn_e_bias),
        "gu": np.ascontiguousarray(gu.transpose(2, 0, 1).reshape(DC, P, E, 2 * I).transpose(1, 2, 0, 3)),
        "dn": np.ascontiguousarray(dn[:, 0:P].transpose(1, 0, 2)),
        "dnr": np.ascontiguousarray(dn[:, P:I].reshape(E // 2, P, D).transpose(1, 0, 2)),
        "sgu": chunks(np.concatenate([np.asarray(L0_ffn_shared_gate_w), np.asarray(L0_ffn_shared_up_w)]).T),
        "sdn": np.ascontiguousarray(sdn[0:P]),
        "sdnr": np.ascontiguousarray(sdn[P:I]),
    } | constants(T)
    nc = bacc.Bacc("TRN2", target_bir_lowering=False, num_devices=1)
    a = {k: nc.dram_tensor(f"in_{k}", v.shape, mybir.dt.from_np(v.dtype), kind="ExternalInput").ap() for k, v in arrays.items()}
    out = nc.dram_tensor("out", [B, S, D], F32, kind="ExternalOutput").ap()
    build(nc, T, a, out)
    r = run_bass_kernel_spmd(nc, [{f"in_{k}": v for k, v in arrays.items()}], core_ids=[0])
    return r.results[0]["out"]
```

```python
from contextlib import ExitStack

import numpy as np

import concourse.bass as bass
from concourse import mybir

ALU = mybir.AluOpType
ACT = mybir.ActivationFunctionType
F32 = mybir.dt.float32
BF16 = mybir.dt.bfloat16
U32 = mybir.dt.uint32
I32 = mybir.dt.int32
AX_X = mybir.AxisListType.X

P = 128
D = 512
DC = D // P
SEQ = 512
NQ = 4
NH = 8
DH = 16
UT = 256
EPS = 1e-5
E = 16
K = 4
I = 192
IR = I - P
PARTS = 3
ROWS = 6 * DH
MROWS = 2
SCALE = 1.0 / float(np.sqrt(np.float32(DH)))


def sizes(T):
    stride = T + P
    return stride, E * stride


def attention(nc, T, io, shared, keep, scratch):
    x, wq, wk, wv, memory, memory_norm, memory_weight, router_w, e_bias = io
    NU = T // UT
    ctx = ExitStack()

    def sb(name, shape, dt=F32):
        return ctx.enter_context(nc.sbuf_tensor(name, shape, dt))

    def sem(name):
        return ctx.enter_context(nc.semaphore(name))

    w_sb = sb("w_sb", [P, DC, D + 2 * P])
    mem_sb = sb("mem_sb", [P, P])
    memn_sb = sb("memn_sb", [P, 1])
    rw_sb = sb("rw_sb", [P, DC, E])
    eb_sb = sb("eb_sb", [P, E])
    identb = sb("identb", [P, P], BF16)
    before = sb("before", [P, P], BF16)
    ones = sb("ones", [P, P], BF16)
    gate = sb("gate", [P, 4])
    half = sb("half", [P, 2])
    x_sb = sb("x_sb", [P, 2, D])
    xn = sb("xn", [P, 2, D])
    xnT = sb("xnT", [P, DC, UT])
    stats = sb("stats", [P, 2, 6])
    mv = sb("mv", [P, 2, 2])
    rs = sb("rs", [P, 4, 2])
    qf = sb("qf", [P, NQ + 1, UT])
    rest = sb("rest", [P, NQ + 1, UT])
    parts = sb("parts", [P, NQ + 1, PARTS, UT], BF16)
    sg = sb("sg", [P, NQ, UT])
    sig = sb("sig", [P, NQ, UT])
    rn = sb("rn", [P, 2, 2, NQ])
    am = sb("am", [P, 2, D])
    v_all = sb("v_all", [P, T // P, P])
    qs = sb("qs", [P, 4, NQ, SEQ], BF16)
    ks = sb("ks", [P, 4, SEQ], BF16)
    vs = sb("vs", [P, 4, 4, 32])
    prob = sb("prob", [P, 4, NQ, SEQ])
    mx = sb("mx", [P, 2, 16])
    mb = sb("mb", [P, 2, 2, 16], BF16)
    mT = sb("mT", [32, 2, P], BF16)
    oT = sb("oT", [P, SEQ])
    rec = sb("rec", [P, 16])
    o_all = sb("o_all", [P, 8, 16, 4, DH])
    xm_sb = sb("xm_sb", [P, 2, D])
    x2 = sb("x2", [P, 2, D])
    xn2 = sb("xn2", [P, 2, D])
    xn2T = sb("xn2T", [P, DC, UT])
    stats2 = sb("stats2", [P, 2, 6])
    mv2 = sb("mv2", [P, 2, 2])
    rs2 = sb("rs2", [P, 4, 2])
    rt = sb("rt", [P, 3, 2, E])
    top8 = sb("top8", [P, 2, 8])
    idx8 = sb("idx8", [P, 2, 8], U32)
    idxf = sb("idxf", [P, 2, K])
    mk = sb("mk", [P, 2, K, E])
    mw = sb("mw", [P, 2, K, E])
    mkb = sb("mkb", [P, 2, E], BF16)
    wk4 = sb("wk4", [P, 3, 2, K])
    rk = sb("rk", [P, 2, 2, E])
    slotf = sb("slotf", [P, 2, K])
    slot_now = sb("slot_now", [P, 2, K], U32)

    ps_max = ctx.enter_context(nc.psum_tensor("ps_max", [P, 2, 2, SEQ], F32))
    ps_exp = ctx.enter_context(nc.psum_tensor("ps_exp", [P, 2, SEQ], F32))
    ps_pv = ctx.enter_context(nc.psum_tensor("ps_pv", [P, SEQ], F32))
    ps_misc = ctx.enter_context(nc.psum_tensor("ps_misc", [P, SEQ], F32))
    misc_b = ps_misc[:, :].bitcast(BF16)

    identf, iota16, iotap, ebase, cnt, w_all, slot_all, e_all = (
        keep[k] for k in ("identf", "iota16", "iotap", "ebase", "cnt", "w_all", "slot_all", "e_all"))
    QK, XM, X2, XN2, XS = (scratch[k] for k in ("QK", "XM", "X2", "XN2", "XS"))
    STRIDE, ZERO_ROW = sizes(T)

    s_w = sem("s_weights")
    s_ws = sem("s_shared_expert_weights")
    s_eb = sem("s_router_weights")
    s_const = sem("s_constants")
    s_cst = sem("s_constants_dve")
    s_cstp = sem("s_constants_pool")
    s_gate = sem("s_gate")
    s_x = sem("s_x_loaded")
    s_bn = sem("s_bn")
    s_mv = sem("s_mean_var")
    s_rst = sem("s_rstd_steps")
    s_rstd = sem("s_rstd")
    s_xn = sem("s_xn")
    s_xnTp = sem("s_xnT_in_psum")
    s_xnT = sem("s_xnT")
    s_proj = sem("s_proj_in_psum")
    s_qf = sem("s_qkv_in_sbuf")
    s_v = sem("s_v")
    s_eq = sem("s_exp_q")
    s_eq1 = sem("s_exp_q_minus_1")
    s_sig = sem("s_sigma")
    s_split = sem("s_split_steps")
    s_parts = sem("s_parts")
    s_qk = sem("s_qk_stored")
    s_den = sem("s_mem_norm_in_psum")
    s_rn = sem("s_mem_norm_steps")
    s_amp = sem("s_mem_in_psum")
    s_am = sem("s_mem_read")
    s_xmst = sem("s_xm_stored")
    s_stage = [sem(f"s_head_staged{k}") for k in range(4)]
    s_maxp = sem("s_scores_for_max")
    s_maxd = sem("s_max_taken")
    s_mh = sem("s_max_high")
    s_mb = sem("s_max_parts")
    s_mTp = sem("s_maxT_in_psum")
    s_mT = sem("s_maxT")
    s_mrow = [sem(f"s_max_rows{k}") for k in range(4)]
    s_sc = sem("s_scores")
    s_exp = sem("s_exp")
    s_vs = sem("s_vs")
    s_pv = sem("s_pv")
    s_oT = sem("s_oT")
    s_otp = sem("s_o_in_psum")
    s_rec = sem("s_o_reciprocal")
    s_o = sem("s_o")
    s_misc = sem("s_misc_free")
    s_xml = sem("s_xm_loaded")
    s_x2 = sem("s_x2")
    s_x2st = sem("s_x2_xn2_stored")
    s_bn2 = sem("s_bn2")
    s_mv2 = sem("s_mean_var2")
    s_rst2 = sem("s_rstd2_steps")
    s_rstd2 = sem("s_rstd2")
    s_xn2 = sem("s_xn2")
    s_xn2Tp = sem("s_xn2T_in_psum")
    s_xn2T = sem("s_xn2T")
    s_lg = sem("s_logits")
    s_el = sem("s_exp_logits")
    s_rt = sem("s_router_steps")
    s_mkb = sem("s_chosen")
    s_rkp = sem("s_rank_in_psum")
    s_rt2 = sem("s_slot_steps")
    s_slot = sem("s_slots")
    s_sct = sem("s_scattered")
    s_spg = sem("s_sp_gate")
    s_plg = sem("s_pool_gate")
    s_dvg = sem("s_dve_gate")

    QK_DMAS = NH * 16
    STAGED = 9 * 16
    ROUTER = 13
    SLOTS = 6

    NB = NU
    PHASES = [(0, None, None, 1), (1, None, None, 2), (3, 0, None, 1), (4, 1, None, 2), (6, 3, 0, 1), (7, 4, 1, NU - 7),
              (None, NB - 3, NU - 6, 1), (None, NB - 2, NU - 5, 2), (None, NB, NU - 3, 1), (None, None, NU - 2, 2)]

    def phases(eng, body):
        for a0, b0, c0, repeats in PHASES:
            if repeats == 1:
                body(a0, b0, c0)
            else:
                with eng.Fori(0, repeats) as r:
                    body(*(None if i is None else r + i for i in (a0, b0, c0)))

    def heads_of(b):
        return [(k, 4 * b + k) for k in range(4)]

    MID, END = 0.0, 0.5

    def schedule(a, c, of_a, of_c):
        def at(place):
            for of, unit in ((of_a, a), (of_c, c)):
                for task in of.get(place, []) if unit is not None else []:
                    task()
        return at

    def alone(at):
        for e in range(16):
            at(e + MID)
            at(e + END)

    def runs(g, lo, hi):
        return lo <= g < hi if isinstance(g, int) else True

    NG = 4 * NB

    block = ctx.enter_context(nc.Block())

    @block.sync
    def _(sp):
        def wait(s, n):
            sp.wait_ge(s, n)
            sp.sem_inc(s_spg, 1)

        sp.dma_start(identf[:], scratch["c_identf"]).then_inc(s_const, 16)
        sp.dma_start(iota16[:], scratch["c_iota16"]).then_inc(s_const, 16)
        sp.dma_start(iotap[:], scratch["c_iotap"]).then_inc(s_const, 16)
        sp.dma_start(rest[:, 0, 0:P], scratch["c_before"]).then_inc(s_const, 16)
        sp.dma_start(gate[:, 0:1], memory_weight.partition_broadcast(P)).then_inc(s_const, 16)

        def store_xm(a):
            wait(s_am, 2 * a + 2)
            sp.dma_start(XM[bass.ds(a, 1)].rearrange("o t p d -> (o p) t d"), am[:]).then_inc(s_xmst, 16)

        def load_x(a):
            if not (isinstance(a, int) and a == 0):
                store_xm(a - 1)
            rows = x.rearrange("(u t p) d -> p u t d", p=P, t=2)
            sp.dma_start(x_sb[:], rows[:, bass.ds(a, 1), :, :]).then_inc(s_x, 16)

        def stage_head(b, k, g):
            if not (isinstance(g, int) and g < 4):
                wait(s_sc, 16 * g - 48)
            if k == 0:
                wait(s_qk, QK_DMAS * 2 * (b // 2) + 2 * QK_DMAS)
            src = QK[bass.ds(b, 1), k]
            q = src[:, 0:NQ].rearrange("o q r t -> (o r) q t")
            kk = src[:, NQ].rearrange("o r t -> (o r) t")
            for to, n in ((0, 3), (3, 2), (5, 1)):
                sp.dma_start(qs[to * DH:(to + n) * DH, k], q[0:n * DH]).then_inc(s_stage[k], 16)
            for to, part in enumerate((0, 0, 0, 1, 1, 2)):
                sp.dma_start(ks[to * DH:(to + 1) * DH, k], kk[part * DH:(part + 1) * DH]).then_inc(s_stage[k], 16)

        def max_rows(g, k):
            wait(s_mT, g + 1)
            for part in range(MROWS):
                sp.dma_start(qs[ROWS + part:ROWS + part + 1, k].rearrange("p q (s j) -> p (q s) j", j=P),
                             mT[16 * part:16 * part + 16, k % 2]).then_inc(s_mrow[k], 16)

        def loads(a, b, c):
            if a is not None:
                load_x(a)
            elif isinstance(b, int) and b == NB - 3:
                store_xm(NU - 1)
            if c is not None:
                if not (isinstance(c, int) and c == 0):
                    wait(s_x2, 2 * c)
                wait(s_xmst, 16 * c + 16)
                sp.dma_start(xm_sb[:], XM[bass.ds(c, 1)].rearrange("o t p d -> (o p) t d")).then_inc(s_xml, 16)

        def body(a, b, c):
            if b is not None:
                for k, g in heads_of(b):
                    if k == 1:
                        loads(a, b, c)
                    if runs(g, 0, NG):
                        stage_head(b, k, g)
                    if runs(g, 2, NG + 2):
                        max_rows(g - 2, (k + 2) % 4)
            else:
                loads(a, b, c)
            if c is not None:
                wait(s_x2, 2 * c + 2)
                sp.dma_start(X2[bass.ds(c, 1)].rearrange("o t p d -> (o p) t d"), x2[:]).then_inc(s_x2st, 16)
                wait(s_xn2, 2 * c + 2)
                sp.dma_start(XN2[bass.ds(c, 1)].rearrange("o t p d -> (o p) t d"), xn2[:]).then_inc(s_x2st, 16)

        sp.dma_start(w_sb[:, :, 0:D], wq).then_inc(s_w, 16)
        sp.dma_start(w_sb[:, :, D:D + P], wk).then_inc(s_w, 16)
        sp.dma_start(w_sb[:, :, D + P:], wv).then_inc(s_w, 16)
        sp.dma_start(mem_sb[:], memory).then_inc(s_w, 16)
        sp.dma_start(memn_sb[:], memory_norm).then_inc(s_w, 16)
        sp.dma_start(rw_sb[:], router_w).then_inc(s_eb, 16)
        sp.dma_start(eb_sb[:], e_bias.partition_broadcast(P)).then_inc(s_eb, 16)
        sp.dma_start(ebase[:], scratch["c_ebase"]).then_inc(s_eb, 16)
        for k in ("sgu", "sdn", "sdnr"):
            sp.dma_start(keep[k][:], shared[k]).then_inc(s_ws, 16)
        phases(sp, body)
        sp.wait_ge(s_ws, 48)
        sp.wait_ge(s_x2st, 32 * NU)

    @block.gpsimd
    def _(pool):
        def wait(s, n):
            pool.wait_ge(s, n)
            pool.sem_inc(s_plg, 1)

        def copy(out, in_):
            return pool.tensor_scalar(out, in_, 1.0, 0.0, ALU.mult, ALU.add)

        pool.memset(half[:], -0.5).then_inc(s_cstp, 1)
        pool.memset(vs[:], 0.0).then_inc(s_cstp, 1)
        pool.wait_ge(s_cstp, 2)
        pool.memset(vs[:, :, :, DH:DH + 1], 1.0).then_inc(s_cstp, 1)
        pool.wait_ge(s_cstp, 3)

        def rstd(u, mv_, rs_, ready, steps, done):
            wait(ready, 2 * u + 2)
            var = mv_[:, :, 1]
            pool.tensor_scalar(rs_[:, 0, :], var, 1.0, EPS, ALU.mult, ALU.add).then_inc(steps, 1)
            wait(steps, 5 * u + 1)
            pool.tensor_tensor(rs_[:, 1, :], rs_[:, 0, :], half[:], ALU.pow).then_inc(steps, 1)
            wait(steps, 5 * u + 2)
            pool.tensor_tensor(rs_[:, 2, :], rs_[:, 0, :], rs_[:, 1, :], ALU.mult).then_inc(steps, 1)
            wait(steps, 5 * u + 3)
            pool.tensor_tensor(rs_[:, 2, :], rs_[:, 2, :], rs_[:, 1, :], ALU.mult).then_inc(steps, 1)
            wait(steps, 5 * u + 4)
            pool.tensor_scalar(rs_[:, 2, :], rs_[:, 2, :], -0.5, 1.5, ALU.mult, ALU.add).then_inc(steps, 1)
            wait(steps, 5 * u + 5)
            pool.tensor_tensor(rs_[:, 3, :], rs_[:, 1, :], rs_[:, 2, :], ALU.mult).then_inc(done, 1)

        def split(a):
            wait(s_qf, 3 * a + 3)
            if not (isinstance(a, int) and a == 0):
                wait(s_qk, QK_DMAS * a)
            copy(parts[:, :, 0], qf[:]).then_inc(s_split, 1)
            wait(s_split, 3 * a + 1)
            pool.tensor_tensor(rest[:], qf[:], parts[:, :, 0], ALU.subtract).then_inc(s_split, 1)
            wait(s_split, 3 * a + 2)
            copy(parts[:, :, 1], rest[:]).then_inc(s_split, 1)
            wait(s_split, 3 * a + 3)
            pool.tensor_tensor(parts[:, :, 2], rest[:], parts[:, :, 1], ALU.subtract).then_inc(s_parts, 1)

        def store_split(a):
            wait(s_parts, a + 1)
            for h in range(NH):
                dst = QK[bass.ds(2 * (a // 2) + h // 4, 1), h % 4].rearrange("o q (s d) t -> (o d) (q s) t", d=DH)
                pool.dma_start(dst[:, :, bass.ds((a % 2) * UT, UT)],
                               parts[h * DH:(h + 1) * DH].rearrange("p q s t -> p (q s) t")).then_inc(s_qk, 16)

        def stage_v(b, k, g):
            if not (isinstance(g, int) and g < 4):
                wait(s_pv, 4 * g - 12)
            if k == 0:
                wait(s_v, 2 * (b // 2) + 2)
            src = v_all[:, bass.ds((b // 2) * 4, 4), bass.ds((b % 2) * 4 * DH + k * DH, DH)]
            pool.tensor_copy(vs[:, k, :, 0:DH], src).then_inc(s_vs, 1)

        def scatter(c):
            wait(s_slot, c + 1)
            wait(s_xn2, 2 * c + 2)
            for t in range(2):
                for j in range(K):
                    at = slot_now[:, t, j:j + 1]
                    pool.indirect_dma_start(XS, bass.IndirectOffsetOnAxis(ap=at, axis=0), xn2[:, t], None).then_inc(s_sct, 16)

        def body(a, b, c):
            def head_v(k):
                if b is not None and runs(4 * b + k, 0, NG):
                    stage_v(b, k, 4 * b + k)

            head_v(0)
            head_v(1)
            if a is not None:
                rstd(a, mv, rs, s_mv, s_rst, s_rstd)
            if c is not None:
                rstd(c, mv2, rs2, s_mv2, s_rst2, s_rstd2)
            head_v(2)
            if a is not None:
                split(a)
            head_v(3)
            if a is not None:
                store_split(a)
            if c is not None:
                scatter(c)

        phases(pool, body)
        pool.wait_ge(s_sct, NU * 2 * K * 16)

    @block.scalar
    def _(act):
        act.wait_ge(s_const, 16 * 5)
        act.activation(gate[:, 1:2], gate[:, 0:1], ACT.Exp, scale=-1.0).then_inc(s_gate, 1)

        def body(a, b, c):
            def xnT_out(t):
                act.wait_ge(s_xnTp, 2 * a + t + 1)
                act.activation(xnT[:, :, t * P:(t + 1) * P], ps_misc[:, :].rearrange("p (c t) -> p c t", c=DC),
                               ACT.Copy).then_inc(s_xnT, 1)

            def q_out(j):
                act.wait_ge(s_proj, 3 * a + j + 1)
                if j == 0 and not (isinstance(a, int) and a == 0):
                    act.wait_ge(s_parts, a)
                    act.wait_ge(s_sig, a)
                act.activation(qf[:, 2 * j:2 * j + 2], ps_misc[:, :].rearrange("p (q t) -> p q t", q=2),
                               ACT.Copy).then_inc(s_qf, 1)

            def kv_out():
                act.wait_ge(s_proj, 3 * a + 3)
                act.activation(v_all[:, bass.ds(2 * a, 2)], ps_misc[:, UT:].rearrange("p (t f) -> p t f", t=2),
                               ACT.Copy).then_inc(s_v, 1)
                act.activation(qf[:, NQ], ps_misc[:, 0:UT], ACT.Copy).then_inc(s_qf, 1)

            def exp_q():
                act.wait_ge(s_qf, 3 * a + 3)
                act.activation(sg[:], qf[:, 0:NQ], ACT.Exp).then_inc(s_eq, 1)

            def xn2T_out(t):
                act.wait_ge(s_xn2Tp, 2 * c + t + 1)
                act.activation(xn2T[:, :, t * P:(t + 1) * P], ps_misc[:, :].rearrange("p (c t) -> p c t", c=DC),
                               ACT.Copy).then_inc(s_xn2T, 1)

            def exp_logits():
                act.wait_ge(s_lg, c + 1)
                act.activation(rt[:, 0], ps_misc[:, 0:2 * E].rearrange("p (t e) -> p t e", t=2), ACT.Exp,
                               scale=-1.0).then_inc(s_el, 1)

            at = schedule(a, c, {5: [lambda: xnT_out(0)], 6: [lambda: xnT_out(1)], 7: [lambda: q_out(0)],
                                 8: [lambda: q_out(1)], 9: [kv_out, exp_q]},
                          {7 + END: [lambda: xn2T_out(0)], 8 + END: [lambda: xn2T_out(1)], 11 + END: [exp_logits]})

            def exps(g, s, qs_):
                for q in qs_:
                    n = 16 * g + 4 * s + q - 32
                    act.wait_ge(s_sc, n + 1)
                    if q == 0 and not (isinstance(g, int) and g < 3):
                        act.wait_ge(s_pv, 4 * g + s - 11)
                    act.activation(prob[:, s, q], ps_exp[:, q % 2], ACT.Exp, scale=SCALE).then_inc(s_exp, 1)

            def oT_out(g):
                act.wait_ge(s_pv, 4 * g - 8)
                if not (isinstance(g, int) and g == 3):
                    act.wait_ge(s_otp, g - 3)
                act.activation(oT[:], ps_pv[:], ACT.Copy).then_inc(s_oT, 1)

            def mT_out(g, k):
                act.wait_ge(s_mTp, g)
                if not (isinstance(g, int) and g < 3):
                    times = (g - 3) // 4 + 1 if isinstance(g, int) else b + (k == 3)
                    act.wait_ge(s_mrow[(k + 1) % 4], 16 * MROWS * times)
                act.activation(mT[:, (k + 1) % 2], misc_b[0:32, 0:P], ACT.Copy).then_inc(s_mT, 1)

            if b is None:
                alone(at)
                return
            for k, g in heads_of(b):
                for s in range(4):
                    if runs(g, 2, NG + 2):
                        exps(g, s, (0, 1))
                    at(4 * k + s + MID)
                    if runs(g, 2, NG + 2):
                        exps(g, s, (2, 3))
                    at(4 * k + s + END)
                    if s == 0 and runs(g, 3, NG + 3):
                        oT_out(g)
                    if s == 1 and runs(g, 1, NG + 1):
                        mT_out(g, k)

        phases(act, body)

    @block.vector
    def _(dve):
        dve.memset(ones[:], 1.0).then_inc(s_cst, 1)
        dve.memset(ks[ROWS:ROWS + 32, :, :], 1.0).then_inc(s_cst, 1)
        dve.memset(cnt[:], 0.0).then_inc(s_cst, 1)
        dve.wait_ge(s_gate, 1)
        dve.tensor_scalar(gate[:, 2:3], gate[:, 1:2], 1.0, None, ALU.add).then_inc(s_gate, 1)
        dve.wait_ge(s_gate, 2)
        dve.reciprocal(gate[:, 1:2], gate[:, 2:3]).then_inc(s_gate, 1)
        dve.wait_ge(s_gate, 3)
        dve.tensor_scalar(gate[:, 3:4], gate[:, 1:2], -1.0, 1.0, ALU.mult, ALU.add).then_inc(s_gate, 1)
        dve.wait_ge(s_gate, 4)
        dve.wait_ge(s_cst, 3)
        dve.wait_ge(s_eb, 48)
        dve.wait_ge(s_const, 16 * 5)
        dve.tensor_copy(identb[:], identf[:]).then_inc(s_cst, 1)
        dve.tensor_copy(before[:], rest[:, 0, 0:P]).then_inc(s_cst, 1)
        dve.sem_inc(s_misc, 1)

        def gated(s, n):
            dve.wait_ge(s, n)
            dve.sem_inc(s_dvg, 1)

        def body(a, b, c):
            def stats_of(u, src, st, mv_, bn, done):
                for t in range(2):
                    dve.bn_stats(st[:, t], src[:, t]).then_inc(bn, 1)
                    gated(bn, 2 * u + t + 1)
                    dve.bn_aggr(mv_[:, t], st[:, t]).then_inc(done, 1)

            def normalise(u, src, out, mv_, rs_, ready, done):
                dve.wait_ge(ready, u + 1)
                for t in range(2):
                    dve.tensor_scalar(out[:, t], src[:, t], mv_[:, t, 0:1], rs_[:, 3, t:t + 1], ALU.subtract,
                                      ALU.mult).then_inc(done, 1)

            def a_stats():
                gated(s_x, 16 * a + 16)
                stats_of(a, x_sb, stats, mv, s_bn, s_mv)

            def a_norm():
                if not (isinstance(a, int) and a == 0):
                    dve.wait_ge(s_xnTp, 2 * a)
                normalise(a, x_sb, xn, mv, rs, s_rstd, s_xn)

            def a_elu():
                dve.wait_ge(s_eq, a + 1)
                dve.tensor_scalar(sg[:], sg[:], 1.0, -1.0, ALU.min, ALU.add).then_inc(s_eq1, 1)
                dve.wait_ge(s_eq1, a + 1)
                dve.tensor_tensor(sig[:], qf[:, 0:NQ], sg[:], ALU.max).then_inc(s_sig, 1)

            def mem_norm():
                dve.wait_ge(s_den, a + 1)
                dve.reciprocal(rn[:, 0], ps_misc[:, 0:2 * NQ].rearrange("p (t q) -> p t q", t=2)).then_inc(s_rn, 1)
                dve.wait_ge(s_rn, 2 * a + 1)
                dve.tensor_scalar(rn[:, 1], rn[:, 0], gate[:, 1:2], None, ALU.mult).then_inc(s_rn, 1)

            def mem_out(t):
                dve.wait_ge(s_rn, 2 * a + 2)
                dve.wait_ge(s_amp, 2 * a + t + 1)
                if t == 0 and not (isinstance(a, int) and a == 0):
                    dve.wait_ge(s_xmst, 16 * a)
                for q in range(NQ):
                    f = slice(q * P, (q + 1) * P)
                    last = dve.scalar_tensor_tensor(am[:, t, f], ps_misc[:, f], rn[:, 1, t, q:q + 1], x_sb[:, t, f],
                                                    ALU.mult, ALU.add)
                last.then_inc(s_am, 1)

            def c_residual():
                dve.wait_ge(s_xml, 16 * c + 16)
                dve.wait_ge(s_o, 8 * (c // 2) + 8)
                if not (isinstance(c, int) and c == 0):
                    dve.wait_ge(s_x2st, 32 * c)
                for t in range(2):
                    for hf in range(2):
                        ring = (2 * (c // 2) + hf) % 8
                        o = o_all[:, bass.ds(ring, 1), bass.ds((2 * (c % 2) + t) * NQ, NQ)].rearrange("p r q h d -> p (r q) (h d)")
                        x4 = x2[:, t].rearrange("p (q v f) -> p q v f", q=NQ, v=2)[:, :, hf]
                        m4 = xm_sb[:, t].rearrange("p (q v f) -> p q v f", q=NQ, v=2)[:, :, hf]
                        last = dve.scalar_tensor_tensor(x4, o, gate[:, 3:4], m4, ALU.mult, ALU.add)
                    last.then_inc(s_x2, 1)

            def c_stats():
                gated(s_x2, 2 * c + 2)
                stats_of(c, x2, stats2, mv2, s_bn2, s_mv2)

            def c_norm():
                if not (isinstance(c, int) and c == 0):
                    dve.wait_ge(s_sct, 2 * K * 16 * c)
                    dve.wait_ge(s_xn2Tp, 2 * c)
                normalise(c, x2, xn2, mv2, rs2, s_rstd2, s_xn2)

            def link(ins, n):
                ins.then_inc(s_rt, 1)
                gated(s_rt, ROUTER * c + n)

            def router():
                dve.wait_ge(s_el, c + 1)
                link(dve.tensor_scalar(rt[:, 2], rt[:, 0], 1.0, None, ALU.add), 1)
                link(dve.reciprocal(rt[:, 1], rt[:, 2]), 2)
                link(dve.tensor_tensor(rt[:, 2], rt[:, 1], eb_sb[:, :].unsqueeze(1).to_broadcast([P, 2, E]), ALU.add), 3)
                for t in range(2):
                    link(dve.max(top8[:, t], rt[:, 2, t]), 4 + t)
                for t in range(2):
                    link(dve.max_index(idx8[:, t], top8[:, t], rt[:, 2, t]), 6 + t)

            def chosen():
                link(dve.tensor_copy(idxf[:], idx8[:, :, 0:K]), 8)
                link(dve.tensor_tensor(mk[:], iota16[:, 0:E].unsqueeze(1).unsqueeze(1).to_broadcast([P, 2, K, E]),
                                       idxf[:, :, :].unsqueeze(3).to_broadcast([P, 2, K, E]), ALU.is_equal), 9)
                dve.tensor_reduce(mkb[:], mk[:, :, :, :].rearrange("p t k e -> p t e k"), AX_X, ALU.max).then_inc(s_mkb, 1)
                link(dve.tensor_tensor(mw[:], mk[:], rt[:, 1].unsqueeze(2).to_broadcast([P, 2, K, E]), ALU.mult), 10)
                link(dve.tensor_reduce(wk4[:, 0], mw[:], AX_X, ALU.add), 11)
                link(dve.tensor_reduce(wk4[:, 1, :, 0:1], wk4[:, 0], AX_X, ALU.add), 12)
                dve.tensor_scalar(wk4[:, 1, :, 1:2], wk4[:, 1, :, 0:1], 1e-20, None, ALU.add).then_inc(s_rt, 1)
                dve.wait_ge(s_rt, ROUTER * c + 13)

            def slots():
                def link(ins, n):
                    ins.then_inc(s_rt2, 1)
                    dve.wait_ge(s_rt2, SLOTS * c + n)

                link(dve.reciprocal(wk4[:, 2, :, 0:1], wk4[:, 1, :, 1:2]), 1)
                link(dve.tensor_tensor(w_all[:, bass.ds(2 * c, 2)], wk4[:, 0], wk4[:, 2, :, 0:1].to_broadcast([P, 2, K]),
                                       ALU.mult), 2)
                dve.wait_ge(s_rkp, c + 1)
                ranks = ps_misc[:, 0:3 * E].rearrange("p (t e) -> p t e", e=E)
                link(dve.tensor_tensor(rk[:, 0], ranks[:, 0:2], cnt[:, 0].unsqueeze(1).to_broadcast([P, 2, E]), ALU.add), 3)
                dve.tensor_tensor(cnt[:, 0], ranks[:, 2], cnt[:, 0], ALU.add).then_inc(s_misc, 1)
                link(dve.tensor_tensor(rk[:, 1], rk[:, 0], ebase[:, :].unsqueeze(1).to_broadcast([P, 2, E]), ALU.add), 4)
                link(dve.tensor_tensor(mw[:], mk[:], rk[:, 1].unsqueeze(2).to_broadcast([P, 2, K, E]), ALU.mult), 5)
                link(dve.tensor_reduce(slotf[:], mw[:], AX_X, ALU.add), 6)
                if not (isinstance(c, int) and c == 0):
                    dve.wait_ge(s_sct, 2 * K * 16 * c)
                dve.tensor_copy(slot_all[:, bass.ds(2 * c, 2)], slotf[:])
                dve.tensor_copy(e_all[:, bass.ds(2 * c, 2)], idxf[:])
                dve.tensor_copy(slot_now[:], slotf[:]).then_inc(s_slot, 1)

            at = schedule(a, c, {2: [a_stats], 4: [a_norm], 10: [a_elu], 12: [mem_norm], 13: [lambda: mem_out(0)],
                                 14: [lambda: mem_out(1)]},
                          {1: [c_residual], 3: [c_stats], 5: [c_norm], 12 + END: [router], 13 + END: [chosen],
                           15 + END: [slots]})

            def split_max(g, k):
                dve.wait_ge(s_maxd, 8 * g)
                j = (k + 1) % 2
                if not (isinstance(g, int) and g < 3):
                    dve.wait_ge(s_mTp, g - 2)
                dve.tensor_scalar(mb[:, j, 0], mx[:, j], -1.0, None, ALU.mult).then_inc(s_mh, 1)
                dve.wait_ge(s_mh, g)
                dve.scalar_tensor_tensor(mb[:, j, 1], mx[:, j], -1.0, mb[:, j, 0], ALU.mult, ALU.subtract).then_inc(s_mb, 1)

            def maxima(g, k, s, p):
                dve.wait_ge(s_maxp, 8 * g + 2 * s + p + 1)
                dve.tensor_reduce(mx[:, k % 2, 4 * s + 2 * p:4 * s + 2 * p + 2], ps_max[:, p], AX_X,
                                  ALU.max).then_inc(s_maxd, 1)

            def o_out(g, k):
                v = ps_misc[:, :].rearrange("p (n e) -> p n e", e=32)
                dve.wait_ge(s_otp, g - 2)
                dve.reciprocal(rec[:, :].unsqueeze(2), v[:, :, DH:DH + 1]).then_inc(s_rec, 1)
                dve.wait_ge(s_rec, g - 2)
                kk = (k + 1) % 4
                bb = b if k == 3 else b - 1
                dve.tensor_tensor(o_all[:, bass.ds(bb % 8, 1), :, kk].rearrange("p r n d -> p (r n) d"), v[:, :, 0:DH],
                                  rec[:, :].unsqueeze(2).to_broadcast([P, 16, DH]), ALU.mult).then_inc(s_o, 1)

            if b is None:
                alone(at)
                return
            for k, g in heads_of(b):
                for s in range(4):
                    if s == 0 and runs(g, 1, NG + 1):
                        split_max(g, k)
                    if runs(g, 0, NG):
                        maxima(g, k, s, 0)
                    at(4 * k + s + MID)
                    if runs(g, 0, NG):
                        maxima(g, k, s, 1)
                    at(4 * k + s + END)
                    if s == 2 and runs(g, 3, NG + 3):
                        o_out(g, k)

        phases(dve, body)

    @block.tensor
    def _(pe):
        pe.wait_ge(s_const, 16 * 5)
        pe.wait_ge(s_w, 16 * 5)
        pe.wait_ge(s_eb, 48)
        pe.wait_ge(s_cst, 5)

        def body(a, b, c):
            def free_misc():
                for s, n in last_use:
                    pe.wait_ge(s, n)

            def set_free(s, n):
                last_use[:] = [(s, n)]

            def transposes(src, t, ready, n, done):
                pe.wait_ge(ready, n)
                for i in range(DC):
                    mm = pe.transpose(ps_misc[:, i * P:(i + 1) * P], src[:, t, i * P:(i + 1) * P], identf[:])
                mm.then_inc(done, 1)

            def a_T(t):
                free_misc()
                transposes(xn, t, s_xn, 2 * a + t + 1, s_xnTp)
                set_free(s_xnT, 2 * a + t + 1)

            def a_q(j):
                free_misc()
                pe.wait_ge(s_xnT, 2 * a + 2)
                for q in range(2):
                    o = (2 * j + q) * P
                    for i in range(DC):
                        mm = pe.matmul(ps_misc[:, q * UT:(q + 1) * UT], w_sb[:, i, o:o + P], xnT[:, i], start=(i == 0),
                                       stop=(i == DC - 1))
                mm.then_inc(s_proj, 1)
                set_free(s_qf, 3 * a + j + 1)

            def a_kv():
                free_misc()
                for i in range(DC):
                    pe.matmul(ps_misc[:, 0:UT], w_sb[:, i, D:D + P], xnT[:, i], start=(i == 0), stop=(i == DC - 1))
                for t in range(2):
                    for i in range(DC):
                        mm = pe.matmul(ps_misc[:, UT + t * P:UT + (t + 1) * P], xnT[:, i, t * P:(t + 1) * P],
                                       w_sb[:, i, D + P:D + 2 * P], start=(i == 0), stop=(i == DC - 1))
                mm.then_inc(s_proj, 1)
                set_free(s_qf, 3 * a + 3)

            def a_den():
                free_misc()
                pe.wait_ge(s_sig, a + 1)
                for t in range(2):
                    for q in range(NQ):
                        mm = pe.matmul(ps_misc[:, t * NQ + q:t * NQ + q + 1], sig[:, q, t * P:(t + 1) * P], memn_sb[:],
                                       start=True, stop=True)
                mm.then_inc(s_den, 1)
                set_free(s_rn, 2 * a + 1)

            def a_mem(t):
                free_misc()
                for q in range(NQ):
                    mm = pe.matmul(ps_misc[:, q * P:(q + 1) * P], sig[:, q, t * P:(t + 1) * P], mem_sb[:], start=True,
                                   stop=True)
                mm.then_inc(s_amp, 1)
                set_free(s_am, 2 * a + t + 1)

            def c_T(t):
                free_misc()
                transposes(xn2, t, s_xn2, 2 * c + t + 1, s_xn2Tp)
                set_free(s_xn2T, 2 * c + t + 1)

            def c_logits():
                free_misc()
                pe.wait_ge(s_xn2T, 2 * c + 2)
                for t in range(2):
                    for i in range(DC):
                        mm = pe.matmul(ps_misc[:, t * E:(t + 1) * E], xn2T[:, i, t * P:(t + 1) * P], rw_sb[:, i],
                                       start=(i == 0), stop=(i == DC - 1))
                mm.then_inc(s_lg, 1)
                set_free(s_el, c + 1)

            def c_rank():
                free_misc()
                pe.wait_ge(s_mkb, c + 1)
                for to, terms in enumerate((((before, 0),), ((before, 1), (ones, 0)), ((ones, 0), (ones, 1)))):
                    for n, (m, t) in enumerate(terms):
                        mm = pe.matmul(ps_misc[:, to * E:(to + 1) * E], m[:], mkb[:, t], start=(n == 0),
                                       stop=(n == len(terms) - 1))
                mm.then_inc(s_rkp, 1)
                set_free(s_misc, c + 2)

            last_use = [(s_am, 2 * a)] if a is not None and (b is None or isinstance(b, int) and b == 0) else []
            if b is not None and not (isinstance(b, int) and b == 0):
                last_use.append((s_o, 4 * b - 3))
            if c is not None:
                last_use.append((s_misc, c + 1))
            if isinstance(a, int) and a == 0:
                last_use = []
            at = schedule(a, c, {5: [lambda: a_T(0)], 6: [lambda: a_T(1)], 7: [lambda: a_q(0)], 8: [lambda: a_q(1)],
                                 9: [a_kv], 12: [a_den], 13: [lambda: a_mem(0)], 14: [lambda: a_mem(1)]},
                          {7 + END: [lambda: c_T(0)], 8 + END: [lambda: c_T(1)], 11 + END: [c_logits], 15: [c_rank]})

            def scores_for_max(g, k, s, p):
                if not (isinstance(g, int) and 8 * g + 2 * s + p < 2):
                    pe.wait_ge(s_maxd, 8 * g + 2 * s + p - 1)
                if s == 0 and p == 0:
                    pe.wait_ge(s_stage[k], STAGED * (b + 1))
                for i in range(2):
                    st = 2 * p + i
                    mm = pe.matmul(ps_max[:, p, i], qs[0:ROWS, k, s, st * P:(st + 1) * P], ks[0:ROWS, k], start=True,
                                   stop=True)
                mm.then_inc(s_maxp, 1)

            def scores(g, k, s, qs_):
                kk = (k + 2) % 4
                for q in qs_:
                    n = 16 * g + 4 * s + q - 32
                    if not (isinstance(g, int) and n < 2):
                        pe.wait_ge(s_exp, n - 1)
                    if s == 0 and q == 0:
                        times = (g - 2) // 4 + 1 if isinstance(g, int) else (b + 1 if k >= 2 else b)
                        pe.wait_ge(s_mrow[kk], 16 * MROWS * times)
                    pe.matmul(ps_exp[:, q % 2], ks[0:ROWS + MROWS, kk, s * P:(s + 1) * P], qs[0:ROWS + MROWS, kk, q],
                              start=True, stop=True).then_inc(s_sc, 1)

            def pv(g, kk, t, n):
                pe.wait_ge(s_exp, 4 * n + 4)
                if t == 0:
                    if not (isinstance(g, int) and g == 2):
                        pe.wait_ge(s_oT, g - 2)
                    pe.wait_ge(s_vs, g - 1)
                for q in range(NQ):
                    mm = pe.matmul(ps_pv[32 * q:32 * q + 32, :], vs[:, kk, t], prob[:, t, q], start=(t == 0), stop=(t == 3))
                mm.then_inc(s_pv, 1)

            def max_T(g, k):
                free_misc()
                pe.wait_ge(s_mb, g)
                pe.transpose(misc_b[0:32, 0:P], mb[:, (k + 1) % 2].rearrange("p a n -> p (a n)"), identb[:]).then_inc(s_mTp, 1)
                set_free(s_mT, g)

            def o_T(g):
                free_misc()
                pe.wait_ge(s_oT, g - 2)
                for i in range(4):
                    mm = pe.transpose(ps_misc[:, i * P:(i + 1) * P], oT[:, i * P:(i + 1) * P], identf[:])
                mm.then_inc(s_otp, 1)
                set_free(s_o, g - 2)

            if b is None:
                alone(at)
                return
            for k, g in heads_of(b):
                for s in range(4):
                    for half_ in range(2):
                        if runs(g, 2, NG + 2):
                            scores(g, k, s, (2 * half_,))
                        if runs(g, 0, NG):
                            scores_for_max(g, k, s, half_)
                        if runs(g, 2, NG + 2):
                            scores(g, k, s, (2 * half_ + 1,))
                        if half_ == 0:
                            at(4 * k + s + MID)
                            if s == 0:
                                if runs(g, 3, NG + 3):
                                    pv(g - 1, (k + 1) % 4, 3, 4 * g - 9)
                            elif runs(g, 2, NG + 2):
                                pv(g, (k + 2) % 4, s - 1, 4 * g - 8 + s - 1)
                    at(4 * k + s + END)
                    if s == 1 and runs(g, 1, NG + 1):
                        max_T(g, k)
                    if s == 2 and runs(g, 3, NG + 3):
                        o_T(g)

        phases(pe, body)

    ctx.close()



def feed_forward(nc, T, io, keep, scratch, out):
    wts_w, dnr_w = io
    NT = T // P
    NR = NT * K + E
    NS0 = 4
    R0, R1 = NS0, NS0 + NR
    NTILES = NT + NR
    LATE = 2
    NREST = NT - (NTILES - R1 - LATE)
    RING = 4
    W = DC * 2 * I + D
    SUMS = 2 * K
    STRIDE, ZERO_ROW = sizes(T)
    ctx = ExitStack()

    def sb(name, shape, dt=F32):
        return ctx.enter_context(nc.sbuf_tensor(name, shape, dt))

    def sem(name):
        return ctx.enter_context(nc.semaphore(name))

    identf, iota16, iotap, ebase, cnt, w_all, slot_all, e_all = (
        keep[k] for k in ("identf", "iota16", "iotap", "ebase", "cnt", "w_all", "slot_all", "e_all"))
    X2, XN2, XS, Y, XO = (scratch[k] for k in ("X2", "XN2", "XS", "Y", "XO"))

    wts_sb = sb("wts_sb", [P, E, W])
    dnr_sb = sb("dnr_sb", [P, E // 2, D])
    sgu_sb, sdn_sb, sdnr_sb = (keep[k] for k in ("sgu", "sdn", "sdnr"))
    xt = sb("xt", [P, 2, D])
    xT = sb("xT", [P, 2, DC, P])
    gs = sb("gs", [P, 2, I])
    hid = sb("hid", [P, 2, 2, P])
    hT = sb("hT", [P, 2, 2, P])
    yt = sb("yt", [P, 2, D])
    x2t = sb("x2t", [P, 2, D])
    wts_flat = wts_sb[:, :, :].rearrange("p e n -> p (e n)")
    rows = wts_flat[:, 0:RING * K * D].rearrange("p (a k d) -> p a k d", a=RING, k=K)
    acc = wts_flat[:, RING * K * D:(RING * K + NT) * D].rearrange("p (t d) -> p t d", t=NT)
    at_now = sb("at_now", [P, RING, K], U32)
    par = sb("par", [P, 2, NR])
    tab = sb("tab", [1, 2, NR], U32)
    small = sb("small", [P, 8, E])
    smi = sb("smi", [P, E], I32)
    zero = sb("zero", [P, D])
    shift = sb("shift", [P, NT * K])
    at_all = sb("at_all", [P, NT * K], U32)
    padf = sb("padf", [P, E])
    padi = sb("padi", [P, E], U32)
    ji = sb("ji", [P, NR], I32)
    room = sb("room", [P, NR * (E + 9)])
    big = room[:, 0:NR * E].rearrange("p (j e) -> p j e", e=E)
    jrow = room[:, NR * E:NR * (E + 3)].rearrange("p (k j) -> p k j", k=3)
    jt = room[:, NR * (E + 3):NR * (E + 9)].rearrange("p (k j) -> p k j", k=6)

    ps_x = ctx.enter_context(nc.psum_tensor("ps_x", [P, 2, DC, P], F32))
    ps_gu = ctx.enter_context(nc.psum_tensor("ps_gu", [P, 2, D], F32))
    ps_h = ctx.enter_context(nc.psum_tensor("ps_h", [P, 2, DC, P], F32))
    ps_y = ctx.enter_context(nc.psum_tensor("ps_y", [P, 2, D], F32))

    s_wr = [sem(f"f_expert_weights{i}") for i in range(2)]
    s_exp = sem("f_experts_ready")
    s_tc = sem("f_table_constants")
    s_tb = sem("f_table_steps")
    s_tab = sem("f_tables")
    s_zero = sem("f_zero")
    s_pad = sem("f_pads")
    s_x = [sem(f"f_x_loaded{p}") for p in range(2)]
    s_xp = sem("f_xT_in_psum")
    s_xT = sem("f_xT")
    s_gu = sem("f_gate_up")
    s_si = sem("f_silu")
    s_h = sem("f_hidden")
    s_hp = sem("f_hT_in_psum")
    s_hT = sem("f_hT")
    s_yp = sem("f_y_in_psum")
    s_y = sem("f_y")
    s_yst = [sem(f"f_y_stored{p}") for p in range(2)]
    s_x2 = [sem(f"f_x2_loaded{p}") for p in range(2)]
    s_at = sem("f_rows_wanted")
    s_rows = [sem(f"f_rows{i}") for i in range(RING)]
    s_acc = sem("f_first_sums_loaded")
    s_sum = sem("f_sum_steps")
    s_out = sem("f_out_stored")
    s_spg = sem("f_sp_gate")
    s_plg = sem("f_pool_gate")
    s_acg = sem("f_act_gate")

    SHARED, ROUTED = 0, 1

    class Tile:

        def __init__(self, h, p):
            self.h, self.p, self.n = h, p, h * 2 + p

        def of(self, kind, late, mod):
            self.kind, self.late = kind, late
            self.th = self.h - NR // 2 if late else self.h
            self.t = self.th * 2 + self.p
            self.j = None if kind == SHARED else self.n - R0
            self.m, self.m_ring = self.n - R1, (mod - R1) % RING
            return self

    H0, H1, H2 = R0 // 2, R1 // 2, NTILES // 2
    RUNS = [(h, SHARED, False, 1, 1) for h in range(H0)] + \
        [(H0, ROUTED, False, 1, 1), (H0 + 1, ROUTED, False, 1, H1 - H0 - 2), (H1 - 1, ROUTED, False, 1, 1),
         (H1, SHARED, True, 1, 1), (H1 + 1, SHARED, True, 1, 1), (H1 + 2, SHARED, True, 1, 1),
         (H1 + 3, SHARED, True, 2, (H2 - H1 - 4) // 2), (H2 - 1, SHARED, True, 1, 1)]

    def kind_of(h):
        return (SHARED, False) if h < H0 else (ROUTED, False) if h < H1 else (SHARED, True)

    def slots(eng, body):
        for h0, kind, late, pairs, repeats in RUNS:
            def pair(h, mod, kinds):
                made = [Tile(h + i // 2, i % 2).of(*kinds(i // 2), mod + i) for i in range(-1, 5)]
                for p in range(2):
                    body(*made[p:p + 4])

            if repeats == 1:
                pair(h0, 2 * h0, lambda i, h0=h0: kind_of(h0 + i))
            else:
                with eng.Fori(0, repeats) as r:
                    for i in range(pairs):
                        pair(r * pairs + (h0 + i), 2 * (h0 + i), lambda i, kind=kind, late=late: (kind, late))

    def exists(tile):
        return not isinstance(tile.n, int) or 0 <= tile.n < NTILES

    def rows_of(dram, t):
        return dram[bass.ds(t, 1)].rearrange("o p d -> (o p) d")

    def after(eng_wait, s, n):
        if not (isinstance(n, int) and n <= 0):
            eng_wait(s, n)

    block = ctx.enter_context(nc.Block())

    @block.sync
    def _(sp):
        def wait(s, n):
            sp.wait_ge(s, n)
            sp.sem_inc(s_spg, 1)

        def load_x(tile):
            after(wait, s_xp, tile.n - 1)
            if tile.kind == SHARED:
                sp.dma_start(xt[:, tile.p], rows_of(XN2, tile.t)).then_inc(s_x[tile.p], 16)
            else:
                row = sp.value_load(tab[0:1, 0, bass.ds(tile.j, 1)], min_val=0, max_val=ZERO_ROW)
                sp.dma_start(xt[:, tile.p], XS[bass.ds(row, P)]).then_inc(s_x[tile.p], 16)

        def load_x2(tile):
            after(wait, s_y, tile.n - 1)
            sp.dma_start(x2t[:, tile.p], rows_of(X2, tile.t)).then_inc(s_x2[tile.p], 16)

        def store_out(n):
            wait(s_sum, SUMS * n + SUMS)
            sp.dma_start(rows_of(out, n), acc[:, bass.ds(n, 1)].rearrange("p o d -> p (o d)")).then_inc(s_out, 16)

        first = [Tile(0, p).of(SHARED, False, p) for p in range(2)]
        load_x(first[0])
        sp.dma_start(jrow, scratch["c_jrow"]).then_inc(s_tc, 16)
        load_x(first[1])
        def body(before, tile, following, later):
            if exists(later):
                if isinstance(later.n, int) and later.n == R0:
                    wait(s_tab, 1)
                    wait(s_pad, 16 * (E + 1))
                load_x(later)
            if isinstance(tile.n, int) and tile.n == R1 + 1:
                wait(s_yp, R1)
                for p in range(2):
                    wait(s_yst[p], 16 * (R0 // 2))
                sp.dma_start(acc[:, 0:NS0], XO.rearrange("t p d -> p t d")).then_inc(s_acc, 16)
            if tile.late and not (isinstance(tile.m, int) and tile.m <= LATE):
                store_out(tile.m - LATE - 1)
            if tile.kind == SHARED:
                load_x2(tile)

        slots(sp, body)
        for n in range(NT - NREST - 1, NT):
            store_out(n)
        sp.wait_ge(s_out, 16 * NT)

    @block.gpsimd
    def _(pool):
        def wait(s, n):
            pool.wait_ge(s, n)
            pool.sem_inc(s_plg, 1)

        def load_weights(e, i):
            pool.dma_start(wts_sb[:, bass.ds(e, 1)], wts_w[:, bass.ds(e, 1)]).then_inc(s_wr[i], 16)
            if i == 0:
                pool.dma_start(dnr_sb[:, bass.ds(e // 2, 1)], dnr_w[:, bass.ds(e // 2, 1)]).then_inc(s_wr[i], 16)

        def weights_ready(h, i):
            wait(s_wr[i], (32 if i == 0 else 16) * (h + 1))
            pool.sem_inc(s_exp, 1)

        for i in range(2):
            load_weights(i, i)
        pool.memset(zero[:], 0.0).then_inc(s_zero, 1)
        wait(s_zero, 1)
        pool.dma_start(XS[ZERO_ROW:ZERO_ROW + P], zero[:]).then_inc(s_pad, 16)
        wait(s_tb, 2)
        for e in range(E):
            pool.indirect_dma_start(XS, bass.IndirectOffsetOnAxis(ap=padi[:, e:e + 1], axis=0), zero[:],
                                    None).then_inc(s_pad, 16)

        with pool.Fori(0, E // 2 - 1) as r:
            for i in range(2):
                weights_ready(r, i)
                load_weights(2 * r + (2 + i), i)
        for i in range(2):
            weights_ready(E // 2 - 1, i)

        for p in range(2):
            wait(s_yst[p], 16 * (R1 // 2))
        with pool.Fori(0, NT // RING) as r:
            for i in range(RING):
                wait(s_at, RING * r + i + 1)
                for j in range(K):
                    pool.indirect_dma_start(rows[:, i, j], None, Y.rearrange("j p d -> (j p) d"),
                                            bass.IndirectOffsetOnAxis(ap=at_now[:, i, j:j + 1], axis=0)).then_inc(s_rows[i], 16)

    @block.scalar
    def _(act):
        def x_out(tile):
            act.wait_ge(s_xp, tile.n + 1)
            after(act.wait_ge, s_gu, tile.n - 1)
            act.activation(xT[:, tile.p], ps_x[:, tile.p], ACT.Copy).then_inc(s_xT, 1)

        def y_out(tile):
            act.wait_ge(s_yp, tile.n + 1)
            after(act.wait_ge, s_yst[tile.p], 16 * tile.h)
            act.activation(yt[:, tile.p], ps_y[:, tile.p], ACT.Copy).then_inc(s_y, 1)

        def store(tile):
            act.wait_ge(s_y, tile.n + 1)
            act.sem_inc(s_acg, 1)
            if tile.kind == SHARED:
                act.dma_start(rows_of(XO, tile.t), yt[:, tile.p]).then_inc(s_yst[tile.p], 16)
            else:
                act.dma_start(rows_of(Y, tile.j), yt[:, tile.p]).then_inc(s_yst[tile.p], 16)

        def body(before, tile, following, later):
            act.wait_ge(s_gu, tile.n + 1)
            act.activation(gs[:, tile.p], ps_gu[:, tile.p, 0:I], ACT.Silu).then_inc(s_si, 1)
            if exists(following):
                x_out(following)
            if exists(before) and not before.late:
                if before.kind == ROUTED:
                    y_out(before)
                store(before)

        x_out(Tile(0, 0))
        slots(act, body)

    @block.vector
    def _(dve):
        steps = [0]

        def step(ins):
            steps[0] += 1
            ins.then_inc(s_tb, 1)
            dve.wait_ge(s_tb, steps[0])

        def pads():
            step(dve.tensor_scalar(padf[:], cnt[:, 0], iotap[:, 0:1], None, ALU.add))
            step(dve.tensor_tensor(padi[:], padf[:], ebase[:], ALU.add))

        bc = [P, NR, E]
        upto = small[:, 4]

        def tiles_of_experts():
            step(dve.tensor_scalar(smi[:], cnt[:, 0], float(P - 1), None, ALU.add))
            step(dve.tensor_scalar(smi[:], smi[:], 7, None, ALU.logical_shift_right))
            step(dve.tensor_copy(small[:, 0], smi[:]))
            for i, s in enumerate((1, 2, 4, 8)):
                step(dve.tensor_copy(small[:, i + 1, 0:s], small[:, i, 0:s]))
                step(dve.tensor_tensor(small[:, i + 1, s:E], small[:, i, s:E], small[:, i, 0:E - s], ALU.add))
            step(dve.tensor_tensor(small[:, 5], upto, small[:, 0], ALU.subtract))
            step(dve.scalar_tensor_tensor(small[:, 6], small[:, 5], -float(P), ebase[:], ALU.mult, ALU.add))
            dve.wait_ge(s_tc, 16)
            step(dve.tensor_tensor(big, jrow[:, 0].unsqueeze(2).to_broadcast(bc), upto.unsqueeze(1).to_broadcast(bc), ALU.is_ge))

        def experts_of_tiles():
            step(dve.tensor_reduce(jt[:, 0], big, AX_X, ALU.add))
            step(dve.tensor_scalar(jt[:, 1], jt[:, 0], float(E - 1), None, ALU.min))
            step(dve.tensor_scalar(jt[:, 2], jt[:, 0], float(E), None, ALU.is_lt))
            step(dve.tensor_tensor(big, jt[:, 1].unsqueeze(2).to_broadcast(bc), iota16[:, :].unsqueeze(1).to_broadcast(bc),
                                   ALU.is_equal))

        def starts_of_tiles():
            step(dve.tensor_tensor(big, big, small[:, 6].unsqueeze(1).to_broadcast(bc), ALU.mult))
            step(dve.tensor_reduce(jt[:, 3], big, AX_X, ALU.add))

        def tables():
            step(dve.tensor_tensor(jt[:, 3], jt[:, 3], jrow[:, 1], ALU.add))
            step(dve.tensor_tensor(jt[:, 4], jt[:, 3], jrow[:, 2], ALU.subtract))
            step(dve.tensor_tensor(jt[:, 5], jt[:, 4], jt[:, 2], ALU.mult))
            step(dve.tensor_tensor(tab[0:1, 0], jt[0:1, 5], jrow[0:1, 2], ALU.add))
            step(dve.tensor_copy(tab[0:1, 1], jt[0:1, 1]))
            step(dve.tensor_copy(ji[:], jt[:, 1]))
            step(dve.tensor_scalar(ji[:], ji[:], 1, None, ALU.bitwise_and))
            step(dve.tensor_copy(par[:, 1], ji[:]))
            dve.tensor_scalar(par[:, 0], par[:, 1], -1.0, 1.0, ALU.mult, ALU.add).then_inc(s_tab, 1)
            dve.wait_ge(s_tab, 1)

        def result_rows():
            bc = [P, NT * K, E]
            of_tokens = room[:, 0:NT * K * E].rearrange("p (n e) -> p n e", e=E)
            slots_ = slot_all[:, :, :].rearrange("p t k -> p (t k)")
            step(dve.tensor_tensor(of_tokens, e_all[:, :, :].rearrange("p t k -> p (t k)").unsqueeze(2).to_broadcast(bc),
                                   iota16[:, :].unsqueeze(1).to_broadcast(bc), ALU.is_equal))
            step(dve.tensor_tensor(of_tokens, of_tokens, small[:, 6].unsqueeze(1).to_broadcast(bc), ALU.mult))
            step(dve.tensor_reduce(shift[:], of_tokens, AX_X, ALU.add))
            step(dve.tensor_tensor(at_all[:], slots_, shift[:], ALU.subtract))

        def hT_out(tile):
            dve.wait_ge(s_hp, tile.n + 1)
            after(dve.wait_ge, s_yp, tile.n - 1)
            if tile.kind == ROUTED:
                dve.tensor_copy(hT[:, tile.p], ps_h[:, tile.p, 0:2]).then_inc(s_hT, 1)
            else:
                dve.tensor_copy(hT[:, tile.p, 0], ps_h[:, tile.p, 0])
                dve.tensor_copy(hT[0:IR, tile.p, 1], ps_h[0:IR, tile.p, 1]).then_inc(s_hT, 1)

        def hidden(tile):
            dve.wait_ge(s_si, tile.n + 1)
            after(dve.wait_ge, s_hp, tile.n - 1)
            up = ps_gu[:, tile.p, I:2 * I]
            h = hid[:, tile.p].rearrange("p a b -> p (a b)")
            if tile.kind == ROUTED:
                dve.tensor_tensor(h[:, 0:P], up[:, 0:P], gs[:, tile.p, 0:P], ALU.mult)
                for k in range(2):
                    last = dve.scalar_tensor_tensor(h[:, P + k * IR:P + (k + 1) * IR], up[:, P:I],
                                                    par[:, k, bass.ds(tile.j, 1)], gs[:, tile.p, P:I], ALU.mult, ALU.mult)
            else:
                last = dve.tensor_tensor(h[:, 0:I], up, gs[:, tile.p], ALU.mult)
            last.then_inc(s_h, 1)

        def y_sum(tile):
            dve.wait_ge(s_yp, tile.n + 1)
            dve.wait_ge(s_x2[tile.p], 16 * tile.th + 16)
            if tile.late:
                to = acc[:, bass.ds(tile.t, 1)].rearrange("p o d -> p (o d)")
            else:
                after(dve.wait_ge, s_yst[tile.p], 16 * tile.h)
                to = yt[:, tile.p]
            dve.tensor_tensor(to, ps_y[:, tile.p], x2t[:, tile.p], ALU.add).then_inc(s_y, 1)

        def want(n, ring):
            dve.tensor_copy(at_now[:, ring], at_all[:, bass.ds(K * n, K)]).then_inc(s_at, 1)

        def combine(n, ring, more):
            if isinstance(n, int) and n < NS0:
                dve.wait_ge(s_acc, 16)
            else:
                dve.wait_ge(s_y, n + (R1 - NS0 + 1))
            dve.wait_ge(s_rows[ring], 16 * K * (n // RING) + 16 * K)
            w = w_all[:, :, :].rearrange("p t k -> p (t k)")
            for j in range(K):
                for c in range(2):
                    f = slice(c * D // 2, (c + 1) * D // 2)
                    if j:
                        dve.wait_ge(s_sum, SUMS * n + 2 * j + c - 1)
                    sum_ = acc[:, bass.ds(n, 1), f].rearrange("p o d -> p (o d)")
                    dve.scalar_tensor_tensor(sum_, rows[:, ring, j, f], w[:, bass.ds(K * n + j, 1)], sum_, ALU.mult,
                                             ALU.add).then_inc(s_sum, 1)
            if more:
                dve.wait_ge(s_sum, SUMS * n + SUMS)
                want(n + RING, ring)

        def body(before, tile, following, later):
            if exists(before):
                hT_out(before)
            if tile.late and not (isinstance(tile.m, int) and tile.m < LATE):
                combine(tile.m - LATE, (tile.m_ring - LATE) % RING, True)
            hidden(tile)
            if exists(before) and before.kind == SHARED:
                y_sum(before)
            if isinstance(tile.n, int) and tile.n < 2:
                if tile.n == 0:
                    tiles_of_experts()
                    experts_of_tiles()
                else:
                    starts_of_tiles()
                    tables()
            if isinstance(tile.n, int) and tile.n == R0:
                result_rows()
            if isinstance(tile.n, int) and tile.n == R1:
                for i in range(RING):
                    want(i, i)

        pads()
        slots(dve, body)
        end = Tile(H2 - 1, 1).of(SHARED, True, NTILES - 1)
        hT_out(end)
        y_sum(end)
        for n in range(NT - NREST, NT):
            combine(n, n % RING, n + RING < NT)

    @block.tensor
    def _(pe):
        def transpose_x(tile):
            pe.wait_ge(s_x[tile.p], 16 * tile.h + 16)
            after(pe.wait_ge, s_xT, tile.n - 1)
            for i in range(DC):
                mm = pe.transpose(ps_x[:, tile.p, i], xt[:, tile.p, i * P:(i + 1) * P], identf[:])
            mm.then_inc(s_xp, 1)

        def expert(tile):
            if not exists(tile) or tile.kind == SHARED:
                return None
            return pe.value_load(tab[0:1, 1, bass.ds(tile.j, 1)], min_val=0, max_val=E - 1)

        def of_expert(e, part):
            return wts_sb[:, bass.ds(e, 1), part].rearrange("p o n -> p (o n)")

        def gate_up(tile, e):
            if tile.kind == ROUTED:
                pe.wait_ge(s_exp, e + 1)
            pe.wait_ge(s_xT, tile.n + 1)
            after(pe.wait_ge, s_h, tile.n - 1)
            for i in range(DC):
                w = sgu_sb[:, i] if tile.kind == SHARED else of_expert(e, slice(2 * I * i, 2 * I * (i + 1)))
                mm = pe.matmul(ps_gu[:, tile.p, 0:2 * I], xT[:, tile.p, i], w, start=(i == 0), stop=(i == DC - 1))
            mm.then_inc(s_gu, 1)

        def transpose_h(tile):
            pe.wait_ge(s_h, tile.n + 1)
            after(pe.wait_ge, s_hT, tile.n - 1)
            pe.transpose(ps_h[:, tile.p, 0], hid[:, tile.p, 0], identf[:])
            if tile.kind == ROUTED:
                mm = pe.transpose(ps_h[:, tile.p, 1], hid[:, tile.p, 1], identf[:])
            else:
                mm = pe.transpose(ps_h[0:IR, tile.p, 1], hid[:, tile.p, 1, 0:IR], identf[:])
            mm.then_inc(s_hp, 1)

        def down(tile, e):
            pe.wait_ge(s_hT, tile.n + 1)
            after(pe.wait_ge, s_y, tile.n - 1)
            if tile.kind == ROUTED:
                pe.matmul(ps_y[:, tile.p], hT[:, tile.p, 0], of_expert(e, slice(W - D, W)),
                          start=True, stop=False)
                mm = pe.matmul(ps_y[:, tile.p], hT[:, tile.p, 1], dnr_sb[:, bass.ds(e // 2, 1)].rearrange("p o n -> p (o n)"),
                               start=False, stop=True)
            else:
                pe.matmul(ps_y[:, tile.p], hT[:, tile.p, 0], sdn_sb[:], start=True, stop=False)
                mm = pe.matmul(ps_y[:, tile.p], hT[0:IR, tile.p, 1], sdnr_sb[:], start=False, stop=True)
            mm.then_inc(s_yp, 1)

        def body(before, tile, following, later):
            if isinstance(tile.n, int) and tile.n == R0:
                pe.wait_ge(s_tab, 1)
            e_before, e = expert(before), expert(tile)
            if exists(before):
                transpose_h(before)
            gate_up(tile, e)
            if exists(following):
                transpose_x(following)
            if exists(before):
                down(before, e_before)

        transpose_x(Tile(0, 0))
        slots(pe, body)
        end = Tile(H2 - 1, 1).of(SHARED, True, NTILES - 1)
        transpose_h(end)
        down(end, None)

    ctx.close()


INPUTS = ["wq", "wk", "wv", "memory", "memory_norm", "memory_weight", "router_w", "e_bias"]


def build(nc, T, a, out):
    stride, zero_row = sizes(T)
    NU, NT = T // UT, T // P

    def dram(name, shape, dt=F32):
        return nc.dram_tensor(name, shape, dt).ap()

    scratch = {
        "QK": dram("qk_parts", [NU, NH // 2, NQ + 1, PARTS * DH, SEQ], BF16),
        "XM": dram("x_plus_memory", [NU, 2, P, D]),
        "X2": dram("x2_rows", [NU, 2, P, D]),
        "XN2": dram("xn2_rows", [NU, 2, P, D]),
        "XS": dram("rows_by_expert", [zero_row + P, D]),
        "Y": dram("results_by_expert", [NT * K + E, P, D]),
        "XO": dram("x2_plus_shared", [4, P, D]),
    } | {k: v for k, v in a.items() if k.startswith("c_")}
    with ExitStack() as ctx:
        keep = kept(nc, ctx, T)
        attention(nc, T, [a["x"]] + [a[k] for k in INPUTS], {k: a[k] for k in ("sgu", "sdn", "sdnr")},
                  keep, scratch)
        for k in ("X2", "XN2"):
            scratch[k] = scratch[k].rearrange("u t p d -> (u t) p d")
        feed_forward(nc, T, [a["wts"], a["dnr"]], keep, scratch,
                     out.rearrange("b (s p) d -> (b s) p d", p=P))


def constants(T):
    i = np.arange(P)
    stride, zero_row = sizes(T)
    nr = T // P * K + E
    j = np.arange(nr)
    jrow = np.stack([j, j * P, np.full(nr, zero_row)])
    return {
        "c_identf": np.eye(P, dtype=np.float32),
        "c_before": (i[:, None] < i[None, :]).astype(np.float32),
        "c_iota16": np.tile(np.arange(E, dtype=np.float32), (P, 1)),
        "c_iotap": i[:, None].astype(np.float32),
        "c_ebase": np.tile(np.arange(E, dtype=np.float32) * stride, (P, 1)),
        "c_jrow": np.tile(jrow.astype(np.float32), (P, 1, 1)),
    }


def kept(nc, ctx, T):
    def sb(name, shape, dt=F32):
        return ctx.enter_context(nc.sbuf_tensor(name, shape, dt))
    return {"identf": sb("identf", [P, P]), "iota16": sb("iota16", [P, E]), "iotap": sb("iotap", [P, 1]),
            "ebase": sb("ebase", [P, E]), "cnt": sb("cnt", [P, 1, E]), "w_all": sb("w_all", [P, T // P, K]),
            "slot_all": sb("slot_all", [P, T // P, K]), "e_all": sb("e_all", [P, T // P, K]),
            "sgu": sb("sgu_sb", [P, DC, 2 * I]), "sdn": sb("sdn_sb", [P, D]), "sdnr": sb("sdnr_sb", [IR, D])}


def kernel(L0_attn_x, L0_attn_Wq, L0_attn_Wk, L0_attn_Wv, L0_attn_memory, L0_attn_memory_norm, L0_attn_memory_weight,
           L0_ffn_router_w, L0_ffn_e_bias, L0_ffn_gate_up_proj, L0_ffn_down_proj, L0_ffn_shared_gate_w,
           L0_ffn_shared_up_w, L0_ffn_shared_down_w):
    import concourse.bacc as bacc
    from concourse.bass_utils import run_bass_kernel_spmd

    def chunks(w, rows=P):
        w = np.asarray(w)
        return np.ascontiguousarray(w.reshape(w.shape[0] // rows, rows, -1).transpose(1, 0, 2))

    x = np.asarray(L0_attn_x)
    B, S, _ = x.shape
    T = B * S
    gu = np.asarray(L0_ffn_gate_up_proj)
    dn = np.asarray(L0_ffn_down_proj).transpose(0, 2, 1)
    sdn = np.asarray(L0_ffn_shared_down_w).T
    arrays = {
        "x": np.ascontiguousarray(x.reshape(T, D)),
        "wq": chunks(np.asarray(L0_attn_Wq).T),
        "wk": chunks(np.asarray(L0_attn_Wk).T),
        "wv": chunks(np.asarray(L0_attn_Wv).T),
        "memory": np.ascontiguousarray(L0_attn_memory),
        "memory_norm": np.ascontiguousarray(L0_attn_memory_norm),
        "memory_weight": np.ascontiguousarray(L0_attn_memory_weight),
        "router_w": chunks(np.asarray(L0_ffn_router_w).T),
        "e_bias": np.ascontiguousarray(L0_ffn_e_bias),
        "wts": np.ascontiguousarray(np.concatenate([
            gu.transpose(2, 0, 1).reshape(DC, P, E, 2 * I).transpose(1, 2, 0, 3).reshape(P, E, -1),
            dn[:, 0:P].transpose(1, 0, 2)], axis=2)),
        "dnr": np.ascontiguousarray(dn[:, P:I].reshape(E // 2, P, D).transpose(1, 0, 2)),
        "sgu": chunks(np.concatenate([np.asarray(L0_ffn_shared_gate_w), np.asarray(L0_ffn_shared_up_w)]).T),
        "sdn": np.ascontiguousarray(sdn[0:P]),
        "sdnr": np.ascontiguousarray(sdn[P:I]),
    } | constants(T)
    nc = bacc.Bacc("TRN2", target_bir_lowering=False, num_devices=1)
    a = {k: nc.dram_tensor(f"in_{k}", v.shape, mybir.dt.from_np(v.dtype), kind="ExternalInput").ap() for k, v in arrays.items()}
    out = nc.dram_tensor("out", [B, S, D], F32, kind="ExternalOutput").ap()
    build(nc, T, a, out)
    r = run_bass_kernel_spmd(nc, [{f"in_{k}": v for k, v in arrays.items()}], core_ids=[0])
    return r.results[0]["out"]
```

```python
from contextlib import ExitStack

import numpy as np

import concourse.bass as bass
from concourse import mybir

ALU = mybir.AluOpType
ACT = mybir.ActivationFunctionType
F32 = mybir.dt.float32
BF16 = mybir.dt.bfloat16
U32 = mybir.dt.uint32
I32 = mybir.dt.int32
AX_X = mybir.AxisListType.X

P = 128
D = 512
DC = D // P
SEQ = 512
NQ = 4
NH = 8
DH = 16
UT = 256
EPS = 1e-5
E = 16
K = 4
I = 192
IR = I - P
FIRST = 4
PARTS = 3
ROWS = 6 * DH
MROWS = 2
SCALE = 1.0 / float(np.sqrt(np.float32(DH)))


def sizes(T):
    stride = T + P
    return stride, E * stride


def attention(nc, T, io, shared, keep, scratch):
    x, wq, wk, wv, memory, memory_norm, memory_weight, router_w, e_bias = io
    NU = T // UT
    ctx = ExitStack()

    def sb(name, shape, dt=F32):
        return ctx.enter_context(nc.sbuf_tensor(name, shape, dt))

    def sem(name):
        return ctx.enter_context(nc.semaphore(name))

    w_sb = sb("w_sb", [P, DC, D + 2 * P])
    mem_sb = sb("mem_sb", [P, P])
    memn_sb = sb("memn_sb", [P, 1])
    rw_sb = sb("rw_sb", [P, DC, E])
    eb_sb = sb("eb_sb", [P, E])
    identb = sb("identb", [P, P], BF16)
    before = sb("before", [P, P], BF16)
    ones = sb("ones", [P, P], BF16)
    gate = sb("gate", [P, 4])
    half = sb("half", [P, 2])
    x_sb = sb("x_sb", [P, 2, 2, D])
    xn = sb("xn", [P, 2, D])
    xnT = sb("xnT", [P, DC, UT])
    stats = sb("stats", [P, 2, 6])
    mv = sb("mv", [P, 2, 2])
    rs = sb("rs", [P, 4, 2])
    qf = sb("qf", [P, NQ + 1, UT])
    rest = sb("rest", [P, NQ + 1, UT])
    parts = sb("parts", [P, NQ + 1, PARTS, UT], BF16)
    sg = sb("sg", [P, NQ, UT])
    sig = sb("sig", [P, NQ, UT])
    rn = sb("rn", [P, 2, 2, NQ])
    am = sb("am", [P, 2, D])
    v_all = sb("v_all", [P, T // P, P])
    qs = sb("qs", [P, 4, NQ, SEQ], BF16)
    ks = sb("ks", [P, 4, SEQ], BF16)
    vs = sb("vs", [P, 4, 4, 32])
    prob = sb("prob", [P, 4, NQ, SEQ])
    mx = sb("mx", [P, 2, 16])
    mb = sb("mb", [P, 2, 2, 16], BF16)
    mT = sb("mT", [32, 2, P], BF16)
    oT = sb("oT", [P, SEQ])
    rec = sb("rec", [P, 16])
    o_all = sb("o_all", [P, 8, 16, 4, DH])
    xm_sb = sb("xm_sb", [P, 2, D])
    x2 = sb("x2", [P, 2, D])
    xn2 = sb("xn2", [P, 2, D])
    xn2T = sb("xn2T", [P, DC, UT])
    stats2 = sb("stats2", [P, 2, 6])
    mv2 = sb("mv2", [P, 2, 2])
    rs2 = sb("rs2", [P, 4, 2])
    rt = sb("rt", [P, 3, 2, E])
    top8 = sb("top8", [P, 2, 8])
    idx8 = sb("idx8", [P, 2, 8], U32)
    idxf = sb("idxf", [P, 2, K])
    mk = sb("mk", [P, 2, K, E])
    mw = sb("mw", [P, 2, K, E])
    mkb = sb("mkb", [P, 2, E], BF16)
    wk4 = sb("wk4", [P, 3, 2, K])
    rk = sb("rk", [P, 2, 2, E])
    slotf = sb("slotf", [P, 2, K])
    slot_now = sb("slot_now", [P, 2, K], U32)

    ps_max = ctx.enter_context(nc.psum_tensor("ps_max", [P, 2, 2, SEQ], F32))
    ps_exp = ctx.enter_context(nc.psum_tensor("ps_exp", [P, 2, SEQ], F32))
    ps_pv = ctx.enter_context(nc.psum_tensor("ps_pv", [P, SEQ], F32))
    ps_misc = ctx.enter_context(nc.psum_tensor("ps_misc", [P, SEQ], F32))
    misc_b = ps_misc[:, :].bitcast(BF16)

    identf, iota16, iotap, ebase, cnt, w_all, slot_all, e_all = (
        keep[k] for k in ("identf", "iota16", "iotap", "ebase", "cnt", "w_all", "slot_all", "e_all"))
    QK, XM, X2, XN2, XS = (scratch[k] for k in ("QK", "XM", "X2", "XN2", "XS"))

    s_w = sem("s_weights")
    s_ws = sem("s_shared_expert_weights")
    s_eb = sem("s_router_weights")
    s_const = sem("s_constants")
    s_cst = sem("s_constants_dve")
    s_cstp = sem("s_constants_pool")
    s_gate = sem("s_gate")
    s_x = sem("s_x_loaded")
    s_bn = sem("s_bn")
    s_mv = sem("s_mean_var")
    s_rst = sem("s_rstd_steps")
    s_rstd = sem("s_rstd")
    s_xn = sem("s_xn")
    s_xnTp = sem("s_xnT_in_psum")
    s_xnT = sem("s_xnT")
    s_proj = sem("s_proj_in_psum")
    s_qf = sem("s_qkv_in_sbuf")
    s_v = sem("s_v")
    s_eq = sem("s_exp_q")
    s_eq1 = sem("s_exp_q_minus_1")
    s_sig = sem("s_sigma")
    s_split = sem("s_split_steps")
    s_parts = sem("s_parts")
    s_qk = sem("s_qk_stored")
    s_den = sem("s_mem_norm_in_psum")
    s_rn = sem("s_mem_norm_steps")
    s_amp = sem("s_mem_in_psum")
    s_am = sem("s_mem_read")
    s_xmst = sem("s_xm_stored")
    s_stage = [sem(f"s_head_staged{k}") for k in range(4)]
    s_maxp = sem("s_scores_for_max")
    s_maxd = sem("s_max_taken")
    s_mh = sem("s_max_high")
    s_mb = sem("s_max_parts")
    s_mTp = sem("s_maxT_in_psum")
    s_mT = sem("s_maxT")
    s_mrow = [sem(f"s_max_rows{k}") for k in range(4)]
    s_sc = sem("s_scores")
    s_exp = sem("s_exp")
    s_vs = sem("s_vs")
    s_pv = sem("s_pv")
    s_oT = sem("s_oT")
    s_otp = sem("s_o_in_psum")
    s_rec = sem("s_o_reciprocal")
    s_o = sem("s_o")
    s_misc = sem("s_misc_free")
    s_xml = sem("s_xm_loaded")
    s_x2 = sem("s_x2")
    s_x2st = sem("s_x2_xn2_stored")
    s_bn2 = sem("s_bn2")
    s_mv2 = sem("s_mean_var2")
    s_rst2 = sem("s_rstd2_steps")
    s_rstd2 = sem("s_rstd2")
    s_xn2 = sem("s_xn2")
    s_xn2Tp = sem("s_xn2T_in_psum")
    s_xn2T = sem("s_xn2T")
    s_lg = sem("s_logits")
    s_el = sem("s_exp_logits")
    s_rt = sem("s_router_steps")
    s_mkb = sem("s_chosen")
    s_rkp = sem("s_rank_in_psum")
    s_rt2 = sem("s_slot_steps")
    s_slot = sem("s_slots")
    s_sct = sem("s_scattered")
    s_spg = sem("s_sp_gate")
    s_plg = sem("s_pool_gate")
    s_dvg = sem("s_dve_gate")

    QK_DMAS = NH * 16
    STAGED = 9 * 16
    ROUTER = 13
    SLOTS = 6

    NB = NU
    PHASES = [(0, None, None, 2), (2, 0, None, 1), (3, 1, None, 2), (5, 3, 0, 1), (6, 4, 1, NU - 7), (NU - 1, NB - 3, NU - 6, 1),
              (None, NB - 2, NU - 5, 1), (None, NB - 1, NU - 4, 1), (None, NB, NU - 3, 1), (None, None, NU - 2, 2)]

    def phases(eng, body, pair):
        for a0, b0, c0, repeats in PHASES:
            if b0 is None:
                pair([[None if i is None else i + n for i in (a0, None, c0)] for n in range(2)])
            elif repeats == 1:
                body(a0, b0, c0)
            else:
                with eng.Fori(0, repeats) as r:
                    body(*(None if i is None else r + i for i in (a0, b0, c0)))

    def heads_of(b):
        return [(k, 4 * b + k) for k in range(4)]

    MID, END = 0.0, 0.5
    STAGGER = 6

    def schedule(a, c, of_a, of_c):
        def at(place):
            for of, unit in ((of_a, a), (of_c, c)):
                for task in of.get(place, []) if unit is not None else []:
                    task()
        return at

    def staggered(ats):
        for e in range(16 + STAGGER):
            for place in (MID, END):
                for n, at in enumerate(ats):
                    at(e - STAGGER * n + place)

    def xn2_of(c):
        return keep["last_rows"] if isinstance(c, int) and c == NU - 1 else xn2

    def runs(g, lo, hi):
        return lo <= g < hi if isinstance(g, int) else True

    NG = 4 * NB

    block = ctx.enter_context(nc.Block())

    @block.sync
    def _(sp):
        def wait(s, n):
            sp.wait_ge(s, n)
            sp.sem_inc(s_spg, 1)

        def store_xm(a):
            wait(s_am, 2 * a + 2)
            sp.dma_start(XM[bass.ds(a, 1)].rearrange("o t p d -> (o p) t d"), am[:]).then_inc(s_xmst, 16)

        def load_x(a):
            rows = x.rearrange("(u t p) d -> p u t d", p=P, t=2)
            sp.dma_start(x_sb[:, bass.ds(a % 2, 1)], rows[:, bass.ds(a, 1), :, :]).then_inc(s_x, 16)

        def stage_head(b, k, g):
            if not (isinstance(g, int) and g < 4):
                wait(s_sc, 16 * g - 48)
            if k == 0:
                wait(s_qk, QK_DMAS * 2 * (b // 2) + 2 * QK_DMAS)
            src = QK[bass.ds(b, 1), k]
            q = src[:, 0:NQ].rearrange("o q r t -> (o r) q t")
            kk = src[:, NQ].rearrange("o r t -> (o r) t")
            for to, n in ((0, 3), (3, 2), (5, 1)):
                sp.dma_start(qs[to * DH:(to + n) * DH, k], q[0:n * DH]).then_inc(s_stage[k], 16)
            for to, part in enumerate((0, 0, 0, 1, 1, 2)):
                sp.dma_start(ks[to * DH:(to + 1) * DH, k], kk[part * DH:(part + 1) * DH]).then_inc(s_stage[k], 16)

        def max_rows(g, k):
            wait(s_mT, g + 1)
            for part in range(MROWS):
                sp.dma_start(qs[ROWS + part:ROWS + part + 1, k].rearrange("p q (s j) -> p (q s) j", j=P),
                             mT[16 * part:16 * part + 16, k % 2]).then_inc(s_mrow[k], 16)

        def loads(a, b, c):
            if c is not None:
                if not (isinstance(c, int) and c == 0):
                    wait(s_x2, 2 * c)
                wait(s_xmst, 16 * c + 16)
                sp.dma_start(xm_sb[:], XM[bass.ds(c, 1)].rearrange("o t p d -> (o p) t d")).then_inc(s_xml, 16)
            if a is not None:
                if not (isinstance(a, int) and a == 0):
                    store_xm(a - 1)
            elif isinstance(b, int) and b == NB - 2:
                store_xm(NU - 1)

        def next_x(a):
            if a is not None and not (isinstance(a, int) and a == NU - 1):
                wait(s_mv, 2 * a + 2)
                load_x(a + 1)

        def store_x2(c):
            wait(s_x2, 2 * c + 2)
            sp.dma_start(X2[bass.ds(c, 1)].rearrange("o t p d -> (o p) t d"), x2[:]).then_inc(s_x2st, 16)

        def store_xn2(c):
            wait(s_xn2, 2 * c + 2)
            sp.dma_start(XN2[bass.ds(c, 1)].rearrange("o t p d -> (o p) t d"), xn2_of(c)[:]).then_inc(s_x2st, 16)

        def body(a, b, c):
            for k, g in heads_of(b):
                if k == 2:
                    next_x(a)
                if k == 1:
                    loads(a, b, c)
                if runs(g, 0, NG):
                    stage_head(b, k, g)
                if runs(g, 2, NG + 2):
                    max_rows(g - 2, (k + 2) % 4)
            if c is not None:
                store_x2(c)
                store_xn2(c)

        def pair(units):
            (a0, _, c0), (a1, _, c1) = units
            loads(a0, None, c0)
            if a0 is not None:
                next_x(a0)
                loads(a1, None, None)
                next_x(a1)
            else:
                store_x2(c0)
                loads(None, None, c1)
                store_xn2(c0)
                store_x2(c1)
                store_xn2(c1)

        load_x(0)
        sp.dma_start(identf[:], scratch["c_identf"]).then_inc(s_const, 16)
        sp.dma_start(iota16[:], scratch["c_iota16"]).then_inc(s_const, 16)
        sp.dma_start(iotap[:], scratch["c_iotap"]).then_inc(s_const, 16)
        sp.dma_start(rest[:, 0, 0:P], scratch["c_before"]).then_inc(s_const, 16)
        sp.dma_start(gate[:, 0:1], memory_weight.partition_broadcast(P)).then_inc(s_const, 16)
        sp.dma_start(w_sb[:, :, 0:D], wq).then_inc(s_w, 16)
        sp.dma_start(w_sb[:, :, D:D + P], wk).then_inc(s_w, 16)
        sp.dma_start(w_sb[:, :, D + P:], wv).then_inc(s_w, 16)
        sp.dma_start(mem_sb[:], memory).then_inc(s_w, 16)
        sp.dma_start(memn_sb[:], memory_norm).then_inc(s_w, 16)
        sp.dma_start(rw_sb[:], router_w).then_inc(s_eb, 16)
        sp.dma_start(eb_sb[:], e_bias.partition_broadcast(P)).then_inc(s_eb, 16)
        sp.dma_start(ebase[:], scratch["c_ebase"]).then_inc(s_eb, 16)
        for k in ("sgu", "sdn", "sdnr"):
            sp.dma_start(keep[k][:], shared[k]).then_inc(s_ws, 16)
        phases(sp, body, pair)
        sp.wait_ge(s_ws, 48)
        sp.wait_ge(s_x2st, 32 * NU)

    @block.gpsimd
    def _(pool):
        def wait(s, n):
            pool.wait_ge(s, n)
            pool.sem_inc(s_plg, 1)

        def copy(out, in_):
            return pool.tensor_scalar(out, in_, 1.0, 0.0, ALU.mult, ALU.add)

        pool.memset(half[:], -0.5).then_inc(s_cstp, 1)
        pool.memset(vs[:], 0.0).then_inc(s_cstp, 1)
        pool.wait_ge(s_cstp, 2)
        pool.memset(vs[:, :, :, DH:DH + 1], 1.0).then_inc(s_cstp, 1)
        pool.wait_ge(s_cstp, 3)

        def rstd(u, mv_, rs_, ready, steps, done):
            wait(ready, 2 * u + 2)
            var = mv_[:, :, 1]
            pool.tensor_scalar(rs_[:, 0, :], var, 1.0, EPS, ALU.mult, ALU.add).then_inc(steps, 1)
            wait(steps, 5 * u + 1)
            pool.tensor_tensor(rs_[:, 1, :], rs_[:, 0, :], half[:], ALU.pow).then_inc(steps, 1)
            wait(steps, 5 * u + 2)
            pool.tensor_tensor(rs_[:, 2, :], rs_[:, 0, :], rs_[:, 1, :], ALU.mult).then_inc(steps, 1)
            wait(steps, 5 * u + 3)
            pool.tensor_tensor(rs_[:, 2, :], rs_[:, 2, :], rs_[:, 1, :], ALU.mult).then_inc(steps, 1)
            wait(steps, 5 * u + 4)
            pool.tensor_scalar(rs_[:, 2, :], rs_[:, 2, :], -0.5, 1.5, ALU.mult, ALU.add).then_inc(steps, 1)
            wait(steps, 5 * u + 5)
            pool.tensor_tensor(rs_[:, 3, :], rs_[:, 1, :], rs_[:, 2, :], ALU.mult).then_inc(done, 1)

        def split(a):
            wait(s_qf, 3 * a + 3)
            if not (isinstance(a, int) and a == 0):
                wait(s_qk, QK_DMAS * a)
            copy(parts[:, :, 0], qf[:]).then_inc(s_split, 1)
            wait(s_split, 3 * a + 1)
            pool.tensor_tensor(rest[:], qf[:], parts[:, :, 0], ALU.subtract).then_inc(s_split, 1)
            wait(s_split, 3 * a + 2)
            copy(parts[:, :, 1], rest[:]).then_inc(s_split, 1)
            wait(s_split, 3 * a + 3)
            pool.tensor_tensor(parts[:, :, 2], rest[:], parts[:, :, 1], ALU.subtract).then_inc(s_parts, 1)

        def store_split(a):
            wait(s_parts, a + 1)
            for h in range(NH):
                dst = QK[bass.ds(2 * (a // 2) + h // 4, 1), h % 4].rearrange("o q (s d) t -> (o d) (q s) t", d=DH)
                pool.dma_start(dst[:, :, bass.ds((a % 2) * UT, UT)],
                               parts[h * DH:(h + 1) * DH].rearrange("p q s t -> p (q s) t")).then_inc(s_qk, 16)

        def stage_v(b, k, g):
            if not (isinstance(g, int) and g < 4):
                wait(s_pv, 4 * g - 12)
            if k == 0:
                wait(s_v, 2 * (b // 2) + 2)
            src = v_all[:, bass.ds((b // 2) * 4, 4), bass.ds((b % 2) * 4 * DH + k * DH, DH)]
            pool.tensor_copy(vs[:, k, :, 0:DH], src).then_inc(s_vs, 1)

        def scatter(c):
            wait(s_slot, c + 1)
            wait(s_xn2, 2 * c + 2)
            for t in range(2):
                for j in range(K):
                    at = slot_now[:, t, j:j + 1]
                    pool.indirect_dma_start(XS, bass.IndirectOffsetOnAxis(ap=at, axis=0), xn2_of(c)[:, t],
                                             None).then_inc(s_sct, 16)

        def body(a, b, c):
            def head_v(k):
                if b is not None and runs(4 * b + k, 0, NG):
                    stage_v(b, k, 4 * b + k)

            head_v(0)
            head_v(1)
            if a is not None:
                rstd(a, mv, rs, s_mv, s_rst, s_rstd)
            if c is not None:
                rstd(c, mv2, rs2, s_mv2, s_rst2, s_rstd2)
            head_v(2)
            if a is not None:
                split(a)
            head_v(3)
            if a is not None:
                store_split(a)
            if c is not None:
                scatter(c)

        def pair(units):
            (a0, _, c0), (a1, _, c1) = units
            if a0 is not None:
                for a in (a0, a1):
                    rstd(a, mv, rs, s_mv, s_rst, s_rstd)
                for a in (a0, a1):
                    split(a)
                    store_split(a)
            else:
                for c in (c0, c1):
                    rstd(c, mv2, rs2, s_mv2, s_rst2, s_rstd2)
                scatter(c0)

        phases(pool, body, pair)
        pool.wait_ge(s_sct, (NU - 1) * 2 * K * 16)

    @block.scalar
    def _(act):
        act.wait_ge(s_const, 16 * 5)
        act.activation(gate[:, 1:2], gate[:, 0:1], ACT.Exp, scale=-1.0).then_inc(s_gate, 1)

        def body(a, b, c):
            def xnT_out(t):
                act.wait_ge(s_xnTp, 2 * a + t + 1)
                act.activation(xnT[:, :, t * P:(t + 1) * P], ps_misc[:, :].rearrange("p (c t) -> p c t", c=DC),
                               ACT.Copy).then_inc(s_xnT, 1)

            def q_out(j):
                act.wait_ge(s_proj, 3 * a + j + 1)
                if j == 0 and not (isinstance(a, int) and a == 0):
                    act.wait_ge(s_parts, a)
                    act.wait_ge(s_sig, a)
                act.activation(qf[:, 2 * j:2 * j + 2], ps_misc[:, :].rearrange("p (q t) -> p q t", q=2),
                               ACT.Copy).then_inc(s_qf, 1)

            def kv_out():
                act.wait_ge(s_proj, 3 * a + 3)
                act.activation(v_all[:, bass.ds(2 * a, 2)], ps_misc[:, UT:].rearrange("p (t f) -> p t f", t=2),
                               ACT.Copy).then_inc(s_v, 1)
                act.activation(qf[:, NQ], ps_misc[:, 0:UT], ACT.Copy).then_inc(s_qf, 1)

            def exp_q():
                act.wait_ge(s_qf, 3 * a + 3)
                act.activation(sg[:], qf[:, 0:NQ], ACT.Exp).then_inc(s_eq, 1)

            def xn2T_out(t):
                act.wait_ge(s_xn2Tp, 2 * c + t + 1)
                act.activation(xn2T[:, :, t * P:(t + 1) * P], ps_misc[:, :].rearrange("p (c t) -> p c t", c=DC),
                               ACT.Copy).then_inc(s_xn2T, 1)

            def exp_logits():
                act.wait_ge(s_lg, c + 1)
                act.activation(rt[:, 0], ps_misc[:, 0:2 * E].rearrange("p (t e) -> p t e", t=2), ACT.Exp,
                               scale=-1.0).then_inc(s_el, 1)

            at = schedule(a, c, {5: [lambda: xnT_out(0)], 6: [lambda: xnT_out(1)], 7 + END: [lambda: q_out(0)],
                                 8 + END: [lambda: q_out(1)], 9: [kv_out, exp_q]},
                          {7 + END: [lambda: xn2T_out(0)], 8 + END: [lambda: xn2T_out(1)], 10: [exp_logits]}
                          if a is None else
                          {10: [lambda: xn2T_out(0)], 11: [lambda: xn2T_out(1)], 11 + END: [exp_logits]})

            def exps(g, s, qs_):
                for q in qs_:
                    n = 16 * g + 4 * s + q - 32
                    act.wait_ge(s_sc, n + 1)
                    if q == 0 and not (isinstance(g, int) and g < 3):
                        act.wait_ge(s_pv, 4 * g + s - 11)
                    act.activation(prob[:, s, q], ps_exp[:, q % 2], ACT.Exp, scale=SCALE).then_inc(s_exp, 1)

            def oT_out(g):
                act.wait_ge(s_pv, 4 * g - 8)
                if not (isinstance(g, int) and g == 3):
                    act.wait_ge(s_otp, g - 3)
                act.activation(oT[:], ps_pv[:], ACT.Copy).then_inc(s_oT, 1)

            def mT_out(g, k):
                act.wait_ge(s_mTp, g)
                if not (isinstance(g, int) and g < 3):
                    times = (g - 3) // 4 + 1 if isinstance(g, int) else b + (k == 3)
                    act.wait_ge(s_mrow[(k + 1) % 4], 16 * MROWS * times)
                act.activation(mT[:, (k + 1) % 2], misc_b[0:32, 0:P], ACT.Copy).then_inc(s_mT, 1)

            if b is None:
                return at
            for k, g in heads_of(b):
                for s in range(4):
                    if runs(g, 2, NG + 2):
                        exps(g, s, (0, 1))
                    at(4 * k + s + MID)
                    if runs(g, 2, NG + 2):
                        exps(g, s, (2, 3))
                    at(4 * k + s + END)
                    if s == 0 and runs(g, 3, NG + 3):
                        oT_out(g)
                    if s == 1 and runs(g, 1, NG + 1):
                        mT_out(g, k)

        phases(act, body, lambda units: staggered([body(*unit) for unit in units]))

    @block.vector
    def _(dve):
        dve.memset(ones[:], 1.0).then_inc(s_cst, 1)
        dve.memset(ks[ROWS:ROWS + 32, :, :], 1.0).then_inc(s_cst, 1)
        dve.memset(cnt[:], 0.0).then_inc(s_cst, 1)
        dve.wait_ge(s_gate, 1)
        dve.tensor_scalar(gate[:, 2:3], gate[:, 1:2], 1.0, None, ALU.add).then_inc(s_gate, 1)
        dve.wait_ge(s_gate, 2)
        dve.reciprocal(gate[:, 1:2], gate[:, 2:3]).then_inc(s_gate, 1)
        dve.wait_ge(s_gate, 3)
        dve.tensor_scalar(gate[:, 3:4], gate[:, 1:2], -1.0, 1.0, ALU.mult, ALU.add).then_inc(s_gate, 1)
        dve.wait_ge(s_gate, 4)
        dve.wait_ge(s_cst, 3)
        dve.wait_ge(s_const, 16 * 5)
        dve.tensor_copy(identb[:], identf[:]).then_inc(s_cst, 1)
        dve.tensor_copy(before[:], rest[:, 0, 0:P]).then_inc(s_cst, 1)
        dve.sem_inc(s_misc, 1)

        def gated(s, n):
            dve.wait_ge(s, n)
            dve.sem_inc(s_dvg, 1)

        def body(a, b, c):
            def stats_of(u, t, src, st, mv_, bn, done):
                dve.bn_stats(st[:, t], src).then_inc(bn, 1)
                gated(bn, 2 * u + t + 1)
                dve.bn_aggr(mv_[:, t], st[:, t]).then_inc(done, 1)

            def normalise(u, t, src, out, mv_, rs_, ready, done):
                dve.wait_ge(ready, u + 1)
                dve.tensor_scalar(out[:, t], src, mv_[:, t, 0:1], rs_[:, 3, t:t + 1], ALU.subtract,
                                  ALU.mult).then_inc(done, 1)

            def x_of(t):
                return x_sb[:, bass.ds(a % 2, 1), t].rearrange("p o d -> p (o d)")

            def a_stats(t):
                gated(s_x, 16 * a + 16)
                stats_of(a, t, x_of(t), stats, mv, s_bn, s_mv)

            def a_norm(t):
                if not (isinstance(a, int) and a == 0):
                    dve.wait_ge(s_xnTp, 2 * a)
                normalise(a, t, x_of(t), xn, mv, rs, s_rstd, s_xn)

            def a_elu(step):
                if step == 0:
                    dve.wait_ge(s_eq, a + 1)
                    dve.tensor_scalar(sg[:], sg[:], 1.0, -1.0, ALU.min, ALU.add).then_inc(s_eq1, 1)
                else:
                    dve.wait_ge(s_eq1, a + 1)
                    dve.tensor_tensor(sig[:], qf[:, 0:NQ], sg[:], ALU.max).then_inc(s_sig, 1)

            def mem_norm():
                dve.wait_ge(s_den, a + 1)
                dve.reciprocal(rn[:, 0], ps_misc[:, 0:2 * NQ].rearrange("p (t q) -> p t q", t=2)).then_inc(s_rn, 1)
                dve.wait_ge(s_rn, 2 * a + 1)
                dve.tensor_scalar(rn[:, 1], rn[:, 0], gate[:, 1:2], None, ALU.mult).then_inc(s_rn, 1)

            def mem_out(t):
                dve.wait_ge(s_rn, 2 * a + 2)
                dve.wait_ge(s_amp, 2 * a + t + 1)
                if t == 0 and not (isinstance(a, int) and a == 0):
                    dve.wait_ge(s_xmst, 16 * a)
                for q in range(NQ):
                    f = slice(q * P, (q + 1) * P)
                    last = dve.scalar_tensor_tensor(am[:, t, f], ps_misc[:, f], rn[:, 1, t, q:q + 1], x_of(t)[:, f],
                                                    ALU.mult, ALU.add)
                last.then_inc(s_am, 1)

            def c_residual(t):
                dve.wait_ge(s_xml, 16 * c + 16)
                dve.wait_ge(s_o, 8 * (c // 2) + 8)
                if not (isinstance(c, int) and c == 0):
                    dve.wait_ge(s_x2st, 32 * c)
                for hf in range(2):
                    ring = (2 * (c // 2) + hf) % 8
                    o = o_all[:, bass.ds(ring, 1), bass.ds((2 * (c % 2) + t) * NQ, NQ)].rearrange("p r q h d -> p (r q) (h d)")
                    x4 = x2[:, t].rearrange("p (q v f) -> p q v f", q=NQ, v=2)[:, :, hf]
                    m4 = xm_sb[:, t].rearrange("p (q v f) -> p q v f", q=NQ, v=2)[:, :, hf]
                    last = dve.scalar_tensor_tensor(x4, o, gate[:, 3:4], m4, ALU.mult, ALU.add)
                last.then_inc(s_x2, 1)

            def c_stats(t):
                gated(s_x2, 2 * c + t + 1)
                stats_of(c, t, x2[:, t], stats2, mv2, s_bn2, s_mv2)

            def c_norm(t):
                if not (isinstance(c, int) and c in (0, NU - 1)):
                    dve.wait_ge(s_sct, 2 * K * 16 * c)
                    dve.wait_ge(s_xn2Tp, 2 * c)
                normalise(c, t, x2[:, t], xn2_of(c), mv2, rs2, s_rstd2, s_xn2)

            def link(ins, n):
                ins.then_inc(s_rt, 1)
                gated(s_rt, ROUTER * c + n)

            def router():
                if isinstance(c, int) and c == 0:
                    dve.wait_ge(s_eb, 48)
                dve.wait_ge(s_el, c + 1)
                link(dve.tensor_scalar(rt[:, 2], rt[:, 0], 1.0, None, ALU.add), 1)
                link(dve.reciprocal(rt[:, 1], rt[:, 2]), 2)
                link(dve.tensor_tensor(rt[:, 2], rt[:, 1], eb_sb[:, :].unsqueeze(1).to_broadcast([P, 2, E]), ALU.add), 3)

            def best():
                for t in range(2):
                    link(dve.max(top8[:, t], rt[:, 2, t]), 4 + t)
                for t in range(2):
                    link(dve.max_index(idx8[:, t], top8[:, t], rt[:, 2, t]), 6 + t)

            def chosen():
                link(dve.tensor_copy(idxf[:], idx8[:, :, 0:K]), 8)
                link(dve.tensor_tensor(mk[:], iota16[:, 0:E].unsqueeze(1).unsqueeze(1).to_broadcast([P, 2, K, E]),
                                       idxf[:, :, :].unsqueeze(3).to_broadcast([P, 2, K, E]), ALU.is_equal), 9)
                dve.tensor_reduce(mkb[:], mk[:, :, :, :].rearrange("p t k e -> p t e k"), AX_X, ALU.max).then_inc(s_mkb, 1)

            def weights():
                link(dve.tensor_tensor(mw[:], mk[:], rt[:, 1].unsqueeze(2).to_broadcast([P, 2, K, E]), ALU.mult), 10)
                link(dve.tensor_reduce(wk4[:, 0], mw[:], AX_X, ALU.add), 11)
                link(dve.tensor_reduce(wk4[:, 1, :, 0:1], wk4[:, 0], AX_X, ALU.add), 12)
                dve.tensor_scalar(wk4[:, 1, :, 1:2], wk4[:, 1, :, 0:1], 1e-20, None, ALU.add).then_inc(s_rt, 1)
                dve.wait_ge(s_rt, ROUTER * c + 13)

            def link2(ins, n):
                ins.then_inc(s_rt2, 1)
                dve.wait_ge(s_rt2, SLOTS * c + n)

            def ranks_of():
                dve.wait_ge(s_rkp, c + 1)
                ranks = ps_misc[:, 0:3 * E].rearrange("p (t e) -> p t e", e=E)
                link2(dve.tensor_tensor(rk[:, 0], ranks[:, 0:2], cnt[:, 0].unsqueeze(1).to_broadcast([P, 2, E]), ALU.add), 1)
                dve.tensor_tensor(cnt[:, 0], ranks[:, 2], cnt[:, 0], ALU.add).then_inc(s_misc, 1)

            def slots():
                link2(dve.reciprocal(wk4[:, 2, :, 0:1], wk4[:, 1, :, 1:2]), 2)
                link2(dve.tensor_tensor(w_all[:, bass.ds(2 * c, 2)], wk4[:, 0], wk4[:, 2, :, 0:1].to_broadcast([P, 2, K]),
                                        ALU.mult), 3)
                link2(dve.tensor_tensor(rk[:, 1], rk[:, 0], ebase[:, :].unsqueeze(1).to_broadcast([P, 2, E]), ALU.add), 4)
                link2(dve.tensor_tensor(mw[:], mk[:], rk[:, 1].unsqueeze(2).to_broadcast([P, 2, K, E]), ALU.mult), 5)
                link2(dve.tensor_reduce(slotf[:], mw[:], AX_X, ALU.add), 6)
                last = isinstance(c, int) and c == NU - 1
                if not (last or isinstance(c, int) and c == 0):
                    dve.wait_ge(s_sct, 2 * K * 16 * c)
                dve.tensor_copy(slot_all[:, bass.ds(2 * c, 2)], slotf[:])
                dve.tensor_copy(e_all[:, bass.ds(2 * c, 2)], idxf[:])
                dve.tensor_copy((keep["last_slots"] if last else slot_now)[:], slotf[:]).then_inc(s_slot, 1)

            at = schedule(a, c, {0: [lambda: a_stats(0)], 1: [lambda: a_stats(1)], 4: [lambda: a_norm(0)],
                                 4 + END: [lambda: a_norm(1)], 9 + END: [lambda: a_elu(0)], 10: [lambda: a_elu(1)],
                                 12: [mem_norm], 12 + END: [lambda: mem_out(0)], 15 + END: [lambda: mem_out(1)]},
                          {1: [lambda: c_residual(0)], 1 + END: [lambda: c_residual(1)], 3: [lambda: c_stats(0)],
                           3 + END: [lambda: c_stats(1)], 5: [lambda: c_norm(0)], 5 + END: [lambda: c_norm(1)],
                           10 + END: [router], 11: [best], 11 + END: [chosen], 12 + END: [ranks_of], 13: [weights],
                           13 + END: [slots]}
                          if a is None else
                          {7: [lambda: c_residual(0)], 7 + END: [lambda: c_residual(1)], 8: [lambda: c_stats(0)],
                           8 + END: [lambda: c_stats(1)], 9: [lambda: c_norm(0), lambda: c_norm(1)],
                           11 + END: [router], 12: [best], 12 + END: [chosen], 13: [ranks_of], 13 + END: [weights], 14 + END: [slots]})

            def split_max(g, k):
                dve.wait_ge(s_maxd, 8 * g)
                j = (k + 1) % 2
                if not (isinstance(g, int) and g < 3):
                    dve.wait_ge(s_mTp, g - 2)
                dve.tensor_scalar(mb[:, j, 0], mx[:, j], -1.0, None, ALU.mult).then_inc(s_mh, 1)
                dve.wait_ge(s_mh, g)
                dve.scalar_tensor_tensor(mb[:, j, 1], mx[:, j], -1.0, mb[:, j, 0], ALU.mult, ALU.subtract).then_inc(s_mb, 1)

            def maxima(g, k, s, p):
                dve.wait_ge(s_maxp, 8 * g + 2 * s + p + 1)
                dve.tensor_reduce(mx[:, k % 2, 4 * s + 2 * p:4 * s + 2 * p + 2], ps_max[:, p], AX_X,
                                  ALU.max).then_inc(s_maxd, 1)

            def o_out(g, k):
                v = ps_misc[:, :].rearrange("p (n e) -> p n e", e=32)
                dve.wait_ge(s_otp, g - 2)
                dve.reciprocal(rec[:, :].unsqueeze(2), v[:, :, DH:DH + 1]).then_inc(s_rec, 1)
                dve.wait_ge(s_rec, g - 2)
                kk = (k + 1) % 4
                bb = b if k == 3 else b - 1
                dve.tensor_tensor(o_all[:, bass.ds(bb % 8, 1), :, kk].rearrange("p r n d -> p (r n) d"), v[:, :, 0:DH],
                                  rec[:, :].unsqueeze(2).to_broadcast([P, 16, DH]), ALU.mult).then_inc(s_o, 1)

            if b is None:
                return at
            for k, g in heads_of(b):
                for s in range(4):
                    if s == 0 and runs(g, 1, NG + 1):
                        split_max(g, k)
                    if runs(g, 0, NG):
                        maxima(g, k, s, 0)
                    at(4 * k + s + MID)
                    if runs(g, 0, NG):
                        maxima(g, k, s, 1)
                    if s == 2 and runs(g, 3, NG + 3):
                        o_out(g, k)
                    at(4 * k + s + END)

        phases(dve, body, lambda units: staggered([body(*unit) for unit in units]))

    @block.tensor
    def _(pe):
        pe.wait_ge(s_const, 16 * 5)
        pe.wait_ge(s_cst, 5)
        last_use = []

        def body(a, b, c):
            def free_misc():
                for s, n in last_use:
                    pe.wait_ge(s, n)

            def set_free(s, n):
                last_use[:] = [(s, n)]

            def transposes(src, t, ready, n, done):
                pe.wait_ge(ready, n)
                for i in range(DC):
                    mm = pe.transpose(ps_misc[:, i * P:(i + 1) * P], src[:, t, i * P:(i + 1) * P], identf[:])
                mm.then_inc(done, 1)

            def a_T(t):
                free_misc()
                transposes(xn, t, s_xn, 2 * a + t + 1, s_xnTp)
                set_free(s_xnT, 2 * a + t + 1)

            def a_q(j):
                if isinstance(a, int) and a == 0 and j == 0:
                    pe.wait_ge(s_w, 16 * 5)
                free_misc()
                pe.wait_ge(s_xnT, 2 * a + 2)
                for q in range(2):
                    o = (2 * j + q) * P
                    for i in range(DC):
                        mm = pe.matmul(ps_misc[:, q * UT:(q + 1) * UT], w_sb[:, i, o:o + P], xnT[:, i], start=(i == 0),
                                       stop=(i == DC - 1))
                mm.then_inc(s_proj, 1)
                set_free(s_qf, 3 * a + j + 1)

            def a_kv():
                free_misc()
                for i in range(DC):
                    pe.matmul(ps_misc[:, 0:UT], w_sb[:, i, D:D + P], xnT[:, i], start=(i == 0), stop=(i == DC - 1))
                for t in range(2):
                    for i in range(DC):
                        mm = pe.matmul(ps_misc[:, UT + t * P:UT + (t + 1) * P], xnT[:, i, t * P:(t + 1) * P],
                                       w_sb[:, i, D + P:D + 2 * P], start=(i == 0), stop=(i == DC - 1))
                mm.then_inc(s_proj, 1)
                set_free(s_qf, 3 * a + 3)

            def a_den():
                free_misc()
                pe.wait_ge(s_sig, a + 1)
                for t in range(2):
                    for q in range(NQ):
                        mm = pe.matmul(ps_misc[:, t * NQ + q:t * NQ + q + 1], sig[:, q, t * P:(t + 1) * P], memn_sb[:],
                                       start=True, stop=True)
                mm.then_inc(s_den, 1)
                set_free(s_rn, 2 * a + 1)

            def a_mem(t):
                free_misc()
                for q in range(NQ):
                    mm = pe.matmul(ps_misc[:, q * P:(q + 1) * P], sig[:, q, t * P:(t + 1) * P], mem_sb[:], start=True,
                                   stop=True)
                mm.then_inc(s_amp, 1)
                set_free(s_am, 2 * a + t + 1)

            def c_T(t):
                free_misc()
                transposes(xn2_of(c), t, s_xn2, 2 * c + t + 1, s_xn2Tp)
                set_free(s_xn2T, 2 * c + t + 1)

            def c_logits():
                if isinstance(c, int) and c == 0:
                    pe.wait_ge(s_eb, 48)
                free_misc()
                pe.wait_ge(s_xn2T, 2 * c + 2)
                for t in range(2):
                    for i in range(DC):
                        mm = pe.matmul(ps_misc[:, t * E:(t + 1) * E], xn2T[:, i, t * P:(t + 1) * P], rw_sb[:, i],
                                       start=(i == 0), stop=(i == DC - 1))
                mm.then_inc(s_lg, 1)
                set_free(s_el, c + 1)

            def c_rank():
                free_misc()
                pe.wait_ge(s_mkb, c + 1)
                for to, terms in enumerate((((before, 0),), ((before, 1), (ones, 0)), ((ones, 0), (ones, 1)))):
                    for n, (m, t) in enumerate(terms):
                        mm = pe.matmul(ps_misc[:, to * E:(to + 1) * E], m[:], mkb[:, t], start=(n == 0),
                                       stop=(n == len(terms) - 1))
                mm.then_inc(s_rkp, 1)
                set_free(s_misc, c + 2)

            if b is None and (a == 1 or c == NU - 1):
                pass
            elif a is not None:
                last_use[:] = [] if isinstance(a, int) and a == 0 else [(s_am, 2 * a)]
            else:
                last_use[:] = [(s_am, 2 * NU), (s_misc, c + 1)] + ([(s_o, 4 * b - 3)] if b is not None else [])
            at = schedule(a, c, {5: [lambda: a_T(0)], 6: [lambda: a_T(1)], 7 + END: [lambda: a_q(0)], 8 + END: [lambda: a_q(1)],
                                 9: [a_kv], 12: [a_den], 12 + END: [lambda: a_mem(0)], 15 + END: [lambda: a_mem(1)]},
                          {7 + END: [lambda: c_T(0)], 8 + END: [lambda: c_T(1)], 10: [c_logits], 12 + END: [c_rank]}
                          if a is None else
                          {10: [lambda: c_T(0)], 11: [lambda: c_T(1)], 11 + END: [c_logits], 13: [c_rank]})

            def scores_for_max(g, k, s, p):
                if not (isinstance(g, int) and 8 * g + 2 * s + p < 2):
                    pe.wait_ge(s_maxd, 8 * g + 2 * s + p - 1)
                if s == 0 and p == 0:
                    pe.wait_ge(s_stage[k], STAGED * (b + 1))
                for i in range(2):
                    st = 2 * p + i
                    mm = pe.matmul(ps_max[:, p, i], qs[0:ROWS, k, s, st * P:(st + 1) * P], ks[0:ROWS, k], start=True,
                                   stop=True)
                mm.then_inc(s_maxp, 1)

            def scores(g, k, s, qs_):
                kk = (k + 2) % 4
                for q in qs_:
                    n = 16 * g + 4 * s + q - 32
                    if not (isinstance(g, int) and n < 2):
                        pe.wait_ge(s_exp, n - 1)
                    if s == 0 and q == 0:
                        times = (g - 2) // 4 + 1 if isinstance(g, int) else (b + 1 if k >= 2 else b)
                        pe.wait_ge(s_mrow[kk], 16 * MROWS * times)
                    pe.matmul(ps_exp[:, q % 2], ks[0:ROWS + MROWS, kk, s * P:(s + 1) * P], qs[0:ROWS + MROWS, kk, q],
                              start=True, stop=True).then_inc(s_sc, 1)

            def pv(g, kk, t, n):
                pe.wait_ge(s_exp, 4 * n + 4)
                if t == 0:
                    if not (isinstance(g, int) and g == 2):
                        pe.wait_ge(s_oT, g - 2)
                    pe.wait_ge(s_vs, g - 1)
                for q in range(NQ):
                    mm = pe.matmul(ps_pv[32 * q:32 * q + 32, :], vs[:, kk, t], prob[:, t, q], start=(t == 0), stop=(t == 3))
                mm.then_inc(s_pv, 1)

            def max_T(g, k):
                free_misc()
                pe.wait_ge(s_mb, g)
                pe.transpose(misc_b[0:32, 0:P], mb[:, (k + 1) % 2].rearrange("p a n -> p (a n)"), identb[:]).then_inc(s_mTp, 1)
                set_free(s_mT, g)

            def o_T(g):
                free_misc()
                pe.wait_ge(s_oT, g - 2)
                for i in range(4):
                    mm = pe.transpose(ps_misc[:, i * P:(i + 1) * P], oT[:, i * P:(i + 1) * P], identf[:])
                mm.then_inc(s_otp, 1)
                set_free(s_o, g - 2)

            if b is None:
                return at
            for k, g in heads_of(b):
                for s in range(4):
                    for half_ in range(2):
                        if runs(g, 2, NG + 2):
                            scores(g, k, s, (2 * half_,))
                        if runs(g, 0, NG):
                            scores_for_max(g, k, s, half_)
                        if runs(g, 2, NG + 2):
                            scores(g, k, s, (2 * half_ + 1,))
                        if half_ == 0:
                            at(4 * k + s + MID)
                            if s == 0:
                                if runs(g, 3, NG + 3):
                                    pv(g - 1, (k + 1) % 4, 3, 4 * g - 9)
                            elif runs(g, 2, NG + 2):
                                pv(g, (k + 2) % 4, s - 1, 4 * g - 8 + s - 1)
                    at(4 * k + s + END)
                    if s == 1 and runs(g, 1, NG + 1):
                        max_T(g, k)
                    if s == 2 and runs(g, 3, NG + 3):
                        o_T(g)

        phases(pe, body, lambda units: staggered([body(*unit) for unit in units]))

    ctx.close()



def feed_forward(nc, T, io, keep, scratch, out):
    wts_w, dnr_w = io
    NT = T // P
    NR = NT * K + E
    NS0 = FIRST
    R0, R1 = NS0, NS0 + NR
    NTILES = NT + NR
    LATE = 2
    NREST = NT - (NTILES - R1 - LATE)
    RING = 4
    W = DC * 2 * I + D
    POOL_PADS = 10
    SUMS = 2 * K
    ZERO_ROW = sizes(T)[1]
    ctx = ExitStack()

    def sb(name, shape, dt=F32):
        return ctx.enter_context(nc.sbuf_tensor(name, shape, dt))

    def sem(name):
        return ctx.enter_context(nc.semaphore(name))

    identf, iota16, iotap, ebase, cnt, w_all, slot_all, e_all = (
        keep[k] for k in ("identf", "iota16", "iotap", "ebase", "cnt", "w_all", "slot_all", "e_all"))
    X2, XN2, XS, Y, XO = (scratch[k] for k in ("X2", "XN2", "XS", "Y", "XO"))

    wts_sb = sb("wts_sb", [P, E, W])
    dnr_sb = sb("dnr_sb", [P, E // 2, D])
    sgu_sb, sdn_sb, sdnr_sb = (keep[k] for k in ("sgu", "sdn", "sdnr"))
    xt = sb("xt", [P, 2, D])
    xT = sb("xT", [P, 2, DC, P])
    gs = sb("gs", [P, 2, I])
    hid = sb("hid", [P, 2, 2, P])
    hT = sb("hT", [P, 2, 2, P])
    yt = sb("yt", [P, 2, D])
    x2t = sb("x2t", [P, 2, D])
    wts_flat = wts_sb[:, :, :].rearrange("p e n -> p (e n)")
    rows = wts_flat[:, 0:RING * K * D].rearrange("p (a k d) -> p a k d", a=RING, k=K)
    acc = wts_flat[:, RING * K * D:(RING * K + NT) * D].rearrange("p (t d) -> p t d", t=NT)
    at_now = sb("at_now", [P, RING, K], U32)
    par = sb("par", [P, 2, NR])
    tab = sb("tab", [1, 2, NR], U32)
    small = sb("small", [P, 8, E])
    smi = sb("smi", [P, E], I32)
    zero = sb("zero", [P, D])
    shift = sb("shift", [P, NT * K])
    at_all = sb("at_all", [P, NT * K], U32)
    padf = sb("padf", [P, E])
    padi = sb("padi", [P, E], U32)
    ji = sb("ji", [P, NR], I32)
    room = sb("room", [P, NR * (E + 9)])
    big = room[:, 0:NR * E].rearrange("p (j e) -> p j e", e=E)
    jrow = room[:, NR * E:NR * (E + 3)].rearrange("p (k j) -> p k j", k=3)
    jt = room[:, NR * (E + 3):NR * (E + 9)].rearrange("p (k j) -> p k j", k=6)

    ps_x = ctx.enter_context(nc.psum_tensor("ps_x", [P, 2, DC, P], F32))
    ps_gu = ctx.enter_context(nc.psum_tensor("ps_gu", [P, 2, D], F32))
    ps_h = ctx.enter_context(nc.psum_tensor("ps_h", [P, 2, DC, P], F32))
    ps_y = ctx.enter_context(nc.psum_tensor("ps_y", [P, 2, D], F32))

    s_wr = [sem(f"f_expert_weights{i}") for i in range(2)]
    s_exp = sem("f_experts_ready")
    s_tc = sem("f_table_constants")
    s_tb = sem("f_table_steps")
    s_tab = sem("f_tables")
    s_zero = sem("f_zero")
    s_pad = sem("f_pads")
    s_pad2 = sem("f_last_pads")
    s_last = sem("f_last_rows_scattered")
    s_x = [sem(f"f_x_loaded{p}") for p in range(2)]
    s_xp = sem("f_xT_in_psum")
    s_xT = sem("f_xT")
    s_gu = sem("f_gate_up")
    s_si = sem("f_silu")
    s_h = sem("f_hidden")
    s_hp = sem("f_hT_in_psum")
    s_hT = sem("f_hT")
    s_yp = sem("f_y_in_psum")
    s_y = sem("f_y")
    s_yst = [sem(f"f_y_stored{p}") for p in range(2)]
    s_x2 = [sem(f"f_x2_loaded{p}") for p in range(2)]
    s_at = sem("f_rows_wanted")
    s_rows = [sem(f"f_rows{i}") for i in range(RING)]
    s_acc = sem("f_first_sums_loaded")
    s_sum = sem("f_sum_steps")
    s_out = sem("f_out_stored")
    s_spg = sem("f_sp_gate")
    s_plg = sem("f_pool_gate")
    s_acg = sem("f_act_gate")

    SHARED, ROUTED = 0, 1

    class Tile:

        def __init__(self, h, p):
            self.h, self.p, self.n = h, p, h * 2 + p

        def of(self, kind, late, mod):
            self.kind, self.late = kind, late
            self.th = self.h - NR // 2 if late else self.h
            self.t = self.th * 2 + self.p
            self.j = None if kind == SHARED else self.n - R0
            self.m, self.m_ring = self.n - R1, (mod - R1) % RING
            return self

    H0, H1, H2 = R0 // 2, R1 // 2, NTILES // 2
    RUNS = [(h, SHARED, False, 1, 1) for h in range(H0)] + \
        [(H0, ROUTED, False, 1, 1), (H0 + 1, ROUTED, False, 1, H1 - H0 - 2), (H1 - 1, ROUTED, False, 1, 1),
         (H1, SHARED, True, 1, 1), (H1 + 1, SHARED, True, 1, 1), (H1 + 2, SHARED, True, 1, 1),
         (H1 + 3, SHARED, True, 2, (H2 - H1 - 4) // 2), (H2 - 1, SHARED, True, 1, 1)]

    def kind_of(h):
        return (SHARED, False) if h < H0 else (ROUTED, False) if h < H1 else (SHARED, True)

    def slots(eng, body):
        for h0, kind, late, pairs, repeats in RUNS:
            def pair(h, mod, kinds):
                made = [Tile(h + i // 2, i % 2).of(*kinds(i // 2), mod + i) for i in range(-1, 5)]
                for p in range(2):
                    body(*made[p:p + 4])

            if repeats == 1:
                pair(h0, 2 * h0, lambda i, h0=h0: kind_of(h0 + i))
            else:
                with eng.Fori(0, repeats) as r:
                    for i in range(pairs):
                        pair(r * pairs + (h0 + i), 2 * (h0 + i), lambda i, kind=kind, late=late: (kind, late))

    def exists(tile):
        return not isinstance(tile.n, int) or 0 <= tile.n < NTILES

    def rows_of(dram, t):
        return dram[bass.ds(t, 1)].rearrange("o p d -> (o p) d")

    def after(eng_wait, s, n):
        if not (isinstance(n, int) and n <= 0):
            eng_wait(s, n)

    block = ctx.enter_context(nc.Block())

    @block.sync
    def _(sp):
        def wait(s, n):
            sp.wait_ge(s, n)
            sp.sem_inc(s_spg, 1)

        def load_x(tile):
            after(wait, s_xp, tile.n - 1)
            if tile.kind == SHARED:
                sp.dma_start(xt[:, tile.p], rows_of(XN2, tile.t)).then_inc(s_x[tile.p], 16)
            else:
                row = sp.value_load(tab[0:1, 0, bass.ds(tile.j, 1)], min_val=0, max_val=ZERO_ROW)
                sp.dma_start(xt[:, tile.p], XS[bass.ds(row, P)]).then_inc(s_x[tile.p], 16)

        def load_x2(tile):
            after(wait, s_y, tile.n - 1)
            sp.dma_start(x2t[:, tile.p], rows_of(X2, tile.t)).then_inc(s_x2[tile.p], 16)

        def store_out(n):
            wait(s_sum, SUMS * n + SUMS)
            sp.dma_start(rows_of(out, n), acc[:, bass.ds(n, 1)].rearrange("p o d -> p (o d)")).then_inc(s_out, 16)

        first = [Tile(0, p).of(SHARED, False, p) for p in range(2)]
        load_x(first[0])
        sp.dma_start(jrow, scratch["c_jrow"]).then_inc(s_tc, 16)
        load_x(first[1])
        def pad(e):
            row = sp.value_load(padi[0:1, e:e + 1], min_val=0, max_val=ZERO_ROW)
            sp.dma_start(XS[bass.ds(row, P)], zero[:]).then_inc(s_pad2, 16)

        def body(before, tile, following, later):
            if exists(later):
                if isinstance(later.n, int) and later.n == R0:
                    wait(s_tab, 1)
                    wait(s_last, 16 * 2 * K)
                    wait(s_pad, 16 * (POOL_PADS + 1))
                    wait(s_pad2, 16 * (E - POOL_PADS))
                load_x(later)
            if isinstance(tile.n, int) and tile.n == R1 + 1:
                wait(s_yp, R1)
                for p in range(2):
                    wait(s_yst[p], 16 * (R0 // 2))
                sp.dma_start(acc[:, 0:NS0], XO.rearrange("t p d -> p t d")).then_inc(s_acc, 16)
            if tile.late and not (isinstance(tile.m, int) and tile.m <= LATE):
                store_out(tile.m - LATE - 1)
            if tile.kind == SHARED:
                load_x2(tile)
            if isinstance(tile.n, int) and tile.n == 0:
                wait(s_zero, 1)
                wait(s_tb, 2)
                for e in range(POOL_PADS, E):
                    pad(e)

        slots(sp, body)
        for n in range(NT - NREST - 1, NT):
            store_out(n)
        sp.wait_ge(s_out, 16 * NT)

    @block.gpsimd
    def _(pool):
        def wait(s, n):
            pool.wait_ge(s, n)
            pool.sem_inc(s_plg, 1)

        def load_weights(e, i):
            pool.dma_start(wts_sb[:, bass.ds(e, 1)], wts_w[:, bass.ds(e, 1)]).then_inc(s_wr[i], 16)
            if i == 0:
                pool.dma_start(dnr_sb[:, bass.ds(e // 2, 1)], dnr_w[:, bass.ds(e // 2, 1)]).then_inc(s_wr[i], 16)

        def weights_ready(h, i):
            wait(s_wr[i], (32 if i == 0 else 16) * (h + 1))
            pool.sem_inc(s_exp, 1)

        for i in range(2):
            load_weights(i, i)
        for t in range(2):
            for j in range(K):
                pool.indirect_dma_start(XS, bass.IndirectOffsetOnAxis(ap=keep["last_slots"][:, t, j:j + 1], axis=0),
                                        keep["last_rows"][:, t], None).then_inc(s_last, 16)
        pool.memset(zero[:], 0.0).then_inc(s_zero, 1)
        wait(s_zero, 1)
        pool.dma_start(XS[ZERO_ROW:ZERO_ROW + P], zero[:]).then_inc(s_pad, 16)
        wait(s_tb, 2)
        for e in range(POOL_PADS):
            pool.indirect_dma_start(XS, bass.IndirectOffsetOnAxis(ap=padi[:, e:e + 1], axis=0), zero[:],
                                    None).then_inc(s_pad, 16)

        wait(s_x[R0 % 2], 16 * (R0 // 2 + 1))
        with pool.Fori(0, E // 2 - 1) as r:
            for i in range(2):
                weights_ready(r, i)
                load_weights(2 * r + (2 + i), i)
        for i in range(2):
            weights_ready(E // 2 - 1, i)

        for p in range(2):
            wait(s_yst[p], 16 * (R1 // 2))
        with pool.Fori(0, NT // RING) as r:
            for i in range(RING):
                wait(s_at, RING * r + i + 1)
                for j in range(K):
                    pool.indirect_dma_start(rows[:, i, j], None, Y.rearrange("j p d -> (j p) d"),
                                            bass.IndirectOffsetOnAxis(ap=at_now[:, i, j:j + 1], axis=0)).then_inc(s_rows[i], 16)

    @block.scalar
    def _(act):
        def x_out(tile):
            act.wait_ge(s_xp, tile.n + 1)
            after(act.wait_ge, s_gu, tile.n - 1)
            act.activation(xT[:, tile.p], ps_x[:, tile.p], ACT.Copy).then_inc(s_xT, 1)

        def y_out(tile):
            act.wait_ge(s_yp, tile.n + 1)
            after(act.wait_ge, s_yst[tile.p], 16 * tile.h)
            act.activation(yt[:, tile.p], ps_y[:, tile.p], ACT.Copy).then_inc(s_y, 1)

        def store(tile):
            act.wait_ge(s_y, tile.n + 1)
            act.sem_inc(s_acg, 1)
            if tile.kind == SHARED:
                act.dma_start(rows_of(XO, tile.t), yt[:, tile.p]).then_inc(s_yst[tile.p], 16)
            else:
                act.dma_start(rows_of(Y, tile.j), yt[:, tile.p]).then_inc(s_yst[tile.p], 16)

        def body(before, tile, following, later):
            act.wait_ge(s_gu, tile.n + 1)
            act.activation(gs[:, tile.p], ps_gu[:, tile.p, 0:I], ACT.Silu).then_inc(s_si, 1)
            if exists(following):
                x_out(following)
            if exists(before) and not before.late:
                if before.kind == ROUTED:
                    y_out(before)
                store(before)

        x_out(Tile(0, 0))
        slots(act, body)

    @block.vector
    def _(dve):
        steps = [0]

        def step(ins):
            steps[0] += 1
            ins.then_inc(s_tb, 1)
            dve.wait_ge(s_tb, steps[0])

        def pads():
            step(dve.tensor_scalar(padf[:], cnt[:, 0], iotap[:, 0:1], None, ALU.add))
            step(dve.tensor_tensor(padi[:], padf[:], ebase[:], ALU.add))

        bc = [P, NR, E]
        upto = small[:, 4]

        def tiles_of_experts():
            step(dve.tensor_scalar(smi[:], cnt[:, 0], float(P - 1), None, ALU.add))
            step(dve.tensor_scalar(smi[:], smi[:], 7, None, ALU.logical_shift_right))
            step(dve.tensor_copy(small[:, 0], smi[:]))
            for i, s in enumerate((1, 2, 4, 8)):
                step(dve.tensor_copy(small[:, i + 1, 0:s], small[:, i, 0:s]))
                step(dve.tensor_tensor(small[:, i + 1, s:E], small[:, i, s:E], small[:, i, 0:E - s], ALU.add))
            step(dve.tensor_tensor(small[:, 5], upto, small[:, 0], ALU.subtract))
            step(dve.scalar_tensor_tensor(small[:, 6], small[:, 5], -float(P), ebase[:], ALU.mult, ALU.add))
            dve.wait_ge(s_tc, 16)
            step(dve.tensor_tensor(big, jrow[:, 0].unsqueeze(2).to_broadcast(bc), upto.unsqueeze(1).to_broadcast(bc), ALU.is_ge))
            step(dve.tensor_reduce(jt[:, 0], big, AX_X, ALU.add))

        def experts_of_tiles():
            step(dve.tensor_scalar(jt[:, 1], jt[:, 0], float(E - 1), None, ALU.min))
            step(dve.tensor_scalar(jt[:, 2], jt[:, 0], float(E), None, ALU.is_lt))
            step(dve.tensor_tensor(big, jt[:, 1].unsqueeze(2).to_broadcast(bc), iota16[:, :].unsqueeze(1).to_broadcast(bc),
                                   ALU.is_equal))

        def starts_of_tiles():
            step(dve.tensor_tensor(big, big, small[:, 6].unsqueeze(1).to_broadcast(bc), ALU.mult))

        def tables():
            step(dve.tensor_reduce(jt[:, 3], big, AX_X, ALU.add))
            step(dve.tensor_tensor(jt[:, 3], jt[:, 3], jrow[:, 1], ALU.add))
            step(dve.tensor_tensor(jt[:, 4], jt[:, 3], jrow[:, 2], ALU.subtract))
            step(dve.tensor_tensor(jt[:, 5], jt[:, 4], jt[:, 2], ALU.mult))
            step(dve.tensor_tensor(tab[0:1, 0], jt[0:1, 5], jrow[0:1, 2], ALU.add))
            step(dve.tensor_copy(tab[0:1, 1], jt[0:1, 1]))
            step(dve.tensor_copy(ji[:], jt[:, 1]))
            step(dve.tensor_scalar(ji[:], ji[:], 1, None, ALU.bitwise_and))
            step(dve.tensor_copy(par[:, 1], ji[:]))
            dve.tensor_scalar(par[:, 0], par[:, 1], -1.0, 1.0, ALU.mult, ALU.add).then_inc(s_tab, 1)
            dve.wait_ge(s_tab, 1)

        bt = [P, NT * K, E]
        of_tokens = room[:, 0:NT * K * E].rearrange("p (n e) -> p n e", e=E)
        slots_ = slot_all[:, :, :].rearrange("p t k -> p (t k)")

        def rows_of_experts():
            step(dve.tensor_tensor(of_tokens, e_all[:, :, :].rearrange("p t k -> p (t k)").unsqueeze(2).to_broadcast(bt),
                                   iota16[:, :].unsqueeze(1).to_broadcast(bt), ALU.is_equal))

        def result_rows():
            step(dve.tensor_tensor(of_tokens, of_tokens, small[:, 6].unsqueeze(1).to_broadcast(bt), ALU.mult))
            step(dve.tensor_reduce(shift[:], of_tokens, AX_X, ALU.add))
            step(dve.tensor_tensor(at_all[:], slots_, shift[:], ALU.subtract))

        def hT_out(tile):
            dve.wait_ge(s_hp, tile.n + 1)
            after(dve.wait_ge, s_yp, tile.n - 1)
            if tile.kind == ROUTED:
                dve.tensor_copy(hT[:, tile.p], ps_h[:, tile.p, 0:2]).then_inc(s_hT, 1)
            else:
                dve.tensor_copy(hT[:, tile.p, 0], ps_h[:, tile.p, 0])
                dve.tensor_copy(hT[0:IR, tile.p, 1], ps_h[0:IR, tile.p, 1]).then_inc(s_hT, 1)

        def hidden(tile):
            dve.wait_ge(s_si, tile.n + 1)
            after(dve.wait_ge, s_hp, tile.n - 1)
            up = ps_gu[:, tile.p, I:2 * I]
            h = hid[:, tile.p].rearrange("p a b -> p (a b)")
            if tile.kind == ROUTED:
                dve.tensor_tensor(h[:, 0:P], up[:, 0:P], gs[:, tile.p, 0:P], ALU.mult)
                for k in range(2):
                    last = dve.scalar_tensor_tensor(h[:, P + k * IR:P + (k + 1) * IR], up[:, P:I],
                                                    par[:, k, bass.ds(tile.j, 1)], gs[:, tile.p, P:I], ALU.mult, ALU.mult)
            else:
                last = dve.tensor_tensor(h[:, 0:I], up, gs[:, tile.p], ALU.mult)
            last.then_inc(s_h, 1)

        def y_sum(tile):
            dve.wait_ge(s_yp, tile.n + 1)
            dve.wait_ge(s_x2[tile.p], 16 * tile.th + 16)
            if tile.late:
                to = acc[:, bass.ds(tile.t, 1)].rearrange("p o d -> p (o d)")
            else:
                after(dve.wait_ge, s_yst[tile.p], 16 * tile.h)
                to = yt[:, tile.p]
            dve.tensor_tensor(to, ps_y[:, tile.p], x2t[:, tile.p], ALU.add).then_inc(s_y, 1)

        def want(n, ring):
            dve.tensor_copy(at_now[:, ring], at_all[:, bass.ds(K * n, K)]).then_inc(s_at, 1)

        def want_next(n, ring):
            dve.wait_ge(s_sum, SUMS * n + SUMS)
            want(n + RING, ring)

        def combine(n, ring):
            if isinstance(n, int) and n < NS0:
                dve.wait_ge(s_acc, 16)
            else:
                dve.wait_ge(s_y, n + (R1 - NS0 + 1))
            dve.wait_ge(s_rows[ring], 16 * K * (n // RING) + 16 * K)
            w = w_all[:, :, :].rearrange("p t k -> p (t k)")
            for j in range(K):
                for c in range(2):
                    f = slice(c * D // 2, (c + 1) * D // 2)
                    if j:
                        dve.wait_ge(s_sum, SUMS * n + 2 * j + c - 1)
                    sum_ = acc[:, bass.ds(n, 1), f].rearrange("p o d -> p (o d)")
                    dve.scalar_tensor_tensor(sum_, rows[:, ring, j, f], w[:, bass.ds(K * n + j, 1)], sum_, ALU.mult,
                                             ALU.add).then_inc(s_sum, 1)

        def body(before, tile, following, later):
            if exists(before):
                hT_out(before)
            if isinstance(tile.n, int) and tile.n < 2:
                (starts_of_tiles, tables)[tile.n]()
            sums = tile.late and not (isinstance(tile.m, int) and tile.m < LATE)
            if sums:
                combine(tile.m - LATE, (tile.m_ring - LATE) % RING)
            hidden(tile)
            if sums:
                want_next(tile.m - LATE, (tile.m_ring - LATE) % RING)
            if exists(before) and before.kind == SHARED:
                y_sum(before)
            if isinstance(tile.n, int) and R0 <= tile.n < R0 + 2:
                (rows_of_experts, result_rows)[tile.n - R0]()
            if isinstance(tile.n, int) and tile.n == R1:
                for i in range(RING):
                    want(i, i)

        pads()
        tiles_of_experts()
        experts_of_tiles()
        slots(dve, body)
        end = Tile(H2 - 1, 1).of(SHARED, True, NTILES - 1)
        hT_out(end)
        y_sum(end)
        for n in range(NT - NREST, NT):
            combine(n, n % RING)
            if n + RING < NT:
                want_next(n, n % RING)

    @block.tensor
    def _(pe):
        def transpose_x(tile):
            pe.wait_ge(s_x[tile.p], 16 * tile.h + 16)
            after(pe.wait_ge, s_xT, tile.n - 1)
            for i in range(DC):
                mm = pe.transpose(ps_x[:, tile.p, i], xt[:, tile.p, i * P:(i + 1) * P], identf[:])
            mm.then_inc(s_xp, 1)

        def expert(tile):
            if not exists(tile) or tile.kind == SHARED:
                return None
            return pe.value_load(tab[0:1, 1, bass.ds(tile.j, 1)], min_val=0, max_val=E - 1)

        def of_expert(e, part):
            return wts_sb[:, bass.ds(e, 1), part].rearrange("p o n -> p (o n)")

        def gate_up(tile, e):
            if tile.kind == ROUTED:
                pe.wait_ge(s_exp, e + 1)
            pe.wait_ge(s_xT, tile.n + 1)
            after(pe.wait_ge, s_h, tile.n - 1)
            for i in range(DC):
                w = sgu_sb[:, i] if tile.kind == SHARED else of_expert(e, slice(2 * I * i, 2 * I * (i + 1)))
                mm = pe.matmul(ps_gu[:, tile.p, 0:2 * I], xT[:, tile.p, i], w, start=(i == 0), stop=(i == DC - 1))
            mm.then_inc(s_gu, 1)

        def transpose_h(tile):
            pe.wait_ge(s_h, tile.n + 1)
            after(pe.wait_ge, s_hT, tile.n - 1)
            pe.transpose(ps_h[:, tile.p, 0], hid[:, tile.p, 0], identf[:])
            if tile.kind == ROUTED:
                mm = pe.transpose(ps_h[:, tile.p, 1], hid[:, tile.p, 1], identf[:])
            else:
                mm = pe.transpose(ps_h[0:IR, tile.p, 1], hid[:, tile.p, 1, 0:IR], identf[:])
            mm.then_inc(s_hp, 1)

        def down(tile, e):
            pe.wait_ge(s_hT, tile.n + 1)
            after(pe.wait_ge, s_y, tile.n - 1)
            if tile.kind == ROUTED:
                pe.matmul(ps_y[:, tile.p], hT[:, tile.p, 0], of_expert(e, slice(W - D, W)),
                          start=True, stop=False)
                mm = pe.matmul(ps_y[:, tile.p], hT[:, tile.p, 1], dnr_sb[:, bass.ds(e // 2, 1)].rearrange("p o n -> p (o n)"),
                               start=False, stop=True)
            else:
                pe.matmul(ps_y[:, tile.p], hT[:, tile.p, 0], sdn_sb[:], start=True, stop=False)
                mm = pe.matmul(ps_y[:, tile.p], hT[0:IR, tile.p, 1], sdnr_sb[:], start=False, stop=True)
            mm.then_inc(s_yp, 1)

        def body(before, tile, following, later):
            if isinstance(tile.n, int) and tile.n == R0:
                pe.wait_ge(s_tab, 1)
            e_before, e = expert(before), expert(tile)
            if exists(before):
                transpose_h(before)
            gate_up(tile, e)
            if exists(following):
                transpose_x(following)
            if exists(before):
                down(before, e_before)

        transpose_x(Tile(0, 0))
        slots(pe, body)
        end = Tile(H2 - 1, 1).of(SHARED, True, NTILES - 1)
        transpose_h(end)
        down(end, None)

    ctx.close()


INPUTS = ["wq", "wk", "wv", "memory", "memory_norm", "memory_weight", "router_w", "e_bias"]


def build(nc, T, a, out):
    zero_row = sizes(T)[1]
    NU, NT = T // UT, T // P

    def dram(name, shape, dt=F32):
        return nc.dram_tensor(name, shape, dt).ap()

    scratch = {
        "QK": dram("qk_parts", [NU, NH // 2, NQ + 1, PARTS * DH, SEQ], BF16),
        "XM": dram("x_plus_memory", [NU, 2, P, D]),
        "X2": dram("x2_rows", [NU, 2, P, D]),
        "XN2": dram("xn2_rows", [NU, 2, P, D]),
        "XS": dram("rows_by_expert", [zero_row + P, D]),
        "Y": dram("results_by_expert", [NT * K + E, P, D]),
        "XO": dram("x2_plus_shared", [FIRST, P, D]),
    } | {k: v for k, v in a.items() if k.startswith("c_")}
    with ExitStack() as ctx:
        keep = kept(nc, ctx, T)
        attention(nc, T, [a["x"]] + [a[k] for k in INPUTS], {k: a[k] for k in ("sgu", "sdn", "sdnr")},
                  keep, scratch)
        for k in ("X2", "XN2"):
            scratch[k] = scratch[k].rearrange("u t p d -> (u t) p d")
        feed_forward(nc, T, [a["wts"], a["dnr"]], keep, scratch,
                     out.rearrange("b (s p) d -> (b s) p d", p=P))


def constants(T):
    i = np.arange(P)
    stride, zero_row = sizes(T)
    nr = T // P * K + E
    j = np.arange(nr)
    jrow = np.stack([j, j * P, np.full(nr, zero_row)])
    return {
        "c_identf": np.eye(P, dtype=np.float32),
        "c_before": (i[:, None] < i[None, :]).astype(np.float32),
        "c_iota16": np.tile(np.arange(E, dtype=np.float32), (P, 1)),
        "c_iotap": i[:, None].astype(np.float32),
        "c_ebase": np.tile(np.arange(E, dtype=np.float32) * stride, (P, 1)),
        "c_jrow": np.tile(jrow.astype(np.float32), (P, 1, 1)),
    }


def kept(nc, ctx, T):
    def sb(name, shape, dt=F32):
        return ctx.enter_context(nc.sbuf_tensor(name, shape, dt))
    return {"identf": sb("identf", [P, P]), "iota16": sb("iota16", [P, E]), "iotap": sb("iotap", [P, 1]),
            "ebase": sb("ebase", [P, E]), "cnt": sb("cnt", [P, 1, E]), "w_all": sb("w_all", [P, T // P, K]),
            "slot_all": sb("slot_all", [P, T // P, K]), "e_all": sb("e_all", [P, T // P, K]),
            "last_rows": sb("last_rows", [P, 2, D]), "last_slots": sb("last_slots", [P, 2, K], U32),
            "sgu": sb("sgu_sb", [P, DC, 2 * I]), "sdn": sb("sdn_sb", [P, D]), "sdnr": sb("sdnr_sb", [IR, D])}


def kernel(L0_attn_x, L0_attn_Wq, L0_attn_Wk, L0_attn_Wv, L0_attn_memory, L0_attn_memory_norm, L0_attn_memory_weight,
           L0_ffn_router_w, L0_ffn_e_bias, L0_ffn_gate_up_proj, L0_ffn_down_proj, L0_ffn_shared_gate_w,
           L0_ffn_shared_up_w, L0_ffn_shared_down_w):
    import concourse.bacc as bacc
    from concourse.bass_utils import run_bass_kernel_spmd

    def chunks(w, rows=P):
        w = np.asarray(w)
        return np.ascontiguousarray(w.reshape(w.shape[0] // rows, rows, -1).transpose(1, 0, 2))

    x = np.asarray(L0_attn_x)
    B, S, _ = x.shape
    T = B * S
    gu = np.asarray(L0_ffn_gate_up_proj)
    dn = np.asarray(L0_ffn_down_proj).transpose(0, 2, 1)
    sdn = np.asarray(L0_ffn_shared_down_w).T
    arrays = {
        "x": np.ascontiguousarray(x.reshape(T, D)),
        "wq": chunks(np.asarray(L0_attn_Wq).T),
        "wk": chunks(np.asarray(L0_attn_Wk).T),
        "wv": chunks(np.asarray(L0_attn_Wv).T),
        "memory": np.ascontiguousarray(L0_attn_memory),
        "memory_norm": np.ascontiguousarray(L0_attn_memory_norm),
        "memory_weight": np.ascontiguousarray(L0_attn_memory_weight),
        "router_w": chunks(np.asarray(L0_ffn_router_w).T),
        "e_bias": np.ascontiguousarray(L0_ffn_e_bias),
        "wts": np.ascontiguousarray(np.concatenate([
            gu.transpose(2, 0, 1).reshape(DC, P, E, 2 * I).transpose(1, 2, 0, 3).reshape(P, E, -1),
            dn[:, 0:P].transpose(1, 0, 2)], axis=2)),
        "dnr": np.ascontiguousarray(dn[:, P:I].reshape(E // 2, P, D).transpose(1, 0, 2)),
        "sgu": chunks(np.concatenate([np.asarray(L0_ffn_shared_gate_w), np.asarray(L0_ffn_shared_up_w)]).T),
        "sdn": np.ascontiguousarray(sdn[0:P]),
        "sdnr": np.ascontiguousarray(sdn[P:I]),
    } | constants(T)
    nc = bacc.Bacc("TRN2", target_bir_lowering=False, num_devices=1)
    a = {k: nc.dram_tensor(f"in_{k}", v.shape, mybir.dt.from_np(v.dtype), kind="ExternalInput").ap() for k, v in arrays.items()}
    out = nc.dram_tensor("out", [B, S, D], F32, kind="ExternalOutput").ap()
    build(nc, T, a, out)
    r = run_bass_kernel_spmd(nc, [{f"in_{k}": v for k, v in arrays.items()}], core_ids=[0])
    return r.results[0]["out"]
```
